# Optimizing a Trainium2 kernel written in Bass

```python
import numpy as np
import jax
import jax.numpy as jnp

def _softmax(x, axis=-1):
    return jax.nn.softmax(x, axis=axis)

def _gelu(x):
    return jax.nn.gelu(x, approximate=True)

def _silu(x):
    return jax.nn.silu(x)

def _sigmoid(x):
    return jax.nn.sigmoid(x)

def _layernorm(x, axis=-1, eps=1e-05):
    m = jnp.mean(x, axis=axis, keepdims=True)
    v = jnp.var(x, axis=axis, keepdims=True)
    return (x - m) / jnp.sqrt(v + eps)

def _scatter_add(tgt, idx, src, axis=0):
    return tgt.at[idx].add(src)

def _segment_sum(src, seg, n):
    return jax.ops.segment_sum(src, seg, n)
kernel_name = 'mk_xattn_seq_d2_seqx_r4_578f0b'

def setup_inputs(seed: int=0):
    np.random.seed(seed)
    _w = jnp.asarray

    def _rec_inputs():
        import jax
        import jax.numpy as jnp
        _rk = jax.random.key(seed)
        x = -0.0005146 + 1 * jax.random.normal(jax.random.fold_in(_rk, 1), (8, 100, 512), jnp.float32)
        _lenS = 100 - jax.random.randint(jax.random.fold_in(_rk, 7), (8,), 0, max(1, 100 // 4) + 1, jnp.int32)
        _lenS2 = 361 - jax.random.randint(jax.random.fold_in(_rk, 8), (8,), 0, max(1, 361 // 4) + 1, jnp.int32)
        _ctx_2048P = jax.random.normal(jax.random.fold_in(_rk, 11), (8, 16, 512), jnp.float32)
        _ctx_2048c = jax.random.dirichlet(jax.random.fold_in(_rk, 511), 0.3 * jnp.ones((16,), jnp.float32), (8, 361))
        _ctx_2048t = jnp.einsum('bsk,bkd->bsd', _ctx_2048c, _ctx_2048P)
        _ctx_2048t = _ctx_2048t * jax.lax.rsqrt(jnp.mean(jnp.square(_ctx_2048t)) + 1e-12) * 0.953939
        ctx_2048 = -0.000392918 + 0.999932 * (_ctx_2048t + 0.3 * jax.random.normal(jax.random.fold_in(_rk, 611), (8, 361, 512), jnp.float32))
        _validS = jnp.arange(100)[None, :] < _lenS[:, None]
        _validS2 = jnp.arange(361)[None, :] < _lenS2[:, None]
        _causal = jnp.tril(jnp.ones((100, 100), dtype=bool))
        mask_BxS2_ik0 = jnp.where(jnp.broadcast_to(_validS2[:, :], (8, 361)), 0, 1).astype(jnp.int32)
        return (x, ctx_2048, mask_BxS2_ik0)
    x, ctx_2048, mask_BxS2_ik0 = _rec_inputs()

    def _L0_xattn_setup():
        import jax, jax.numpy as jnp
        import numpy as np
        B, P, K, H, NH = (4, 512, 64, 512, 16)
        DH = H // NH
        EPS = 1e-06

        def rmsnorm(x, w):
            var = jnp.mean(jnp.square(x), axis=-1, keepdims=True)
            return x * jax.lax.rsqrt(var + EPS) * w
        key = jax.random.key(seed)
        ks = jax.random.split(key, 12)
        s = 0.02
        return {'x': jax.random.normal(ks[0], (B, P, H), jnp.float32), 'latents': jax.random.normal(ks[1], (B, K, H), jnp.float32), 'attention_mask': jax.random.randint(ks[2], (B, P), 0, 2, jnp.int32), 'q_w': s * jax.random.normal(ks[3], (H, H), jnp.float32), 'q_b': jnp.zeros((H,), jnp.float32), 'kv_w': s * jax.random.normal(ks[4], (H, 2 * H), jnp.float32), 'kv_b': jnp.zeros((2 * H,), jnp.float32), 'out_w': s * jax.random.normal(ks[5], (H, H), jnp.float32), 'out_b': jnp.zeros((H,), jnp.float32), 'postnorm_w': jnp.ones((H,), jnp.float32), 'mlp_w1': s * jax.random.normal(ks[6], (H, 4 * H), jnp.float32), 'mlp_b1': jnp.zeros((4 * H,), jnp.float32), 'mlp_w2': s * jax.random.normal(ks[7], (4 * H, H), jnp.float32), 'mlp_b2': jnp.zeros((H,), jnp.float32)}
    _L0_xattn_all = _L0_xattn_setup()
    _L0_xattn_in = {k: v for k, v in _L0_xattn_all.items() if k in ('q_w', 'q_b', 'kv_w', 'kv_b', 'out_w', 'out_b', 'postnorm_w', 'mlp_w1', 'mlp_b1', 'mlp_w2', 'mlp_b2')}
    del _L0_xattn_all

    def _L1_xattn_setup():
        import jax, jax.numpy as jnp
        import numpy as np
        N_HEAD = 32
        EPS = 1e-05

        def _ln(x, w, b):
            m = jnp.mean(x, axis=-1, keepdims=True)
            v = jnp.mean((x - m) ** 2, axis=-1, keepdims=True)
            return (x - m) * jax.lax.rsqrt(v + EPS) * w + b

        def _forward(x, state, i, ln1_w, ln1_b, ln2_w, ln2_b, maa_x, maa_w, maa_k, maa_v, maa_r, maa_g, maa_w1, maa_w2, time_decay, decay_w1, decay_w2, faaaa, Wr, Wk, Wv, Wg, Wo, gn_w, gn_b, fmaa_k, fmaa_r, fWk, fWr, fWv):
            B, L, C = x.shape
            H = N_HEAD
            S = C // H
            i0 = (2 + S) * i
            xa = _ln(x, ln1_w, ln1_b)
            sx = jnp.concatenate([state[:, i0 + 1][:, None], xa[:, :-1]], axis=1) - xa
            xxx = xa + sx * maa_x
            t = jnp.tanh(xxx @ maa_w1).reshape(B, L, 5, -1)
            m = jnp.einsum('blfd,fdc->blfc', t, maa_w2)
            mw, mk, mv, mr, mg = (m[:, :, j] for j in range(5))
            xw = xa + sx * (maa_w + mw)
            xk = xa + sx * (maa_k + mk)
            xv = xa + sx * (maa_v + mv)
            xr = xa + sx * (maa_r + mr)
            xg = xa + sx * (maa_g + mg)
            w = time_decay + jnp.tanh(xw @ decay_w1) @ decay_w2
            w = jnp.exp(-jnp.exp(w)).reshape(B, L, H, S)
            r = (xr @ Wr.T).reshape(B, L, H, S)
            k = (xk @ Wk.T).reshape(B, L, H, S)
            v = (xv @ Wv.T).reshape(B, L, H, S)
            g = jax.nn.silu(xg @ Wg.T)
            s0 = state[:, i0 + 2:i0 + 2 + S].reshape(B, H, S, S)

            def step(s, inp):
                k_l, v_l, w_l, r_l = inp
                a = k_l[..., :, None] * v_l[..., None, :]
                out = jnp.einsum('bhs,bhst->bht', r_l, faaaa * a + s)
                s_new = a + w_l[..., None] * s
                return (s_new, out)
            seq = tuple((z.transpose(1, 0, 2, 3) for z in (k, v, w, r)))
            _, outs = jax.lax.scan(step, s0, seq)
            y = outs.transpose(1, 0, 2, 3)
            gm = jnp.mean(y, axis=-1, keepdims=True)
            gv = jnp.mean((y - gm) ** 2, axis=-1, keepdims=True)
            y = ((y - gm) * jax.lax.rsqrt(gv + EPS)).reshape(B, L, C) * gn_w + gn_b
            x = x + y * g @ Wo.T
            xc = _ln(x, ln2_w, ln2_b)
            sxc = jnp.concatenate([state[:, i0][:, None], xc[:, :-1]], axis=1) - xc
            xk2 = xc + sxc * fmaa_k
            xr2 = xc + sxc * fmaa_r
            rr = jax.nn.sigmoid(xr2 @ fWr.T)
            kk = jnp.square(jax.nn.relu(xk2 @ fWk.T))
            x = x + rr * (kk @ fWv.T)
            return x
        key = jax.random.key(seed)
        B, L, C, H = (8, 128, 512, N_HEAD)
        S = C // H
        DM, DD = (32, 64)
        ks = jax.random.split(key, 32)
        n = lambda k, shp, s=1.0: jax.random.normal(k, shp, dtype=jnp.float32) * s
        u = lambda k, shp: jax.random.uniform(k, shp, dtype=jnp.float32)
        inp = {'x': n(ks[0], (B, L, C)), 'state': n(ks[1], (B, 2 + S, C), 0.1), 'i': 0, 'ln1_w': jnp.ones((C,), jnp.float32), 'ln1_b': jnp.zeros((C,), jnp.float32), 'ln2_w': jnp.ones((C,), jnp.float32), 'ln2_b': jnp.zeros((C,), jnp.float32), 'maa_x': u(ks[2], (C,)), 'maa_w': u(ks[3], (C,)), 'maa_k': u(ks[4], (C,)), 'maa_v': u(ks[5], (C,)), 'maa_r': u(ks[6], (C,)), 'maa_g': u(ks[7], (C,)), 'maa_w1': n(ks[8], (C, 5 * DM), 0.02), 'maa_w2': n(ks[9], (5, DM, C), 0.02), 'time_decay': n(ks[10], (C,), 0.5), 'decay_w1': n(ks[11], (C, DD), 0.02), 'decay_w2': n(ks[12], (DD, C), 0.02), 'faaaa': n(ks[13], (H, S, 1), 0.1), 'Wr': n(ks[14], (C, C), 0.02), 'Wk': n(ks[15], (C, C), 0.02), 'Wv': n(ks[16], (C, C), 0.02), 'Wg': n(ks[17], (C, C), 0.02), 'Wo': n(ks[18], (C, C), 0.02), 'gn_w': jnp.ones((C,), jnp.float32), 'gn_b': jnp.zeros((C,), jnp.float32), 'fmaa_k': u(ks[19], (C,)), 'fmaa_r': u(ks[20], (C,)), 'fWk': n(ks[21], (C, C), 0.02), 'fWr': n(ks[22], (C, C), 0.02), 'fWv': n(ks[23], (C, C), 0.02)}
        return inp
    _L1_xattn_all = _L1_xattn_setup()
    _L1_xattn_in = {k: v for k, v in _L1_xattn_all.items() if k in ('ln1_w', 'ln1_b', 'ln2_w', 'ln2_b', 'maa_x', 'maa_w', 'maa_k', 'maa_v', 'maa_r', 'maa_g', 'maa_w1', 'maa_w2', 'time_decay', 'decay_w1', 'decay_w2', 'faaaa', 'Wr', 'Wk', 'Wv', 'Wg', 'Wo', 'gn_w', 'gn_b', 'fmaa_k', 'fmaa_r', 'fWk', 'fWr', 'fWv')}
    del _L1_xattn_all
    return {'x': x, 'ctx_2048': ctx_2048, 'mask_BxS2_ik0': mask_BxS2_ik0, 'L0_xattn_q_w': _L0_xattn_in['q_w'], 'L0_xattn_q_b': _L0_xattn_in['q_b'], 'L0_xattn_kv_w': _L0_xattn_in['kv_w'], 'L0_xattn_kv_b': _L0_xattn_in['kv_b'], 'L0_xattn_out_w': _L0_xattn_in['out_w'], 'L0_xattn_out_b': _L0_xattn_in['out_b'], 'L0_xattn_postnorm_w': _L0_xattn_in['postnorm_w'], 'L0_xattn_mlp_w1': _L0_xattn_in['mlp_w1'], 'L0_xattn_mlp_b1': _L0_xattn_in['mlp_b1'], 'L0_xattn_mlp_w2': _L0_xattn_in['mlp_w2'], 'L0_xattn_mlp_b2': _L0_xattn_in['mlp_b2'], 'L1_xattn_ln1_w': _L1_xattn_in['ln1_w'], 'L1_xattn_ln1_b': _L1_xattn_in['ln1_b'], 'L1_xattn_ln2_w': _L1_xattn_in['ln2_w'], 'L1_xattn_ln2_b': _L1_xattn_in['ln2_b'], 'L1_xattn_maa_x': _L1_xattn_in['maa_x'], 'L1_xattn_maa_w': _L1_xattn_in['maa_w'], 'L1_xattn_maa_k': _L1_xattn_in['maa_k'], 'L1_xattn_maa_v': _L1_xattn_in['maa_v'], 'L1_xattn_maa_r': _L1_xattn_in['maa_r'], 'L1_xattn_maa_g': _L1_xattn_in['maa_g'], 'L1_xattn_maa_w1': _L1_xattn_in['maa_w1'], 'L1_xattn_maa_w2': _L1_xattn_in['maa_w2'], 'L1_xattn_time_decay': _L1_xattn_in['time_decay'], 'L1_xattn_decay_w1': _L1_xattn_in['decay_w1'], 'L1_xattn_decay_w2': _L1_xattn_in['decay_w2'], 'L1_xattn_faaaa': _L1_xattn_in['faaaa'], 'L1_xattn_Wr': _L1_xattn_in['Wr'], 'L1_xattn_Wk': _L1_xattn_in['Wk'], 'L1_xattn_Wv': _L1_xattn_in['Wv'], 'L1_xattn_Wg': _L1_xattn_in['Wg'], 'L1_xattn_Wo': _L1_xattn_in['Wo'], 'L1_xattn_gn_w': _L1_xattn_in['gn_w'], 'L1_xattn_gn_b': _L1_xattn_in['gn_b'], 'L1_xattn_fmaa_k': _L1_xattn_in['fmaa_k'], 'L1_xattn_fmaa_r': _L1_xattn_in['fmaa_r'], 'L1_xattn_fWk': _L1_xattn_in['fWk'], 'L1_xattn_fWr': _L1_xattn_in['fWr'], 'L1_xattn_fWv': _L1_xattn_in['fWv']}

def reference(x, ctx_2048, mask_BxS2_ik0, L0_xattn_q_w, L0_xattn_q_b, L0_xattn_kv_w, L0_xattn_kv_b, L0_xattn_out_w, L0_xattn_out_b, L0_xattn_postnorm_w, L0_xattn_mlp_w1, L0_xattn_mlp_b1, L0_xattn_mlp_w2, L0_xattn_mlp_b2, L1_xattn_ln1_w, L1_xattn_ln1_b, L1_xattn_ln2_w, L1_xattn_ln2_b, L1_xattn_maa_x, L1_xattn_maa_w, L1_xattn_maa_k, L1_xattn_maa_v, L1_xattn_maa_r, L1_xattn_maa_g, L1_xattn_maa_w1, L1_xattn_maa_w2, L1_xattn_time_decay, L1_xattn_decay_w1, L1_xattn_decay_w2, L1_xattn_faaaa, L1_xattn_Wr, L1_xattn_Wk, L1_xattn_Wv, L1_xattn_Wg, L1_xattn_Wo, L1_xattn_gn_w, L1_xattn_gn_b, L1_xattn_fmaa_k, L1_xattn_fmaa_r, L1_xattn_fWk, L1_xattn_fWr, L1_xattn_fWv):
    import jax
    import jax.numpy as jnp

    def _L0_xattn_ref(x, latents, attention_mask, q_w, q_b, kv_w, kv_b, out_w, out_b, postnorm_w, mlp_w1, mlp_b1, mlp_w2, mlp_b2):
        import jax, jax.numpy as jnp
        import numpy as np
        B, P, K, H, NH = (4, 512, 64, 512, 16)
        DH = H // NH
        EPS = 1e-06

        def rmsnorm(x, w):
            var = jnp.mean(jnp.square(x), axis=-1, keepdims=True)
            return x * jax.lax.rsqrt(var + EPS) * w
        b, p, _ = x.shape
        k_len = latents.shape[1]
        residual = latents
        h = jnp.concatenate([x, latents], axis=1)
        q = (latents @ q_w + q_b).reshape(b, k_len, NH, DH)
        kv = (h @ kv_w + kv_b).reshape(b, p + k_len, NH, DH, 2)
        kmat, v = (kv[..., 0], kv[..., 1])
        attn = jnp.einsum('bkhd,bnhd->bhkn', q, kmat) / DH
        full_mask = jnp.concatenate([attention_mask.astype(bool), jnp.ones((b, k_len), bool)], axis=-1)
        attn = jnp.where(full_mask[:, None, None, :], attn, -jnp.inf)
        attn = jax.nn.softmax(attn.astype(jnp.float32), axis=-1).astype(q.dtype)
        attn_out = jnp.einsum('bhkn,bnhd->bkhd', attn, v).reshape(b, k_len, H)
        attn_out = attn_out @ out_w + out_b + residual
        out = rmsnorm(attn_out, postnorm_w)
        out = jax.nn.gelu(out @ mlp_w1 + mlp_b1) @ mlp_w2 + mlp_b2
        return out + residual

    def _L1_xattn_ref(x, state, i, ln1_w, ln1_b, ln2_w, ln2_b, maa_x, maa_w, maa_k, maa_v, maa_r, maa_g, maa_w1, maa_w2, time_decay, decay_w1, decay_w2, faaaa, Wr, Wk, Wv, Wg, Wo, gn_w, gn_b, fmaa_k, fmaa_r, fWk, fWr, fWv):
        import jax, jax.numpy as jnp
        import numpy as np
        N_HEAD = 32
        EPS = 1e-05

        def _ln(x, w, b):
            m = jnp.mean(x, axis=-1, keepdims=True)
            v = jnp.mean((x - m) ** 2, axis=-1, keepdims=True)
            return (x - m) * jax.lax.rsqrt(v + EPS) * w + b

        def _forward(x, state, i, ln1_w, ln1_b, ln2_w, ln2_b, maa_x, maa_w, maa_k, maa_v, maa_r, maa_g, maa_w1, maa_w2, time_decay, decay_w1, decay_w2, faaaa, Wr, Wk, Wv, Wg, Wo, gn_w, gn_b, fmaa_k, fmaa_r, fWk, fWr, fWv):
            B, L, C = x.shape
            H = N_HEAD
            S = C // H
            i0 = (2 + S) * i
            xa = _ln(x, ln1_w, ln1_b)
            sx = jnp.concatenate([state[:, i0 + 1][:, None], xa[:, :-1]], axis=1) - xa
            xxx = xa + sx * maa_x
            t = jnp.tanh(xxx @ maa_w1).reshape(B, L, 5, -1)
            m = jnp.einsum('blfd,fdc->blfc', t, maa_w2)
            mw, mk, mv, mr, mg = (m[:, :, j] for j in range(5))
            xw = xa + sx * (maa_w + mw)
            xk = xa + sx * (maa_k + mk)
            xv = xa + sx * (maa_v + mv)
            xr = xa + sx * (maa_r + mr)
            xg = xa + sx * (maa_g + mg)
            w = time_decay + jnp.tanh(xw @ decay_w1) @ decay_w2
            w = jnp.exp(-jnp.exp(w)).reshape(B, L, H, S)
            r = (xr @ Wr.T).reshape(B, L, H, S)
            k = (xk @ Wk.T).reshape(B, L, H, S)
            v = (xv @ Wv.T).reshape(B, L, H, S)
            g = jax.nn.silu(xg @ Wg.T)
            s0 = state[:, i0 + 2:i0 + 2 + S].reshape(B, H, S, S)

            def step(s, inp):
                k_l, v_l, w_l, r_l = inp
                a = k_l[..., :, None] * v_l[..., None, :]
                out = jnp.einsum('bhs,bhst->bht', r_l, faaaa * a + s)
                s_new = a + w_l[..., None] * s
                return (s_new, out)
            seq = tuple((z.transpose(1, 0, 2, 3) for z in (k, v, w, r)))
            _, outs = jax.lax.scan(step, s0, seq)
            y = outs.transpose(1, 0, 2, 3)
            gm = jnp.mean(y, axis=-1, keepdims=True)
            gv = jnp.mean((y - gm) ** 2, axis=-1, keepdims=True)
            y = ((y - gm) * jax.lax.rsqrt(gv + EPS)).reshape(B, L, C) * gn_w + gn_b
            x = x + y * g @ Wo.T
            xc = _ln(x, ln2_w, ln2_b)
            sxc = jnp.concatenate([state[:, i0][:, None], xc[:, :-1]], axis=1) - xc
            xk2 = xc + sxc * fmaa_k
            xr2 = xc + sxc * fmaa_r
            rr = jax.nn.sigmoid(xr2 @ fWr.T)
            kk = jnp.square(jax.nn.relu(xk2 @ fWk.T))
            x = x + rr * (kk @ fWv.T)
            return x
        return _forward(x, state, i, ln1_w, ln1_b, ln2_w, ln2_b, maa_x, maa_w, maa_k, maa_v, maa_r, maa_g, maa_w1, maa_w2, time_decay, decay_w1, decay_w2, faaaa, Wr, Wk, Wv, Wg, Wo, gn_w, gn_b, fmaa_k, fmaa_r, fWk, fWr, fWv)
    x = _L0_xattn_ref(ctx_2048, x, mask_BxS2_ik0, L0_xattn_q_w, L0_xattn_q_b, L0_xattn_kv_w, L0_xattn_kv_b, L0_xattn_out_w, L0_xattn_out_b, L0_xattn_postnorm_w, L0_xattn_mlp_w1, L0_xattn_mlp_b1, L0_xattn_mlp_w2, L0_xattn_mlp_b2)
    x = _L1_xattn_ref(x, ctx_2048, 0, L1_xattn_ln1_w, L1_xattn_ln1_b, L1_xattn_ln2_w, L1_xattn_ln2_b, L1_xattn_maa_x, L1_xattn_maa_w, L1_xattn_maa_k, L1_xattn_maa_v, L1_xattn_maa_r, L1_xattn_maa_g, L1_xattn_maa_w1, L1_xattn_maa_w2, L1_xattn_time_decay, L1_xattn_decay_w1, L1_xattn_decay_w2, L1_xattn_faaaa, L1_xattn_Wr, L1_xattn_Wk, L1_xattn_Wv, L1_xattn_Wg, L1_xattn_Wo, L1_xattn_gn_w, L1_xattn_gn_b, L1_xattn_fmaa_k, L1_xattn_fmaa_r, L1_xattn_fWk, L1_xattn_fWr, L1_xattn_fWv)
    return x

_drawn_inputs = setup_inputs


def setup_inputs(seed=0):
    import zlib

    import numpy as np

    out = dict(_drawn_inputs(seed))
    spreads = {'L0_xattn_q_b': (0.0, 0.8),
     'L0_xattn_kv_b': (0.0, 0.731),
     'L0_xattn_out_b': (0.0, 2.0),
     'L0_xattn_postnorm_w': (1.0, 0.2),
     'L0_xattn_mlp_b1': (0.0, 0.1),
     'L0_xattn_mlp_b2': (0.0, 0.1),
     'L1_xattn_ln1_w': (1.0, 0.2),
     'L1_xattn_ln1_b': (0.0, 0.297),
     'L1_xattn_ln2_w': (1.0, 0.6),
     'L1_xattn_ln2_b': (0.0, 0.8),
     'L1_xattn_gn_w': (1.0, 0.6),
     'L1_xattn_gn_b': (0.0, 0.8)}
    factors = {'ctx_2048': 2.862,
     'L0_xattn_q_w': 8.0,
     'L0_xattn_kv_w': 5.643,
     'L0_xattn_out_w': 3.9,
     'L1_xattn_maa_x': 6.966,
     'L1_xattn_maa_w': 8.0,
     'L1_xattn_maa_w1': 3.564,
     'L1_xattn_maa_w2': 3.643,
     'L1_xattn_decay_w1': 8.0,
     'L1_xattn_decay_w2': 8.0,
     'L1_xattn_faaaa': 3.942,
     'L1_xattn_fmaa_k': 2.746,
     'L1_xattn_fmaa_r': 8.0,
     'L1_xattn_fWr': 7.717}
    for name, (base, spread) in spreads.items():
        noise = np.random.default_rng([zlib.crc32(name.encode()), seed]).standard_normal(out[name].shape)
        drawn = base * np.exp(spread * noise) if base else spread * noise
        out[name] = jnp.asarray(drawn.astype(out[name].dtype))
    for name, factor in factors.items():
        out[name] = (out[name] * factor).astype(out[name].dtype)
    return out
```

```python
import numpy as np
import concourse.bass as bass
from concourse import mybir

P = 128
B, T, C = 8, 100, 512
NCTX = 361
NKEY = NCTX + T
NH, DH = 16, 32
KT = C // P
HID = 4 * C
MT = HID // P
GH = P // DH
NG = NH // GH
KOFF = [0, 116, 231, 346]
KSZ = [116, 115, 115, 115]
NCH = 2
CB = B // NCH
N = CB * T
RH, RS = 32, 16
MIX = 32
DEC = 64
BIG = 1.0e30
EPS_RMS, EPS_LN = 1e-6, 1e-5

F32 = mybir.dt.float32
I32 = mybir.dt.int32
ALU = mybir.AluOpType
ACT = mybir.ActivationFunctionType
AX_X = mybir.AxisListType.X

VECS = ["q_b", "k_b", "v_b", "out_b", "post_w", "mlp_b1", "mlp_b2", "ln1_w", "ln1_b", "ln2_w", "ln2_b",
        "maa_x", "maa_w", "maa_k", "maa_v", "maa_r", "maa_g", "decay", "fmaa_k", "fmaa_r", "gn_w", "gn_b"]
VCOL, _at = {}, 0
for _name in VECS:
    VCOL[_name] = _at
    _at += MT if _name == "mlp_b1" else KT
NVEC = _at
MIXES = ["w", "k", "v", "r", "g"]

def schedule():
    s = [("oproj", 0), ("oproj", 1), ("rms", 0), ("rms", 1)]
    s += [("up", 0, 0, MT), ("down", 0)]
    s += [("up", 1, 0, 4), ("mean", 0), ("up", 1, 4, 10), ("var", 0), ("up", 1, 10, MT), ("shift", 0), ("down", 1)]

    def mixing(c, extra):
        order = [("mix1", c), ("mixf", c, 0), ("mixf", c, 1), ("dec1", c), ("mixf", c, 2), ("dec2", c),
                 ("proj", c, 1), ("mixf", c, 3), ("proj", c, 2), ("mixf", c, 4), ("proj", c, 3), ("proj", c, 4)]
        out = []
        for i, st in enumerate(order):
            out.append(st)
            out += extra.get(i, [])
        return out

    s += mixing(0, {3: [("mean", 1)], 5: [("var", 1)], 7: [("shift", 1)]})
    s += [("load", 0), ("prep", 0)]
    sc = [("scan", 0, x) for x in range(RS)]
    s += mixing(1, {0: sc[0:1], 1: sc[1:2], 2: sc[2:3], 3: sc[3:4], 4: sc[4:5], 5: sc[5:8],
                    6: sc[8:9], 7: sc[9:11], 8: sc[11:12], 9: sc[12:14], 10: sc[14:15], 11: sc[15:16]})
    s += [("gn", 0), ("load", 1), ("yturn", 0), ("prep", 1), ("scan", 1, 0), ("scan", 1, 1), ("wo", 0), ("scan", 1, 2),
          ("mean", 2), ("scan", 1, 3), ("var", 2), ("scan", 1, 4), ("shift", 2), ("scan", 1, 5), ("fmix", 0),
          ("scan", 1, 6), ("scan", 1, 7), ("fr", 0), ("scan", 1, 8), ("scan", 1, 9), ("fk", 0), ("scan", 1, 10),
          ("scan", 1, 11), ("fv", 0), ("scan", 1, 12), ("scan", 1, 13), ("scan", 1, 14), ("scan", 1, 15)]
    s += [("gn", 1), ("yturn", 1), ("wo", 1), ("mean", 3), ("var", 3), ("shift", 3), ("fmix", 1), ("fr", 1), ("fk", 1), ("fv", 1)]
    return s


def plan_banks(sched):
    used, tiles = [0] * 8, {}

    def use(bank, *key):
        tiles[key] = (bank, used[bank])
        used[bank] += 1

    for st, c, *a in sched:
        if st == "oproj":
            for m in range(KT):
                use(4 * c + m, "oproj", c, m)
        elif st == "rms":
            use(4 * c, "rms", c)
        elif st == "up":
            for m in range(*a):
                use(m % 4, "up", c, m)
        elif st == "down":
            for m in range(KT):
                use(4 + m, "down", c, m)
        elif st == "mean":
            use(4 if c < 2 else 0, "mean", c)
        elif st == "var":
            use(5 if c < 2 else 1, "var", c)
        elif st == "mix1":
            for m in range(2):
                use(m, "mix1", c, m)
        elif st == "mixf":
            for m in range(KT):
                use(m % 2, "mixf", c, a[0], m)
        elif st == "dec1":
            use(2, "dec1", c)
        elif st in ("dec2", "proj"):
            f = a[0] if a else 0
            for m in range(KT):
                use(2 + (m + 1) % 2, "proj", c, f, m)
        elif st == "scan" and a[0] == 0:
            for m in range(KT):
                use(4 + m, "y", c, m)
        elif st in ("wo", "fr", "fk", "fv"):
            for m in range(KT):
                use(m, st, c, m)
    return tiles


def xattn_rwkv_kernel(nc, d, out):
    from contextlib import ExitStack
    sched = schedule()
    tiles = plan_banks(sched)

    with ExitStack() as ctx:
        WORDS = 53200
        arena = ctx.enter_context(nc.sbuf_tensor("arena", [P, WORDS], F32))
        PS = ctx.enter_context(nc.psum_tensor("PS", [P, 8, 512], F32))
        top = [0]

        def place(*shape, at=None):
            n = int(np.prod(shape))
            o = top[0] if at is None else at
            if at is None:
                top[0] += n
            assert o + n <= WORDS, (o, n)
            v = arena[:, o:o + n]
            if len(shape) == 2:
                v = v.rearrange("p (a b) -> p a b", b=shape[1])
            if len(shape) == 3:
                v = v.rearrange("p (a b c) -> p a b c", b=shape[1], c=shape[2])
            return v

        vec = place(NVEC)
        ident = place(P)
        mean_w = place(P)
        head_mask = place(GH)
        state01 = place(2, KT, B)
        eps = place(2)
        bonus = place(RS)
        xT = place(KT, B * T)
        attnT = place(KT, B * T)
        tail = top[0]
        out_w = place(KT, C)
        b_at = top[0]
        up_w = place(KT, HID)
        down_w = place(MT, C)
        a_at = top[0]
        q_w, k_w, v_w = place(KT, C), place(KT, C), place(KT, C)
        hT = [place(KT, NKEY) for _ in range(2)]
        kT = place(KT, NKEY)
        V = place(4, C)
        q_pad = place(NH, T)
        S = place(2, NKEY)
        probs = [place(GH, NKEY) for _ in range(2)]
        pT = place(4, GH * T)
        mask_in = [place(NCTX) for _ in range(2)]
        mask_add = [place(NKEY) for _ in range(2)]
        att_un = place(KT, T)
        rinv_wide = place(C)
        neg_max, row_sum, rinv = place(NH), place(NH), place(NH)
        a_end = top[0]
        top[0] = a_at
        mix_w1 = place(KT, 2 * P)
        mix_w2 = place(5, C)
        dec_w1 = place(KT, P)
        dec_w2 = place(C)
        rkvg_w = {n: place(KT, C) for n in "rkvg"}
        wo_w, fr_w, fk_w, fv_w = (rkvg_w[n] for n in "kvrg")
        rstd = [place(N) for _ in range(2)]
        hid_at = top[0]
        hid = place(MT, N)
        c_at = top[0]
        sq_rms = [hid[:, 0:KT, :], hid[:, KT:2 * KT, :]]
        xe = [place(KT, CB, T + 1, at=tail), place(KT, CB, T + 1)]
        sq = [place(KT, N, at=tail), place(KT, N, at=c_at)]
        Wl = place(RS, T)
        s0 = [place(RS * RS) for _ in range(NCH)]
        rk, gm, gv = place(T), place(T), place(T)
        assert top[0] <= WORDS and a_end <= WORDS, (top[0], a_end)
        top[0] = b_at
        xf = [place(KT, N) for _ in range(2)]
        small_at = top[0]
        mix_t = [place(N) for _ in range(2)]
        dec_t = place(N)
        stage = [place(N) for _ in range(4)]
        lerp = [place(N) for _ in range(2)]
        gate = [place(KT, N) for _ in range(2)]
        rr, kk = place(KT, N, at=small_at), place(KT, N, at=small_at + KT * N)
        Kl, Vl, Rl = [place(RS, T) for _ in range(3)]
        assert top[0] <= a_at, (top[0], a_at)
        top[0] = hid_at
        slots = [place(RS, T) for _ in range(3)]
        wb = place(RS, T)
        assert top[0] <= c_at

        def bank(b, n=512):
            return PS[:, b, 0:n]

        def col(name, m):
            return vec[:, VCOL[name] + m:VCOL[name] + m + 1]

        def sem(name):
            return ctx.enter_context(nc.semaphore(name))

        full = [sem(f"bank{b}_full") for b in range(8)]
        drained = [sem(f"bank{b}_drained") for b in range(8)]

        def wait_full(eng, *key):
            b, n = tiles[key]
            eng.wait_ge(full[b], n + 1)

        def wait_drained(eng, *key):
            b, n = tiles[key]
            eng.wait_ge(drained[b], n + 1)

        def wait_free(eng, *key):
            b, n = tiles[key]
            if n:
                eng.wait_ge(drained[b], n)

        def tile(*key):
            return PS[:, tiles[key][0], 0:N]

        consts_in, x_in, qk_in, v_in, ow_in, up_in, down_in = (sem(n) for n in (
            "consts_in", "x_in", "qk_w_in", "v_w_in", "out_w_in", "up_w_in", "down_w_in"))
        h_in = [sem("h0_in"), sem("h1_in")]
        fills = sem("constants_filled")
        l1w_in = [sem(f"l1_weights{i}_in") for i in range(3)]
        q_full, k_full, s_full, v_full, t_full, pv_full = (sem(n) for n in (
            "q_full", "k_full", "scores_full", "v_full", "turned_full", "pv_full"))
        q_out, v_out, mask_done, s_out, ptD, unD, recip, att_done = (sem(n) for n in (
            "q_padded", "v_stored", "mask_ready", "scores_masked", "pT_by_vector", "att_by_vector",
            "rinv_ready", "attention_done"))
        k_out, exp_done, ptA, unA = (sem(n) for n in ("k_stored", "exp_done", "pT_by_scalar", "att_by_scalar"))
        wide = sem("rinv_spread")
        vb_done, sqr_done, rstd_done, rn_done = (sem(n) for n in (
            "v_bias_added", "rms_squares", "rms_rstd", "rms_done"))
        lsq_done, lrs_done, xn_done, xe_done, edge_done, sx_done = (sem(n) for n in (
            "ln_squares", "ln_rstd", "ln_scaled", "ln_done", "shift_edge", "shift_done"))
        xx_done, xf_done = sem("mixed_x"), sem("mix_ready")
        dec_done, stage_out = sem("decay_done"), [sem(f"stage{i}_out") for i in range(4)]
        loaded = [[sem(f"{n}{c}_loaded") for n in "KVRW"] for c in range(NCH)]
        s0_in = sem("state_in")
        ruk, ruku, rk_done, wb_zero, wb_done, s0_done, a_done, scan_done, p_done, acc_done = (sem(n) for n in (
            "rk_product", "rk_bonus", "rk_sum", "decay_edge", "decay_spread", "state_placed", "kv_done", "scan_done",
            "r_times_state", "accumulated"))
        vrk_done, y_sum, y_mean, y_cent, y_sq, y_var, y_rs, y_norm, y_st = (sem(n) for n in (
            "bonus_term", "y_summed", "y_mean", "y_centered", "y_squares", "y_var", "y_rstd", "y_normed", "y_stored"))
        y_in, y_aff, y_gated = [sem("yT0_in"), sem("yT1_in")], sem("y_affine"), sem("y_gated")
        fm_done, kk_done, rv_done, o_done, o_st = (sem(n) for n in (
            "ffn_mixed", "relu_squared", "ffn_gated", "result_done", "result_stored"))

        scratch = {n: nc.dram_tensor(f"scratch_{n}", [NCH, CB, C, T], F32).ap() for n in ("k", "v", "r", "w", "y")}
        block = ctx.enter_context(nc.Block())

        L1W = [(mix_w1, "mix_w1", 0), (mix_w2, "mix_w2", 0), (dec_w1, "dec_w1", 0), (dec_w2, "dec_w2", 0),
               (rkvg_w["k"], "Wk", 1), (rkvg_w["v"], "Wv", 1), (rkvg_w["r"], "Wr", 1), (rkvg_w["g"], "Wg", 2)]
        L1N = [16 * sum(g == i for _, _, g in L1W) for i in range(3)]
        LAST = {1: (wo_w, "Wo"), 2: (fr_w, "fWr"), 3: (fk_w, "fWk"), 4: (fv_w, "fWv")}
        last_in = {f: sem(LAST[f][1] + "_in") for f in LAST}

        def flat(v):
            return v.rearrange("p a b -> p (a b)") if len(v.shape) == 3 else v

        def stored_count(c, f, m):
            return (c * 4 + f) * KT + m

        @block.sync
        def _(sp):
            def load_batch(n, u, i, first):
                if not first:
                    sp.wait_ge(qk_in, 32)
                    sp.wait_ge(v_full, values_used)
                    sp.wait_ge(mask_done, masks_used)
                    sp.reg_add(values_used, values_used, 4)
                    sp.reg_add(masks_used, masks_used, 1)
                rows = slice(n * P, n * P + P) if first else bass.ds(n * P, P)
                sp.dma_start(flat(hT[u]), d["h"][rows, :]).then_inc(h_in[u], 16)
                row = slice(n, n + 1) if first else bass.ds(n, 1)
                sp.dma_start(mask_in[u][0:T, :].bitcast(I32),
                             d["mask"][row, :].to_broadcast([T, NCTX])).then_inc(h_in[u], 16)

            sp.dma_start(flat(q_w), d["q_w"]).then_inc(qk_in, 16)
            load_batch(0, 0, 0, True)
            sp.dma_start(arena[:, 0:NVEC], d["vec"]).then_inc(consts_in, 16)
            sp.dma_start(ident, d["ident"]).then_inc(consts_in, 16)
            sp.dma_start(head_mask, d["head_mask"]).then_inc(consts_in, 16)
            sp.dma_start(flat(k_w), d["k_w"]).then_inc(qk_in, 16)
            sp.dma_start(flat(v_w), d["v_w"]).then_inc(v_in, 16)
            load_batch(1, 1, 0, True)
            sp.dma_start(state01.rearrange("p a b c -> p (a b c)"), d["state01"]).then_inc(x_in, 16)
            sp.dma_start(bonus, d["bonus"]).then_inc(x_in, 16)
            sp.dma_start(flat(xT), d["x"]).then_inc(x_in, 16)
            sp.dma_start(flat(out_w), d["out_w"]).then_inc(ow_in, 16)
            sp.dma_start(flat(up_w), d["up_w"]).then_inc(up_in, 16)
            sp.dma_start(flat(down_w), d["down_w"]).then_inc(down_in, 16)
            values_used, masks_used = sp.alloc_register("values_used"), sp.alloc_register("masks_used")
            sp.reg_mov(values_used, 4)
            sp.reg_mov(masks_used, 1)
            with sp.Fori(1, B // 2) as i:
                for u in range(2):
                    load_batch(i * 2 + u, u, i, False)
            sp.wait_ge(att_done, B)
            for dst, name, g in L1W:
                sp.dma_start(flat(dst), d[name]).then_inc(l1w_in[g], 16)
            for c in range(NCH):
                sp.dma_start(s0[c], d["state"][c * P:c * P + P, :]).then_inc(s0_in, 16)

            def store_tile(c, f, m):
                n = stored_count(c, f, m)
                name = MIXES[f]
                if f == 0:
                    sp.wait_ge(dec_done, c * KT + m + 1)
                else:
                    wait_drained(sp, "proj", c, f, m)
                sp.dma_start(scratch[name][c, :, m * P:m * P + P, :].rearrange("b p t -> p b t"),
                             stage[n % 4].rearrange("p (b t) -> p b t", t=T)).then_inc(stage_out[n % 4], 16)

            for st, c, *a in sched:
                if st == "dec2":
                    for m in range(KT):
                        store_tile(c, 0, m)
                elif st == "proj":
                    for m in range(KT if a[0] < 4 else 0):
                        store_tile(c, a[0], m)
                    if c == NCH - 1:
                        wait_full(sp, "proj", c, a[0], KT - 1)
                        sp.dma_start(flat(LAST[a[0]][0]), d[LAST[a[0]][1]]).then_inc(last_in[a[0]], 16)
                elif st == "load":
                    if c:
                        sp.wait_ge(y_sum, c)
                        sp.wait_ge(p_done, RS * c)
                        sp.wait_ge(wb_done, RS * c)
                    for k in range(4):
                        sp.wait_ge(stage_out[k], 16 * 4 * (c + 1))
                    for k, (buf, name) in enumerate(((Kl, "k"), (Vl, "v"), (Rl, "r"), (Wl, "w"))):
                        sp.dma_start(flat(buf), scratch[name][c].rearrange("b (h s) t -> (b h) (s t)", s=RS)
                                     ).then_inc(loaded[c][k], 16)
                elif st == "gn":
                    sp.wait_ge(y_norm, c + 1)
                    sp.dma_start(scratch["y"][c].rearrange("b (h s) t -> (b h) (s t)", s=RS),
                                 flat(slots[1])).then_inc(y_st, 16)
                elif st == "yturn":
                    sp.wait_ge(y_st, 16 * (c + 1))
                    wait_full(sp, "proj", c, 4, KT - 1)
                    for m in range(KT):
                        sp.dma_start(sq[c][:, m, :].rearrange("p (b t) -> p b t", t=T),
                                     scratch["y"][c, :, m * P:m * P + P, :].rearrange("b p t -> p b t")
                                     ).then_inc(y_in[c], 16)
                elif st == "fv":
                    for m in range(KT):
                        sp.wait_ge(o_done, c * KT + m + 1)
                        sp.dma_start(out[:, m, c * N:(c + 1) * N], xT[:, m, c * N:(c + 1) * N]).then_inc(o_st, 16)
            sp.wait_ge(o_st, 16 * KT * NCH)

        @block.tensor
        def _(pe):
            def attention(n, u, i, first):
                h = hT[u]
                pe.wait_ge(h_in[u], i * 32 + 32)
                if first and u == 0:
                    pe.wait_ge(qk_in, 32)
                if not first or u:
                    pe.wait_ge(v_out, n * 4 - 2)
                for m in range(KT):
                    for k in range(KT):
                        mm = pe.matmul(PS[:, 0, m * T:(m + 1) * T], q_w[:, k, m * P:(m + 1) * P],
                                       h[:, k, NCTX:NKEY], start=(k == 0), stop=(k == KT - 1))
                mm.then_inc(q_full, 1)
                for m in range(KT):
                    if m == 2:
                        pe.wait_ge(q_out, n + 1)
                    elif m == 3:
                        pe.wait_ge(k_out, n * 4 + 1)
                    elif not first or u:
                        pe.wait_ge(v_out, n * 4 - 1 + m)
                    for k in range(KT):
                        mm = pe.matmul(PS[:, (m + 1) % 3, 0:NKEY], k_w[:, k, m * P:(m + 1) * P], h[:, k, :],
                                       start=(k == 0), stop=(k == KT - 1))
                    mm.then_inc(k_full, 1)

                def scores(g):
                    for j in range(GH):
                        hd = g * GH + j
                        if j == 0:
                            pe.wait_ge(k_out, n * 4 + g + 1)
                        if g == 0 and j == 0:
                            pe.wait_ge(q_out, n + 1)
                        if hd >= 2:
                            pe.wait_ge(s_out, n * NH + hd - 1)
                        pe.matmul(PS[0:T, 3 + hd % 2, 0:NKEY], q_pad[:, hd, :], kT[:, g, :],
                                  start=True, stop=True).then_inc(s_full, 1)

                def turn(g):
                    for kt in range(4):
                        if kt < 2:
                            if g == 0 and kt == 0:
                                if not first or u:
                                    pe.wait_ge(att_done, n)
                            elif g:
                                pe.wait_ge(ptD, n * 8 + 2 * g - 1 + kt)
                            elif not first or u:
                                pe.wait_ge(ptD, n * 8)
                        else:
                            pe.wait_ge(ptA, n * 8 + 2 * g + kt - 1)
                        for j in range(GH):
                            if kt == 0:
                                pe.wait_ge(exp_done, n * NH + g * GH + j + 1)
                            mm = pe.transpose(PS[0:KSZ[kt], 5 + kt % 2, j * T:(j + 1) * T],
                                              probs[g % 2][0:T, j, KOFF[kt]:KOFF[kt] + KSZ[kt]], ident[0:T, 0:T])
                        mm.then_inc(t_full, 1)

                def pv(g):
                    if g or not first or u:
                        pe.wait_ge(unD, n * 4 + g)
                        pe.wait_ge(unA, n * 4 + g)
                    for kt in range(4):
                        if kt < 2:
                            pe.wait_ge(ptA, n * 8 + 2 * g + kt + 1)
                        else:
                            pe.wait_ge(ptD, n * 8 + 2 * g + kt - 1)
                        if g == 0:
                            pe.wait_ge(v_out, n * 4 + kt + 1)
                        mm = pe.matmul(PS[:, 7, 0:GH * T], V[0:KSZ[kt], kt, g * P:(g + 1) * P], pT[0:KSZ[kt], kt, :],
                                       start=(kt == 0), stop=(kt == 3))
                    mm.then_inc(pv_full, 1)

                scores(0)
                if first and u == 0:
                    pe.wait_ge(v_in, 16)
                for kt in range(4):
                    if kt < 3:
                        pe.wait_ge(k_out, n * 4 + 2 + kt)
                    else:
                        pe.wait_ge(v_out, n * 4 + 1)
                    for k in range(KT):
                        mm = pe.matmul(PS[0:KSZ[kt], (5 + kt) % 3, :], h[:, k, KOFF[kt]:KOFF[kt] + KSZ[kt]],
                                       v_w[:, k, :], start=(k == 0), stop=(k == KT - 1))
                    mm.then_inc(v_full, 1)
                for g in range(NG):
                    turn(g)
                    if g + 1 < NG:
                        scores(g + 1)
                    pv(g)
                pe.wait_ge(wide, n + 1)
                pe.wait_ge(ptD, n * 8 + 7)
                for g in range(NG):
                    mm = pe.transpose(PS[:, 5, g * T:(g + 1) * T], rinv_wide[0:T, g * P:(g + 1) * P], ident[0:T, 0:T])
                mm.then_inc(t_full, 1)

            pe.wait_ge(consts_in, 48)
            for u in range(2):
                attention(u, u, 0, True)
            with pe.Fori(1, B // 2) as i:
                for u in range(2):
                    attention(i * 2 + u, u, i, False)

            def product(key, w, m, rhs, tiles_k, waits=None):
                wait_free(pe, *key)
                for k in range(tiles_k):
                    if waits:
                        waits(k)
                    mm = pe.matmul(tile(*key), w[:, k, m * P:(m + 1) * P], rhs(k), start=(k == 0), stop=(k == tiles_k - 1))
                mm.then_inc(full[tiles[key][0]], 1)
                return mm

            def average(key, rhs):
                wait_free(pe, *key)
                for k in range(KT):
                    mm = pe.matmul(tile(*key), mean_w, rhs(k), start=(k == 0), stop=(k == KT - 1))
                mm.then_inc(full[tiles[key][0]], 1)

            pe.wait_ge(fills, 4)
            for st, c, *a in sched:
                cols = slice(c * N, (c + 1) * N)
                if st == "oproj":
                    if c == 0:
                        pe.wait_ge(ow_in, 16)
                        pe.wait_ge(att_done, B)
                    pe.wait_ge(vb_done, KT * (c + 1))
                    for m in range(KT):
                        product(("oproj", c, m), out_w, m, lambda k: attnT[:, k, cols], KT)
                elif st == "rms":
                    pe.wait_ge(sqr_done, KT * (c + 1))
                    average(("rms", c), lambda k: sq_rms[c][:, k, :])
                elif st == "up":
                    if c == 0:
                        pe.wait_ge(up_in, 16)
                    for m in range(*a):
                        product(("up", c, m), up_w, m, lambda k: attnT[:, k, cols], KT,
                                (lambda k: pe.wait_ge(rn_done, KT * c + k + 1)) if m == 0 else None)
                elif st == "down":
                    if c == 0:
                        pe.wait_ge(down_in, 16)
                    for m in range(KT):
                        product(("down", c, m), down_w, m, lambda k: hid[:, k, :], MT,
                                (lambda k: wait_drained(pe, "up", c, k)) if m == 0 else None)
                elif st == "mean":
                    ch = c % 2
                    for m in range(KT):
                        wait_drained(pe, "down" if c < 2 else "wo", ch, m)
                    average(("mean", c), lambda k: xT[:, k, ch * N:(ch + 1) * N])
                elif st == "var":
                    pe.wait_ge(lsq_done, c + 1)
                    average(("var", c), lambda k: sq[c % 2][:, k, :])
                elif st == "mix1":
                    if c == 0:
                        pe.wait_ge(l1w_in[0], L1N[0])
                    for m in range(2):
                        product(("mix1", c, m), mix_w1, m, lambda k: xf[(6 * c) % 2][:, k, :], KT,
                                (lambda k: pe.wait_ge(xx_done, KT * c + k + 1)) if m == 0 else None)
                elif st == "mixf":
                    f = a[0]
                    wait_drained(pe, "mix1", c, 0)
                    wait_drained(pe, "mix1", c, 1)
                    for m in range(KT):
                        key = ("mixf", c, f, m)
                        wait_free(pe, *key)
                        pe.matmul(tile(*key), mix_w2[:, f, m * P:(m + 1) * P], mix_t[f // 4], start=True,
                                  stop=True).then_inc(full[tiles[key][0]], 1)
                elif st == "dec1":
                    key = ("dec1", c)
                    wait_free(pe, *key)
                    for k in range(KT):
                        pe.wait_ge(xf_done, (5 * c) * KT + k + 1)
                        mm = pe.matmul(tile(*key), dec_w1[:, k, :], xf[1][:, k, :], start=(k == 0), stop=(k == KT - 1))
                    mm.then_inc(full[tiles[key][0]], 1)
                elif st == "dec2":
                    wait_drained(pe, "dec1", c)
                    for m in range(KT):
                        key = ("proj", c, 0, m)
                        wait_free(pe, *key)
                        pe.matmul(tile(*key), dec_w2[:, m * P:(m + 1) * P], dec_t, start=True,
                                  stop=True).then_inc(full[tiles[key][0]], 1)
                elif st == "proj":
                    f = a[0]
                    if c == 0 and f == 1:
                        pe.wait_ge(l1w_in[1], L1N[1])
                    if c == 0 and f == 4:
                        pe.wait_ge(l1w_in[2], L1N[2])
                    for m in range(KT):
                        product(("proj", c, f, m), rkvg_w[MIXES[f]], m, lambda k: xf[(f + 1) % 2][:, k, :], KT,
                                (lambda k: pe.wait_ge(xf_done, (5 * c + f) * KT + k + 1)) if m == 0 else None)
                elif st == "scan":
                    s = a[0]
                    pe.wait_ge(p_done, RS * c + s + 1)
                    for m in range(KT):
                        key = ("y", c, m)
                        if s == 0 and c == 0:
                            wait_free(pe, *key)
                        elif s == 0:
                            pe.wait_ge(y_sum, c)
                        mm = pe.matmul(tile(*key), ident, flat(slots[(RS * c + s) % 3])[:, m * N:(m + 1) * N],
                                       start=(s == 0), stop=(s == RS - 1), skip_group_check=True)
                    mm.then_inc(acc_done, 1)
                elif st == "wo":
                    if c == 0:
                        pe.wait_ge(last_in[1], 16)
                    for m in range(KT):
                        product(("wo", c, m), wo_w, m, lambda k: sq[c][:, k, :], KT,
                                (lambda k: pe.wait_ge(y_gated, c + 1)) if m == 0 else None)
                elif st == "fr":
                    if c == 0:
                        pe.wait_ge(last_in[2], 16)
                    for m in range(KT):
                        product(("fr", c, m), fr_w, m, lambda k: xf[0][:, k, :], KT,
                                (lambda k: pe.wait_ge(fm_done, 2 * KT * c + k + 1)) if m == 0 else None)
                elif st == "fk":
                    if c == 0:
                        pe.wait_ge(last_in[3], 16)
                    for m in range(KT):
                        product(("fk", c, m), fk_w, m, lambda k: xf[1][:, k, :], KT,
                                (lambda k: pe.wait_ge(fm_done, 2 * KT * c + KT + k + 1)) if m == 0 else None)
                elif st == "fv":
                    if c == 0:
                        pe.wait_ge(last_in[4], 16)
                    for m in range(KT):
                        product(("fv", c, m), fv_w, m, lambda k: kk[:, k, :], KT,
                                (lambda k: pe.wait_ge(kk_done, KT * c + k + 1)) if m == 0 else None)

        @block.scalar
        def _(act):
            def attention(n, u, i, first):
                for m in range(KT):
                    act.wait_ge(k_full, n * 4 + m + 1)
                    act.activation(kT[:, m, :], PS[:, (m + 1) % 3, 0:NKEY], ACT.Identity,
                                   bias=col("k_b", m)).then_inc(k_out, 1)

                def exps(g):
                    for j in range(GH):
                        hd = g * GH + j
                        if j == 0:
                            if g >= 2:
                                act.wait_ge(t_full, n * 17 + (g - 1) * 4)
                            if g == 0 and (not first or u):
                                act.wait_ge(recip, n)
                        act.wait_ge(s_out, n * NH + hd + 1)
                        act.activation(probs[g % 2][0:T, j, :], S[0:T, hd % 2, :], ACT.Exp, scale=-1.0,
                                       bias=neg_max[0:T, hd:hd + 1],
                                       accum_out=row_sum[0:T, hd:hd + 1]).then_inc(exp_done, 1)

                exps(0)
                for g in range(NG):
                    for kt in range(2):
                        act.wait_ge(t_full, n * 17 + g * 4 + kt + 1)
                        act.copy(pT[0:KSZ[kt], kt, :], PS[0:KSZ[kt], 5 + kt, 0:GH * T]).then_inc(ptA, 1)
                    if g + 1 < NG:
                        exps(g + 1)
                    act.wait_ge(pv_full, n * 4 + g + 1)
                    if g == 0 and (not first or u):
                        act.wait_ge(att_done, n)
                    for j in range(2, GH):
                        ins = act.copy(att_un[j * DH:(j + 1) * DH, g, :], PS[j * DH:(j + 1) * DH, 7, j * T:(j + 1) * T])
                    ins.then_inc(unA, 1)

            act.wait_ge(consts_in, 48)
            for u in range(2):
                attention(u, u, 0, True)
            with act.Fori(1, B // 2) as i:
                for u in range(2):
                    attention(i * 2 + u, u, i, False)

            act.wait_ge(fills, 4)
            for st, c, *a in sched:
                if st == "oproj":
                    for m in range(KT):
                        wait_drained(act, "oproj", c, m)
                        act.activation(sq_rms[c][:, m, :], attnT[:, m, c * N:(c + 1) * N], ACT.Square).then_inc(sqr_done, 1)
                elif st == "rms":
                    wait_full(act, "rms", c)
                    act.activation(rstd[c], tile("rms", c), ACT.Sqrt, bias=eps[:, 0:1]).then_inc(drained[tiles["rms", c][0]], 1)
                elif st == "up":
                    if c and a[0] == 0:
                        for m in range(KT):
                            wait_full(act, "down", c - 1, m)
                    for m in range(*a):
                        wait_full(act, "up", c, m)
                        act.activation(hid[:, m, :], tile("up", c, m), ACT.Gelu_apprx_tanh,
                                       bias=col("mlp_b1", m)).then_inc(drained[tiles["up", c, m][0]], 1)
                elif st == "mean":
                    wait_drained(act, "mean", c)
                    ch = c % 2
                    act.activation(sq[ch], attnT[:, :, ch * N:(ch + 1) * N], ACT.Square).then_inc(lsq_done, 1)
                elif st == "var":
                    ch = c % 2
                    wait_full(act, "var", c)
                    act.activation(rstd[ch], tile("var", c), ACT.Sqrt, bias=eps[:, 1:2]).then_inc(drained[tiles["var", c][0]], 1)
                    for m in range(KT):
                        act.wait_ge(xn_done, KT * c + m + 1)
                        act.activation(xe[ch][:, m, :, 1:T + 1],
                                       attnT[:, m, ch * N:(ch + 1) * N].rearrange("p (b t) -> p b t", t=T),
                                       ACT.Identity, bias=col("ln1_b" if c < 2 else "ln2_b", m)).then_inc(xe_done, 1)
                elif st == "mix1":
                    if c:
                        for m in range(KT):
                            wait_full(act, "mixf", c - 1, 4, m)
                    for m in range(2):
                        wait_full(act, "mix1", c, m)
                        act.activation(mix_t[m], tile("mix1", c, m), ACT.Tanh).then_inc(drained[tiles["mix1", c, m][0]], 1)
                elif st == "dec1":
                    wait_full(act, "dec1", c)
                    act.activation(dec_t, tile("dec1", c), ACT.Tanh).then_inc(drained[tiles["dec1", c][0]], 1)
                elif st == "dec2" or (st == "proj" and a[0] < 4):
                    f = a[0] if a else 0
                    for m in range(KT):
                        n = stored_count(c, f, m)
                        buf = stage[n % 4]
                        if n >= 4:
                            act.wait_ge(stage_out[n % 4], 16 * (n // 4))
                        wait_full(act, "proj", c, f, m)
                        done = drained[tiles["proj", c, f, m][0]]
                        if f == 0:
                            act.activation(buf, tile("proj", c, f, m), ACT.Exp, bias=col("decay", m)).then_inc(done, 1)
                            wait_drained(act, "proj", c, f, m)
                            act.activation(buf, buf, ACT.Exp, scale=-1.0).then_inc(dec_done, 1)
                        else:
                            act.copy(buf, tile("proj", c, f, m)).then_inc(done, 1)
                elif st == "proj":
                    for m in range(KT):
                        wait_full(act, "proj", c, 4, m)
                        act.activation(gate[c][:, m, :], tile("proj", c, 4, m), ACT.Silu).then_inc(
                            drained[tiles["proj", c, 4, m][0]], 1)
                elif st == "scan":
                    s, idx = a[0], RS * c + a[0]
                    slot = slots[idx % 3]
                    if s == 0:
                        act.wait_ge(loaded[c][3], 16)
                        act.wait_ge(wb_zero, c + 1)
                        act.wait_ge(s0_in, 32)
                    else:
                        act.wait_ge(scan_done, idx)
                    act.copy(wb[:, :, 1:T], Wl[:, s:s + 1, 0:T - 1].to_broadcast([P, RS, T - 1])).then_inc(wb_done, 1)
                    if idx >= 3:
                        act.wait_ge(acc_done, idx - 2)
                    if s == 2:
                        act.wait_ge(rk_done, c + 1)
                    act.copy(slot[:, :, 0:1], s0[c][:, s * RS:(s + 1) * RS].rearrange("p (t o) -> p t o", o=1)
                             ).then_inc(s0_done, 1)
                elif st == "gn":
                    act.wait_ge(y_cent, c + 1)
                    act.activation(flat(slots[0]), flat(wb), ACT.Square, scale=0.25).then_inc(y_sq, 1)
                    act.wait_ge(y_var, c + 1)
                    act.activation(gv, gv, ACT.Sqrt, bias=eps[:, 1:2]).then_inc(y_rs, 1)
                elif st == "fr":
                    if c:
                        act.wait_ge(o_done, KT * c)
                    for m in range(KT):
                        wait_full(act, "fr", c, m)
                        act.activation(rr[:, m, :], tile("fr", c, m), ACT.Sigmoid).then_inc(drained[tiles["fr", c, m][0]], 1)
                elif st == "fk":
                    if c:
                        wait_full(act, "fv", c - 1, KT - 1)
                    for m in range(KT):
                        wait_full(act, "fk", c, m)
                        act.activation(kk[:, m, :], tile("fk", c, m), ACT.Relu).then_inc(drained[tiles["fk", c, m][0]], 1)

        @block.vector
        def _(dve):
            def attention(n, u, i, first):
                dve.wait_ge(h_in[u], i * 32 + 32)
                dve.tensor_scalar(mask_add[u][0:T, 0:NCTX], mask_in[u][0:T, :].bitcast(I32), 0.0, -BIG,
                                  ALU.is_equal, ALU.mult).then_inc(mask_done, 1)
                dve.wait_ge(q_full, n + 1)
                for m in range(KT):
                    ins = dve.scalar_tensor_tensor(
                        q_pad[:, m * GH:(m + 1) * GH, :],
                        PS[:, 0, m * T:(m + 1) * T].rearrange("p (o t) -> p o t", o=1).to_broadcast([P, GH, T]),
                        col("q_b", m), head_mask.rearrange("p (h o) -> p h o", o=1).to_broadcast([P, GH, T]),
                        ALU.add, ALU.mult)
                ins.then_inc(q_out, 1)
                dve.wait_ge(mask_done, n + 1)

                def rows(g):
                    for j in range(GH):
                        hd = g * GH + j
                        free, ready = n * NH + hd - 1, n * NH + hd + 1
                        if not first:
                            free, ready = exps_needed, scores_needed
                            dve.reg_add(free, free, 1)
                            dve.reg_add(ready, ready, 1)
                        dve.wait_ge(fills, 4)
                        if hd >= 2 or not first or u:
                            dve.wait_ge(exp_done, free)
                        dve.wait_ge(s_full, ready)
                        dve.tensor_tensor_reduce(S[0:T, hd % 2, :], PS[0:T, 3 + hd % 2, 0:NKEY], mask_add[u][0:T, :],
                                                 -1.0 / DH, 3.0e38, ALU.add, ALU.min,
                                                 neg_max[0:T, hd:hd + 1]).then_inc(s_out, 1)

                rows(0)
                for kt in range(4):
                    dve.wait_ge(v_full, n * 4 + kt + 1)
                    dve.tensor_copy(V[0:KSZ[kt], kt, :], PS[0:KSZ[kt], (5 + kt) % 3, :]).then_inc(v_out, 1)
                for g in range(NG):
                    for kt in range(2, 4):
                        dve.wait_ge(t_full, n * 17 + g * 4 + kt + 1)
                        dve.tensor_copy(pT[0:KSZ[kt], kt, :], PS[0:KSZ[kt], 3 + kt, 0:GH * T]).then_inc(ptD, 1)
                    if g + 1 < NG:
                        rows(g + 1)
                    else:
                        dve.wait_ge(exp_done, n * NH + NH)
                        if not first or u:
                            dve.wait_ge(wide, n)
                        dve.reciprocal(rinv[0:T, :], row_sum[0:T, :]).then_inc(recip, 1)
                    dve.wait_ge(pv_full, n * 4 + g + 1)
                    if g == 0 and (not first or u):
                        dve.wait_ge(att_done, n)
                    for j in range(2):
                        ins = dve.tensor_copy(att_un[j * DH:(j + 1) * DH, g, :],
                                              PS[j * DH:(j + 1) * DH, 7, j * T:(j + 1) * T])
                    ins.then_inc(unD, 1)
                dve.wait_ge(unA, n * 4 + 4)
                dve.wait_ge(unD, n * 4 + 4)
                dve.wait_ge(t_full, n * 17 + 17)
                dst = attnT[:, :, n * T:(n + 1) * T] if first else attnT[:, :, bass.ds(n * T, T)]
                dve.tensor_tensor(dst, att_un, PS[:, 5, 0:KT * T].rearrange("p (g t) -> p g t", t=T),
                                  ALU.mult).then_inc(att_done, 1)

            dve.wait_ge(consts_in, 48)
            for u in range(2):
                attention(u, u, 0, True)
            scores_needed, exps_needed = dve.alloc_register("scores_needed"), dve.alloc_register("exps_needed")
            dve.reg_mov(scores_needed, 2 * NH)
            dve.reg_mov(exps_needed, 2 * NH - 2)
            with dve.Fori(1, B // 2) as i:
                for u in range(2):
                    attention(i * 2 + u, u, i, False)

            dve.wait_ge(x_in, 48)
            for st, c, *a in sched:
                cols = slice(c * N, (c + 1) * N)
                if st == "oproj":
                    for m in range(KT):
                        wait_full(dve, "oproj", c, m)
                    for m in range(KT):
                        dve.scalar_tensor_tensor(attnT[:, m, cols], tile("oproj", c, m), col("out_b", m), xT[:, m, cols],
                                                 ALU.add, ALU.add).then_inc(drained[tiles["oproj", c, m][0]], 1)
                elif st == "rms":
                    wait_drained(dve, "rms", c)
                    dve.reciprocal(rstd[c], rstd[c]).then_inc(rstd_done, 1)
                    dve.wait_ge(rstd_done, c + 1)
                    for m in range(KT):
                        dve.scalar_tensor_tensor(attnT[:, m, cols], attnT[:, m, cols], col("post_w", m), rstd[c],
                                                 ALU.mult, ALU.mult).then_inc(rn_done, 1)
                elif st == "down":
                    for m in range(KT):
                        wait_full(dve, "down", c, m)
                        dve.scalar_tensor_tensor(xT[:, m, cols], tile("down", c, m), col("mlp_b2", m), xT[:, m, cols],
                                                 ALU.add, ALU.add).then_inc(drained[tiles["down", c, m][0]], 1)
                elif st == "mean":
                    ch = c % 2
                    cc = slice(ch * N, (ch + 1) * N)
                    wait_full(dve, "mean", c)
                    if c < 2:
                        for m in range(MT - 4, MT):
                            wait_full(dve, "up", ch, m)
                    dve.tensor_tensor(attnT[:, :, cc], xT[:, :, cc],
                                      tile("mean", c).rearrange("p (o n) -> p o n", o=1).to_broadcast([P, KT, N]),
                                      ALU.subtract).then_inc(drained[tiles["mean", c][0]], 1)
                elif st == "var":
                    ch = c % 2
                    cc = slice(ch * N, (ch + 1) * N)
                    wait_drained(dve, "var", c)
                    dve.reciprocal(rstd[ch], rstd[ch]).then_inc(lrs_done, 1)
                    dve.wait_ge(lrs_done, c + 1)
                    for m in range(KT):
                        dve.scalar_tensor_tensor(attnT[:, m, cc], attnT[:, m, cc], col("ln1_w" if c < 2 else "ln2_w", m),
                                                 rstd[ch], ALU.mult, ALU.mult).then_inc(xn_done, 1)
                elif st == "shift":
                    ch = c % 2
                    dve.wait_ge(xe_done, KT * (c + 1))
                    dve.wait_ge(edge_done, c + 1)
                    for m in range(KT):
                        ins = dve.tensor_tensor(
                            attnT[:, m, ch * N:(ch + 1) * N].rearrange("p (b t) -> p b t", t=T),
                            xe[ch][:, m, :, 0:T], xe[ch][:, m, :, 1:T + 1], ALU.subtract)
                    ins.then_inc(sx_done, 1)
                elif st == "mix1":
                    dve.wait_ge(sx_done, c + 1)
                    if c:
                        wait_full(dve, "proj", c - 1, 3, KT - 1)
                    for m in range(KT):
                        dve.scalar_tensor_tensor(xf[0][:, m, :].rearrange("p (b t) -> p b t", t=T),
                                                 attnT[:, m, cols].rearrange("p (b t) -> p b t", t=T),
                                                 col("maa_x", m), xe[c][:, m, :, 1:T + 1],
                                                 ALU.mult, ALU.add).then_inc(xx_done, 1)
                elif st == "mixf":
                    f = a[0]
                    for m in range(KT):
                        e = (5 * c + f) * KT + m
                        wait_full(dve, "mixf", c, f, m)
                        if e >= 2:
                            dve.wait_ge(xf_done, e - 1)
                        dve.scalar_tensor_tensor(lerp[e % 2], tile("mixf", c, f, m), col("maa_" + MIXES[f], m),
                                                 attnT[:, m, cols], ALU.add, ALU.mult).then_inc(
                                                     drained[tiles["mixf", c, f, m][0]], 1)
                elif st == "prep":
                    dve.wait_ge(ruk, c + 1)
                    prod = slots[(RS * c + 2) % 3]
                    dve.tensor_tensor(prod, prod,
                                      bonus.rearrange("p (s o) -> p s o", o=1).to_broadcast([P, RS, T]),
                                      ALU.mult).then_inc(ruku, 1)
                    dve.wait_ge(ruku, c + 1)
                    dve.tensor_reduce(rk, prod.rearrange("p s t -> p t s"), AX_X, ALU.add).then_inc(rk_done, 1)
                elif st == "scan":
                    s, idx = a[0], RS * c + a[0]
                    slot = slots[idx % 3]
                    if s == 0:
                        dve.wait_ge(loaded[c][0], 16)
                        dve.wait_ge(loaded[c][1], 16)
                        dve.wait_ge(wb_zero, c + 1)
                    if idx >= 3:
                        dve.wait_ge(acc_done, idx - 2)
                    if s == 2:
                        dve.wait_ge(rk_done, c + 1)
                    dve.tensor_tensor(slot[:, :, 1:T], Kl[:, s:s + 1, 0:T - 1].to_broadcast([P, RS, T - 1]),
                                      Vl[:, :, 0:T - 1], ALU.mult).then_inc(a_done, 1)
                    dve.wait_ge(a_done, idx + 1)
                    dve.wait_ge(s0_done, idx + 1)
                    dve.wait_ge(wb_done, idx + 1)
                    dve.tensor_tensor_scan(flat(slot), flat(wb), flat(slot), 0.0, ALU.mult, ALU.add).then_inc(scan_done, 1)
                elif st == "gn":
                    dve.wait_ge(a_done, RS * (c + 1))
                    rk_b = rk.rearrange("p (o t) -> p o t", o=1).to_broadcast([P, RS, T])
                    dve.tensor_tensor(Vl, Vl, rk_b, ALU.mult).then_inc(vrk_done, 1)
                    dve.wait_ge(vrk_done, c + 1)
                    dve.wait_ge(acc_done, RS * (c + 1))
                    dve.wait_ge(scan_done, RS * (c + 1))
                    dve.tensor_tensor(flat(wb).rearrange("p (m n) -> p m n", n=N), PS[:, 4:8, 0:N],
                                      flat(Vl).rearrange("p (m n) -> p m n", n=N), ALU.add).then_inc(y_sum, 1)
                    dve.wait_ge(y_sum, c + 1)
                    by_time = wb.rearrange("p v t -> p t v")
                    dve.tensor_reduce(gm, by_time, AX_X, ALU.add).then_inc(y_mean, 1)
                    dve.wait_ge(y_mean, c + 1)
                    dve.scalar_tensor_tensor(wb, gm.rearrange("p (o t) -> p o t", o=1).to_broadcast([P, RS, T]),
                                             -1.0 / RS, wb, ALU.mult, ALU.add).then_inc(y_cent, 1)
                    dve.wait_ge(y_sq, c + 1)
                    dve.tensor_reduce(gv, slots[0].rearrange("p v t -> p t v"), AX_X, ALU.add).then_inc(y_var, 1)
                    dve.wait_ge(y_rs, 2 * c + 1)
                    dve.reciprocal(gv, gv).then_inc(y_rs, 1)
                    dve.wait_ge(y_rs, 2 * c + 2)
                    dve.tensor_tensor(slots[1], wb, gv.rearrange("p (o t) -> p o t", o=1).to_broadcast([P, RS, T]),
                                      ALU.mult).then_inc(y_norm, 1)
                elif st == "wo":
                    dve.wait_ge(y_in[c], 16 * KT)
                    for m in range(KT):
                        dve.tensor_scalar(sq[c][:, m, :], sq[c][:, m, :], col("gn_w", m), col("gn_b", m),
                                          ALU.mult, ALU.add).then_inc(y_aff, 1)
                    dve.wait_ge(y_aff, KT * (c + 1))
                    for m in range(KT):
                        wait_drained(dve, "proj", c, 4, m)
                    dve.tensor_tensor(sq[c], sq[c], gate[c], ALU.mult).then_inc(y_gated, 1)
                    for m in range(KT):
                        wait_full(dve, "wo", c, m)
                        dve.tensor_tensor(xT[:, m, cols], tile("wo", c, m), xT[:, m, cols], ALU.add).then_inc(
                            drained[tiles["wo", c, m][0]], 1)
                elif st == "fmix":
                    dve.wait_ge(sx_done, c + 3)
                    if c:
                        for m in range(KT):
                            wait_full(dve, "fk", c - 1, m)
                    else:
                        wait_full(dve, "proj", 1, 4, KT - 1)
                    for j, name in enumerate(("fmaa_r", "fmaa_k")):
                        for m in range(KT):
                            dve.scalar_tensor_tensor(xf[j][:, m, :].rearrange("p (b t) -> p b t", t=T),
                                                     attnT[:, m, cols].rearrange("p (b t) -> p b t", t=T),
                                                     col(name, m), xe[c][:, m, :, 1:T + 1],
                                                     ALU.mult, ALU.add).then_inc(fm_done, 1)
                elif st == "fv":
                    for m in range(KT):
                        wait_drained(dve, "fr", c, m)
                        wait_full(dve, "fv", c, m)
                        dve.tensor_tensor(rr[:, m, :], tile("fv", c, m), rr[:, m, :], ALU.mult).then_inc(
                            drained[tiles["fv", c, m][0]], 1)

        @block.gpsimd
        def _(pool):
            pool.memset(mean_w, 1.0 / C).then_inc(fills, 1)
            pool.memset(eps[:, 0:1], EPS_RMS).then_inc(fills, 1)
            pool.memset(eps[:, 1:2], EPS_LN).then_inc(fills, 1)
            for u in range(2):
                ins = pool.memset(mask_add[u][0:T, NCTX:NKEY], 0.0)
            ins.then_inc(fills, 1)

            def attention(n, first):
                ready = n + 1
                if not first:
                    ready = sums_needed
                    pool.reg_add(ready, ready, 1)
                pool.wait_ge(fills, 4)
                pool.wait_ge(recip, ready)
                pool.tensor_copy(rinv_wide[0:T, :].rearrange("p (h e) -> p h e", e=DH),
                                 rinv[0:T, :].rearrange("p (h o) -> p h o", o=1).to_broadcast([T, NH, DH])
                                 ).then_inc(wide, 1)

            for n in range(2):
                attention(n, True)
            sums_needed = pool.alloc_register("sums_needed")
            pool.reg_mov(sums_needed, 2)
            with pool.Fori(1, B // 2) as i:
                for u in range(2):
                    attention(i * 2 + u, False)

            for st, c, *a in sched:
                cols = slice(c * N, (c + 1) * N)
                if st == "oproj":
                    if c == 0:
                        pool.wait_ge(att_done, B)
                    for m in range(KT):
                        pool.tensor_scalar(attnT[:, m, cols], attnT[:, m, cols], col("v_b", m), None,
                                           ALU.add).then_inc(vb_done, 1)
                elif st == "rms":
                    pass
                elif st == "var":
                    ch = c % 2
                    wait_full(pool, "var", c)
                    pool.tensor_copy(xe[ch][:, :, :, 0:1],
                                     state01[:, 1 if c < 2 else 0, :, ch * CB:(ch + 1) * CB].rearrange(
                                         "p k (b o) -> p k b o", o=1)).then_inc(edge_done, 1)
                elif st == "mixf":
                    f = a[0]
                    for m in range(KT):
                        e = (5 * c + f) * KT + m
                        if m == 0:
                            if f == 0 and c:
                                wait_full(pool, "proj", c - 1, 4, KT - 1)
                            if f == 1:
                                wait_full(pool, "mix1", c, 1)
                            if f == 2:
                                wait_full(pool, "dec1", c)
                            if f > 2:
                                wait_full(pool, "proj", c, f - 2, KT - 1)
                        wait_drained(pool, "mixf", c, f, m)
                        pool.tensor_tensor(xf[(f + 1) % 2][:, m, :].rearrange("p (b t) -> p b t", t=T),
                                           lerp[e % 2].rearrange("p (b t) -> p b t", t=T),
                                           xe[c][:, m, :, 1:T + 1], ALU.add).then_inc(xf_done, 1)
                elif st == "prep":
                    pool.wait_ge(loaded[c][0], 16)
                    pool.wait_ge(loaded[c][2], 16)
                    if c:
                        pool.wait_ge(y_st, 16 * c)
                        pool.wait_ge(y_norm, c)
                    pool.memset(wb[:, :, 0:1], 0.0).then_inc(wb_zero, 1)
                    pool.tensor_tensor(slots[(RS * c + 2) % 3], Kl, Rl, ALU.mult).then_inc(ruk, 1)
                elif st == "scan":
                    s, idx = a[0], RS * c + a[0]
                    slot = slots[idx % 3]
                    pool.wait_ge(scan_done, idx + 1)
                    pool.tensor_tensor(slot, slot, Rl[:, s:s + 1, :].to_broadcast([P, RS, T]), ALU.mult).then_inc(p_done, 1)
                elif st == "fk":
                    for m in range(KT):
                        wait_drained(pool, "fk", c, m)
                        pool.tensor_tensor(kk[:, m, :], kk[:, m, :], kk[:, m, :], ALU.mult).then_inc(kk_done, 1)
                elif st == "fv":
                    for m in range(KT):
                        wait_drained(pool, "fv", c, m)
                        pool.tensor_tensor(xT[:, m, cols], rr[:, m, :], xT[:, m, cols], ALU.add).then_inc(o_done, 1)


def kernel(**inputs):
    import concourse.bacc as bacc
    from concourse.bass_utils import run_bass_kernel_spmd

    a = {k: np.asarray(v) for k, v in inputs.items()}
    l0 = {k[len("L0_xattn_"):]: v for k, v in a.items() if k.startswith("L0_xattn_")}
    l1 = {k[len("L1_xattn_"):]: v for k, v in a.items() if k.startswith("L1_xattn_")}

    def rows(w):
        return np.ascontiguousarray(w.reshape(-1, P, w.shape[1]).transpose(1, 0, 2).reshape(P, -1))

    def vector(v):
        return v.reshape(-1, P).T

    x, ctx = a["x"], a["ctx_2048"]
    kv = l0["kv_w"].reshape(C, C, 2)
    kvb = l0["kv_b"].reshape(C, 2)
    h = np.concatenate([ctx, x], axis=1)
    vecs = {"q_b": l0["q_b"], "k_b": kvb[:, 0], "v_b": kvb[:, 1], "out_b": l0["out_b"], "post_w": l0["postnorm_w"],
            "mlp_b1": l0["mlp_b1"], "mlp_b2": l0["mlp_b2"], "decay": l1["time_decay"], "fmaa_k": l1["fmaa_k"],
            "fmaa_r": l1["fmaa_r"], "gn_w": l1["gn_w"], "gn_b": l1["gn_b"]}
    for n in ("ln1_w", "ln1_b", "ln2_w", "ln2_b", "maa_x", "maa_w", "maa_k", "maa_v", "maa_r", "maa_g"):
        vecs[n] = l1[n]
    w1 = np.zeros((C, 2 * P), np.float32)
    w1[:, 0:5 * MIX] = l1["maa_w1"]
    w2 = np.zeros((P, 5, C), np.float32)
    for f in range(5):
        r0 = MIX * (f % 4)
        w2[r0:r0 + MIX, f, :] = l1["maa_w2"][f]
    d1 = np.zeros((C, P), np.float32)
    d1[:, 0:DEC] = l1["decay_w1"]
    d2 = np.zeros((P, C), np.float32)
    d2[0:DEC] = l1["decay_w2"]
    arrays = {
        "h": h.transpose(0, 2, 1).reshape(B, KT, P, NKEY).transpose(0, 2, 1, 3).reshape(B * P, KT * NKEY),
        "x": rows(x.reshape(B * T, C).T),
        "mask": a["mask_BxS2_ik0"],
        "vec": np.concatenate([vector(vecs[n]) for n in VECS], axis=1),
        "ident": np.eye(P, dtype=np.float32),
        "head_mask": (np.arange(P)[:, None] // DH == np.arange(GH)[None, :]).astype(np.float32),
        "state01": ctx[:, 0:2].transpose(2, 1, 0).reshape(KT, P, 2, B).transpose(1, 2, 0, 3).reshape(P, -1),
        "state": ctx[:, 2:2 + RS].reshape(B * RH, RS * RS),
        "bonus": np.tile(l1["faaaa"].reshape(RH, RS), (CB, 1)),
        "q_w": rows(l0["q_w"]), "k_w": rows(kv[:, :, 0]), "v_w": rows(kv[:, :, 1]), "out_w": rows(l0["out_w"]),
        "up_w": rows(l0["mlp_w1"]), "down_w": rows(l0["mlp_w2"]),
        "mix_w1": rows(w1), "mix_w2": w2.reshape(P, 5 * C), "dec_w1": rows(d1), "dec_w2": d2,
    }
    for n in ("Wr", "Wk", "Wv", "Wg", "Wo", "fWk", "fWr", "fWv"):
        arrays[n] = rows(l1[n].T)
    nc = bacc.Bacc("TRN2", target_bir_lowering=False, num_devices=1)
    data, d = {}, {}
    for name, v in arrays.items():
        v = np.ascontiguousarray(v)
        data["in_" + name] = v
        d[name] = nc.dram_tensor("in_" + name, v.shape, mybir.dt.from_np(v.dtype), kind="ExternalInput").ap()
    out = nc.dram_tensor("out_xT", [P, KT, B * T], F32, kind="ExternalOutput").ap()
    xattn_rwkv_kernel(nc, d, out)
    r = run_bass_kernel_spmd(nc, [data], core_ids=[0])
    got = r.results[0]["out_xT"]
    return np.ascontiguousarray(got.reshape(P, KT, B, T).transpose(2, 3, 1, 0).reshape(B, T, C))
```

```python
import numpy as np
import concourse.bass as bass
from concourse import mybir

P = 128
B, T, C = 8, 100, 512
NCTX = 361
NKEY = NCTX + T
NH, DH = 16, 32
KT = C // P
HID = 4 * C
MT = HID // P
GH = P // DH
NG = NH // GH
KOFF = [0, 116, 231, 346]
KSZ = [116, 115, 115, 115]
NCH = 2
CB = B // NCH
N = CB * T
RH, RS = 32, 16
MIX = 32
DEC = 64
KW = NKEY + NKEY % 2
BIG = 1.0e30
EPS_RMS, EPS_LN = 1e-6, 1e-5

F32 = mybir.dt.float32
F32R = mybir.dt.float32r
I32 = mybir.dt.int32
ALU = mybir.AluOpType
ACT = mybir.ActivationFunctionType
AX_X = mybir.AxisListType.X

VECS = ["q_b", "k_b", "v_b", "out_b", "post_w", "mlp_b1", "mlp_b2", "ln1_w", "ln1_b", "ln2_w", "ln2_b",
        "maa_x", "maa_w", "maa_k", "maa_v", "maa_r", "maa_g", "decay", "fmaa_k", "fmaa_r", "gn_w", "gn_b"]
VCOL, _at = {}, 0
for _name in VECS:
    VCOL[_name] = _at
    _at += MT if _name == "mlp_b1" else KT
NVEC = _at
MIXES = ["w", "k", "v", "r", "g"]

TAKES = {"mix1": (5.4, 2.2), "mixf": (2.7, 2.2), "dec1": (2.7, 0), "dec2": (2.7, 0), "proj": (10.8, 0),
         "mean": (2.7, 1.8), "var": (2.7, 4.6), "shift": (0, 1.9), "wo": (10.8, 6.0), "fmix": (0, 4.0),
         "fr": (10.8, 0), "fk": (10.8, 0), "fv": (10.8, 2.2)}
SCAN_TAKES, P_TAKES, ACC_TAKES = 3.7, 4.2, 2.7
RING = 3


def with_recurrence(main, c, lead, after):
    out, tensor, vector, s, acc, ready = [], 0.0, lead, 0, 0, []

    def step():
        nonlocal vector, s
        out.append(("scan", c, s))
        out.extend(after.get(s, []))
        vector += SCAN_TAKES + 3 * len(after.get(s, []))
        ready.append(vector + P_TAKES)
        s += 1

    for st in main:
        while s < RS and vector <= tensor:
            if s >= RING and acc <= s - RING:
                out.append(("acc", c, acc))
                tensor = max(tensor, ready[acc]) + ACC_TAKES
                vector = max(vector, tensor)
                acc += 1
            step()
        while acc < s and ready[acc] <= tensor:
            out.append(("acc", c, acc))
            tensor += ACC_TAKES
            acc += 1
        out.append(st)
        pe, dve = TAKES.get(st[0], (0, 0))
        tensor += pe
        vector += dve
    while acc < RS:
        if s < RS and s - acc < RING:
            step()
        else:
            out.append(("acc", c, acc))
            acc += 1
    return out


def schedule():
    s = [("oproj", 0), ("oproj", 1), ("rms", 0), ("rms", 1)]
    s += [("up", 0, 0, MT), ("down", 0)]
    s += [("up", 1, 0, 4), ("mean", 0), ("up", 1, 4, 10), ("var", 0), ("up", 1, 10, MT), ("shift", 0), ("down", 1)]

    def mixing(c):
        return [("mix1", c), ("mixf", c, 0), ("mixf", c, 1), ("dec1", c), ("mixf", c, 2), ("dec2", c),
                ("proj", c, 1), ("mixf", c, 3), ("proj", c, 2), ("mixf", c, 4), ("proj", c, 3)]

    first = mixing(0)
    s += first[:4] + [("mean", 1)] + first[4:6] + [("var", 1)] + first[6:8] + [("shift", 1)] + first[8:]
    s += [("load", 0), ("loadw", 0), ("proj", 0, 4), ("prep", 0)]
    s += with_recurrence(mixing(1) + [("load", 1)], 0, 4.0, {})
    s += [("loadw", 1), ("gn1", 0), ("prep", 1)]
    s += with_recurrence([("proj", 1, 4), ("wo", 0), ("mean", 2), ("var", 2), ("shift", 2), ("fmix", 0), ("fr", 0)],
                         1, 0.0, {0: [("gn2", 0)], 1: [("gn3", 0)]})
    s += [("gn1", 1), ("gn2", 1), ("gn3", 1), ("fk", 0), ("fv", 0), ("wo", 1), ("mean", 3), ("var", 3),
          ("shift", 3), ("fmix", 1), ("fr", 1), ("fk", 1), ("fv", 1)]
    return s


def plan_banks(sched):
    used, tiles = [0] * 8, {}

    def use(bank, *key):
        tiles[key] = (bank, used[bank])
        used[bank] += 1

    for st, c, *a in sched:
        if st == "oproj":
            for m in range(KT):
                use(4 * c + m, "oproj", c, m)
        elif st == "rms":
            use(4 * c, "rms", c)
        elif st == "up":
            for m in range(*a):
                use(m % 4, "up", c, m)
        elif st == "down":
            for m in range(KT):
                use(4 + m, "down", c, m)
        elif st == "mean":
            use(4 if c < 2 else 0, "mean", c)
        elif st == "var":
            use(5 if c < 2 else 1, "var", c)
        elif st == "mix1":
            for m in range(2):
                use(m, "mix1", c, m)
        elif st == "mixf":
            for m in range(KT):
                use(m % 2, "mixf", c, a[0], m)
        elif st == "dec1":
            use(2, "dec1", c)
        elif st in ("dec2", "proj"):
            f = a[0] if a else 0
            for m in range(KT):
                use(2 + (m + 1) % 2, "proj", c, f, m)
        elif st == "acc" and a[0] == 0:
            for m in range(KT):
                use(4 + m, "y", c, m)
        elif st in ("wo", "fr", "fk", "fv"):
            for m in range(KT):
                use(m, st, c, m)
    return tiles


def xattn_rwkv_kernel(nc, d, out):
    from contextlib import ExitStack
    sched = schedule()
    tiles = plan_banks(sched)

    with ExitStack() as ctx:
        WORDS = 53200
        base = -(-nc.sbuf_base // 32) * 32
        arena = nc.alloc_sbuf_tensor_at("arena", [P, WORDS], F32, offset=base)
        PS = ctx.enter_context(nc.psum_tensor("PS", [P, 8, 512], F32))
        top = [0]

        def pair(name, *shape):
            n = int(np.prod(shape))
            both = []
            for part in ("hi", "lo"):
                top[0] = -(-top[0] // 8) * 8
                t = nc.alloc_sbuf_tensor_at(f"{name}_{part}", [P, n], F32R, offset=base + 4 * top[0])
                top[0] += n
                assert top[0] <= WORDS
                both.append(t[:, :].rearrange("p (a b) -> p a b", b=shape[1]) if len(shape) == 2 else t[:, :])
            return both

        def place(*shape, at=None):
            n = int(np.prod(shape))
            o = top[0] if at is None else at
            if at is None:
                top[0] += n
            assert o + n <= WORDS, (o, n)
            v = arena[:, o:o + n]
            if len(shape) == 2:
                v = v.rearrange("p (a b) -> p a b", b=shape[1])
            if len(shape) == 3:
                v = v.rearrange("p (a b c) -> p a b c", b=shape[1], c=shape[2])
            return v

        vec = place(NVEC)
        ident = place(P)
        mean_w = place(P)
        head_mask = place(GH)
        state01 = place(2, KT, B)
        eps = place(2)
        bonus = place(RS)
        attnT = place(KT, B * T)
        tail = top[0]
        out_w = place(KT, C)
        b_at = top[0]
        up_w = place(KT, HID)
        a_at = top[0]
        k_w, v_w = pair("k_w", KT, C), pair("v_w", KT, C)
        q_w = place(KT, C)
        hT = place(KT, NKEY)
        h2 = pair("h", KT, KW)
        kT = pair("kT", KT, KW)
        V = pair("V", 4, C)
        q_full32 = place(NH, T)
        q_pad = pair("q_pad", NH, T)
        S = place(2, NKEY)
        probs_at = top[0]
        probs = [place(GH, NKEY) for _ in range(2)]
        pT_at = top[0]
        pT = pair("pT", 4, GH * T)
        k_w_in, v_w_in = place(KT, C, at=probs_at), place(KT, C, at=pT_at)
        mask_in = [place(NCTX) for _ in range(2)]
        mask_add = [place(NKEY) for _ in range(2)]
        att_un = place(KT, T)
        rinv_wide = place(C)
        neg_max, row_sum, rinv = place(NH), place(NH), place(NH)
        a_end = top[0]
        top[0] = a_at
        down_w = place(MT, C)
        xT = place(KT, B * T)
        l1_at = top[0]
        mix_w1 = place(KT, 2 * P)
        mix_w2 = place(5, C)
        dec_w1 = place(KT, P)
        dec_w2 = place(C)
        rkvg_w = {n: place(KT, C) for n in "rkvg"}
        wo_w, fr_w, fk_w, fv_w = (rkvg_w[n] for n in "kvrg")
        rstd = [place(N) for _ in range(2)]
        hid_at = top[0]
        hid = place(MT, N)
        c_at = top[0]
        sq_rms = [hid[:, 0:KT, :], hid[:, KT:2 * KT, :]]
        xe = [place(KT, CB, T + 1, at=tail), place(KT, CB, T + 1)]
        sq = [place(KT, N, at=tail), place(KT, N, at=c_at)]
        Wl = place(RS, T)
        V1, R1 = place(RS, T), place(RS, T)
        dec_t = place(N)
        s0 = [place(RS * RS) for _ in range(NCH)]
        rk, gm, gv = place(T), place(T), place(T)
        assert top[0] <= WORDS and a_end <= WORDS, (top[0], a_end)
        top[0] = b_at
        xf = [place(KT, N) for _ in range(2)]
        small_at = top[0]
        mix_t = [place(N) for _ in range(2)]
        stage = [place(N) for _ in range(4)]
        lerp = [place(N) for _ in range(2)]
        gate = [place(KT, N) for _ in range(2)]
        rr, kk = place(KT, N, at=small_at), place(KT, N, at=small_at + KT * N)
        K_of, V_of, R_of = ([place(RS, T)] for _ in range(3))
        K_of.append(place(RS, T))
        V_of.append(V1)
        R_of.append(R1)
        assert top[0] <= l1_at - KT * B * T, (top[0], l1_at)
        top[0] = hid_at
        slots = [place(RS, T) for _ in range(3)]
        wb = place(RS, T)
        assert top[0] <= c_at

        def bank(b, n=512):
            return PS[:, b, 0:n]

        def col(name, m):
            return vec[:, VCOL[name] + m:VCOL[name] + m + 1]

        def sem(name):
            return ctx.enter_context(nc.semaphore(name))

        full = [sem(f"bank{b}_full") for b in range(8)]
        drained = [sem(f"bank{b}_drained") for b in range(8)]

        def wait_full(eng, *key):
            b, n = tiles[key]
            eng.wait_ge(full[b], n + 1)

        def wait_drained(eng, *key):
            b, n = tiles[key]
            eng.wait_ge(drained[b], n + 1)

        def wait_free(eng, *key):
            b, n = tiles[key]
            if n:
                eng.wait_ge(drained[b], n)

        def tile(*key):
            return PS[:, tiles[key][0], 0:N]

        consts_in, x_in, qk_in, k_in, v_in, ow_in, up_in, down_in = (sem(n) for n in (
            "consts_in", "states_in", "q_w_in", "k_w_in", "v_w_in", "out_w_in", "up_w_in", "down_w_in"))
        h_in, m_in = sem("h_in"), [sem("mask0_in"), sem("mask1_in")]
        kw_split, vw_split, h_split, q_raw, q_hi, k_hi, v_hi = (sem(n) for n in (
            "k_w_split", "v_w_split", "h_split", "q_biased", "q_rounded", "k_rounded", "v_rounded"))
        h_hi, x0_in = sem("h_rounded"), sem("latents_in")
        fills = sem("constants_filled")
        l1w_in = [sem(f"l1_weights{i}_in") for i in range(3)]
        q_full, k_full, s_full, v_full, t_full, pv_full = (sem(n) for n in (
            "q_full", "k_full", "scores_full", "v_full", "turned_full", "pv_full"))
        q_out, v_out, mask_done, s_out, pt_out, unD, recip, att_done = (sem(n) for n in (
            "q_stored", "v_stored", "mask_ready", "scores_masked", "pT_stored", "att_by_vector",
            "rinv_ready", "attention_done"))
        k_out, exp_done, pt_hi, unA = (sem(n) for n in ("k_stored", "exp_done", "pT_rounded", "att_by_scalar"))
        wide = sem("rinv_spread")
        vb_done, sqr_done, rstd_done, rn_done = (sem(n) for n in (
            "v_bias_added", "rms_squares", "rms_rstd", "rms_done"))
        lsq_done, lrs_done, xn_done, xe_done, edge_done, sx_done = (sem(n) for n in (
            "ln_squares", "ln_rstd", "ln_scaled", "ln_done", "shift_edge", "shift_done"))
        xx_done, xf_done = sem("mixed_x"), sem("mix_ready")
        dec_done, stage_out = sem("decay_done"), [sem(f"stage{i}_out") for i in range(4)]
        loaded = [[sem(f"{n}{c}_loaded") for n in "KVRW"] for c in range(NCH)]
        s0_in = sem("state_in")
        ruk, ruku, rk_done, wb_zero, wb_done, s0_done, a_done, scan_done, p_done, acc_done = (sem(n) for n in (
            "rk_product", "rk_bonus", "rk_sum", "decay_edge", "decay_spread", "state_placed", "kv_done", "scan_done",
            "r_times_state", "accumulated"))
        vrk_done, y_sum, y_mean, y_cent, y_sq, y_var, y_rs, y_norm, y_st = (sem(n) for n in (
            "bonus_term", "y_summed", "y_mean", "y_centered", "y_squares", "y_var", "y_rstd", "y_normed", "y_stored"))
        y_in, y_aff, y_gated = [sem("yT0_in"), sem("yT1_in")], sem("y_affine"), sem("y_gated")
        fm_done, kk_done, rv_done, o_done, o_st = (sem(n) for n in (
            "ffn_mixed", "relu_squared", "ffn_gated", "result_done", "result_stored"))

        scratch = {n: nc.dram_tensor(f"scratch_{n}", [NCH, CB, C, T], F32).ap() for n in ("k", "v", "r", "w", "y")}
        block = ctx.enter_context(nc.Block())

        L1W = [(mix_w1, "mix_w1", 0), (mix_w2, "mix_w2", 0), (dec_w1, "dec_w1", 0), (dec_w2, "dec_w2", 0),
               (rkvg_w["k"], "Wk", 1), (rkvg_w["v"], "Wv", 1), (rkvg_w["r"], "Wr", 1), (rkvg_w["g"], "Wg", 2)]
        L1N = [16 * sum(g == i for _, _, g in L1W) for i in range(3)]
        LAST = {1: (wo_w, "Wo"), 2: (fr_w, "fWr"), 3: (fk_w, "fWk"), 4: (fv_w, "fWv")}
        last_in = {f: sem(LAST[f][1] + "_in") for f in LAST}

        def flat(v):
            return v.rearrange("p a b -> p (a b)") if len(v.shape) == 3 else v

        def stored_count(c, f, m):
            return (c * 4 + f) * KT + m

        @block.sync
        def _(sp):
            def load_batch(n, u, first):
                if not first:
                    sp.wait_ge(qk_in, 16)
                    sp.wait_ge(mask_done, masks_used)
                    sp.reg_add(masks_used, masks_used, 1)
                row = slice(n, n + 1) if first else bass.ds(n, 1)
                sp.dma_start(mask_in[u][0:T, :].bitcast(I32),
                             d["mask"][row, :].to_broadcast([T, NCTX])).then_inc(m_in[u], 16)
                if not first:
                    sp.wait_ge(qk_in, 16)
                    sp.wait_ge(q_full, batches_used)
                    sp.wait_ge(h_split, batches_used)
                    sp.reg_add(batches_used, batches_used, 1)
                elif n:
                    sp.wait_ge(q_full, n)
                    sp.wait_ge(h_split, n)
                rows = slice(n * P, n * P + P) if first else bass.ds(n * P, P)
                sp.dma_start(flat(hT), d["h"][rows, :]).then_inc(h_in, 16)

            sp.dma_start(flat(q_w), d["q_w"]).then_inc(qk_in, 16)
            load_batch(0, 0, True)
            sp.dma_start(flat(k_w_in), d["k_w"]).then_inc(k_in, 16)
            sp.dma_start(arena[:, 0:NVEC], d["vec"]).then_inc(consts_in, 16)
            sp.dma_start(ident, d["ident"]).then_inc(consts_in, 16)
            sp.dma_start(head_mask, d["head_mask"]).then_inc(consts_in, 16)
            sp.dma_start(flat(v_w_in), d["v_w"]).then_inc(v_in, 16)
            load_batch(1, 1, True)
            sp.dma_start(state01.rearrange("p a b c -> p (a b c)"), d["state01"]).then_inc(x_in, 16)
            sp.dma_start(bonus, d["bonus"]).then_inc(x_in, 16)
            sp.dma_start(flat(out_w), d["out_w"]).then_inc(ow_in, 16)
            sp.dma_start(flat(up_w), d["up_w"]).then_inc(up_in, 16)
            masks_used, batches_used = sp.alloc_register("masks_used"), sp.alloc_register("batches_used")
            sp.reg_mov(masks_used, 1)
            sp.reg_mov(batches_used, 2)
            with sp.Fori(1, B // 2) as i:
                for u in range(2):
                    load_batch(i * 2 + u, u, False)
            sp.wait_ge(att_done, B)
            sp.dma_start(flat(xT), d["x"]).then_inc(x0_in, 16)
            sp.dma_start(flat(down_w), d["down_w"]).then_inc(down_in, 16)
            for dst, name, g in L1W:
                sp.dma_start(flat(dst), d[name]).then_inc(l1w_in[g], 16)
            for c in range(NCH):
                sp.dma_start(s0[c], d["state"][c * P:c * P + P, :]).then_inc(s0_in, 16)

            def store_tile(c, f, m):
                n = stored_count(c, f, m)
                name = MIXES[f]
                if f == 0:
                    sp.wait_ge(dec_done, c * KT + m + 1)
                else:
                    wait_drained(sp, "proj", c, f, m)
                sp.dma_start(scratch[name][c, :, m * P:m * P + P, :].rearrange("b p t -> p b t"),
                             stage[n % 4].rearrange("p (b t) -> p b t", t=T)).then_inc(stage_out[n % 4], 16)

            for st, c, *a in sched:
                if st == "dec2":
                    for m in range(KT):
                        store_tile(c, 0, m)
                elif st == "proj":
                    for m in range(KT if a[0] < 4 else 0):
                        store_tile(c, a[0], m)
                    if c == NCH - 1:
                        wait_full(sp, "proj", c, a[0], KT - 1)
                        sp.dma_start(flat(LAST[a[0]][0]), d[LAST[a[0]][1]]).then_inc(last_in[a[0]], 16)
                elif st == "load":
                    for k in range(4):
                        sp.wait_ge(stage_out[k], 16 * 4 * (c + 1))
                    for k, (buf, name) in enumerate(((K_of, "k"), (V_of, "v"), (R_of, "r"))):
                        sp.dma_start(flat(buf[c]), scratch[name][c].rearrange("b (h s) t -> (b h) (s t)", s=RS)
                                     ).then_inc(loaded[c][k], 16)
                elif st == "loadw":
                    if c:
                        sp.wait_ge(wb_done, RS * c)
                    sp.dma_start(flat(Wl), scratch["w"][c].rearrange("b (h s) t -> (b h) (s t)", s=RS)
                                 ).then_inc(loaded[c][3], 16)
                elif st == "gn3":
                    sp.wait_ge(y_norm, c + 1)
                    sp.dma_start(scratch["y"][c].rearrange("b (h s) t -> (b h) (s t)", s=RS),
                                 flat(K_of[c])).then_inc(y_st, 16)
                    sp.wait_ge(y_st, 16 * (c + 1))
                    wait_full(sp, "proj", c, 4, KT - 1)
                    for m in range(KT):
                        sp.dma_start(sq[c][:, m, :].rearrange("p (b t) -> p b t", t=T),
                                     scratch["y"][c, :, m * P:m * P + P, :].rearrange("b p t -> p b t")
                                     ).then_inc(y_in[c], 16)
                elif st == "fv":
                    for m in range(KT):
                        sp.wait_ge(o_done, c * KT + m + 1)
                        sp.dma_start(out[:, m, c * N:(c + 1) * N], xT[:, m, c * N:(c + 1) * N]).then_inc(o_st, 16)
            sp.wait_ge(o_st, 16 * KT * NCH)

        @block.tensor
        def _(pe):
            def split_product(out, left, right, start, stop):
                pe.matmul(out, left[1], right[0], start=start, stop=False)
                pe.matmul(out, left[0], right[1], start=False, stop=False)
                return pe.matmul(out, left[0], right[0], start=False, stop=stop)

            def attention(n, u, i, first):
                pe.wait_ge(h_in, n * 16 + 16)
                if first and u == 0:
                    pe.wait_ge(qk_in, 16)
                if not first or u:
                    pe.wait_ge(v_out, n * 4 - 2)
                for m in range(KT):
                    for k in range(KT):
                        mm = pe.matmul(PS[:, 0, m * T:(m + 1) * T], q_w[:, k, m * P:(m + 1) * P],
                                       hT[:, k, NCTX:NKEY], start=(k == 0), stop=(k == KT - 1))
                mm.then_inc(q_full, 1)
                pe.wait_ge(h_split, n + 1)
                if first and u == 0:
                    pe.wait_ge(kw_split, 2)
                for m in range(KT):
                    if m == 2:
                        pe.wait_ge(q_raw, n + 1)
                    elif m == 3:
                        pe.wait_ge(k_out, n * 4 + 1)
                    elif not first or u:
                        pe.wait_ge(v_out, n * 4 - 1 + m)
                    for k in range(KT):
                        mm = split_product(PS[:, (m + 1) % 3, 0:KW], [w[:, k, m * P:(m + 1) * P] for w in k_w],
                                           [h[:, k, :] for h in h2], k == 0, k == KT - 1)
                    mm.then_inc(k_full, 1)

                def scores(g, heads):
                    for j in heads:
                        hd = g * GH + j
                        if j == 0:
                            pe.wait_ge(k_out, n * 4 + g + 1)
                        if g == 0 and j == 0:
                            pe.wait_ge(q_out, n + 1)
                        if hd >= 2:
                            pe.wait_ge(s_out, n * NH + hd - 1)
                        split_product(PS[0:T, 3 + hd % 2, 0:KW], [q[:, hd, :] for q in q_pad],
                                      [k[:, g, :] for k in kT], True, True).then_inc(s_full, 1)

                def turn(g, kts):
                    for kt in kts:
                        if g or kt:
                            if g or kt > 1 or not first or u:
                                pe.wait_ge(pt_out, n * 16 + 4 * g + kt - 1)
                        elif not first or u:
                            pe.wait_ge(att_done, n)
                        for j in range(GH):
                            if kt == 0:
                                pe.wait_ge(exp_done, n * NH + g * GH + j + 1)
                            mm = pe.transpose(PS[0:KSZ[kt], 5 + kt % 2, j * T:(j + 1) * T],
                                              probs[g % 2][0:T, j, KOFF[kt]:KOFF[kt] + KSZ[kt]], ident[0:T, 0:T])
                        mm.then_inc(t_full, 1)

                def pv(g):
                    if g or not first or u:
                        pe.wait_ge(unD, n * 4 + g)
                        pe.wait_ge(unA, n * 4 + g)
                    for kt in range(4):
                        pe.wait_ge(pt_out, n * 16 + 4 * g + kt + 1)
                        if g == 0:
                            pe.wait_ge(v_out, n * 4 + kt + 1)
                        mm = split_product(PS[:, 7, 0:GH * T], [v[0:KSZ[kt], kt, g * P:(g + 1) * P] for v in V],
                                           [p[0:KSZ[kt], kt, :] for p in pT], kt == 0, kt == 3)
                    mm.then_inc(pv_full, 1)

                scores(0, range(GH))
                if first and u == 0:
                    pe.wait_ge(vw_split, 2)
                for kt in range(4):
                    if kt < 3:
                        pe.wait_ge(k_out, n * 4 + 2 + kt)
                    else:
                        pe.wait_ge(v_out, n * 4 + 1)
                    for k in range(KT):
                        mm = split_product(PS[0:KSZ[kt], (5 + kt) % 3, :],
                                           [h[:, k, KOFF[kt]:KOFF[kt] + KSZ[kt]] for h in h2],
                                           [w[:, k, :] for w in v_w], k == 0, k == KT - 1)
                    mm.then_inc(v_full, 1)
                for g in range(NG):
                    turn(g, (0, 1))
                    if g + 1 < NG:
                        scores(g + 1, (0, 1))
                    turn(g, (2, 3))
                    if g + 1 < NG:
                        scores(g + 1, (2, 3))
                    pv(g)
                pe.wait_ge(wide, n + 1)
                pe.wait_ge(pt_out, n * 16 + 15)
                for g in range(NG):
                    mm = pe.transpose(PS[:, 5, g * T:(g + 1) * T], rinv_wide[0:T, g * P:(g + 1) * P], ident[0:T, 0:T])
                mm.then_inc(t_full, 1)

            pe.wait_ge(consts_in, 48)
            for u in range(2):
                attention(u, u, 0, True)
            with pe.Fori(1, B // 2) as i:
                for u in range(2):
                    attention(i * 2 + u, u, i, False)

            def product(key, w, m, rhs, tiles_k, waits=None):
                wait_free(pe, *key)
                for k in range(tiles_k):
                    if waits:
                        waits(k)
                    mm = pe.matmul(tile(*key), w[:, k, m * P:(m + 1) * P], rhs(k), start=(k == 0), stop=(k == tiles_k - 1))
                mm.then_inc(full[tiles[key][0]], 1)
                return mm

            def average(key, rhs):
                wait_free(pe, *key)
                for k in range(KT):
                    mm = pe.matmul(tile(*key), mean_w, rhs(k), start=(k == 0), stop=(k == KT - 1))
                mm.then_inc(full[tiles[key][0]], 1)

            pe.wait_ge(fills, 4)
            for st, c, *a in sched:
                cols = slice(c * N, (c + 1) * N)
                if st == "oproj":
                    if c == 0:
                        pe.wait_ge(ow_in, 16)
                        pe.wait_ge(att_done, B)
                    pe.wait_ge(vb_done, KT * (c + 1))
                    for m in range(KT):
                        product(("oproj", c, m), out_w, m, lambda k: attnT[:, k, cols], KT)
                elif st == "rms":
                    pe.wait_ge(sqr_done, KT * (c + 1))
                    average(("rms", c), lambda k: sq_rms[c][:, k, :])
                elif st == "up":
                    if c == 0:
                        pe.wait_ge(up_in, 16)
                    for m in range(*a):
                        product(("up", c, m), up_w, m, lambda k: attnT[:, k, cols], KT,
                                (lambda k: pe.wait_ge(rn_done, KT * c + k + 1)) if m == 0 else None)
                elif st == "down":
                    if c == 0:
                        pe.wait_ge(down_in, 16)
                    for m in range(KT):
                        product(("down", c, m), down_w, m, lambda k: hid[:, k, :], MT,
                                (lambda k: wait_drained(pe, "up", c, k)) if m == 0 else None)
                elif st == "mean":
                    ch = c % 2
                    for m in range(KT):
                        wait_drained(pe, "down" if c < 2 else "wo", ch, m)
                    average(("mean", c), lambda k: xT[:, k, ch * N:(ch + 1) * N])
                elif st == "var":
                    pe.wait_ge(lsq_done, c + 1)
                    average(("var", c), lambda k: sq[c % 2][:, k, :])
                elif st == "mix1":
                    if c == 0:
                        pe.wait_ge(l1w_in[0], L1N[0])
                    for m in range(2):
                        product(("mix1", c, m), mix_w1, m, lambda k: xf[(6 * c) % 2][:, k, :], KT,
                                (lambda k: pe.wait_ge(xx_done, KT * c + k + 1)) if m == 0 else None)
                elif st == "mixf":
                    f = a[0]
                    wait_drained(pe, "mix1", c, 0)
                    wait_drained(pe, "mix1", c, 1)
                    for m in range(KT):
                        key = ("mixf", c, f, m)
                        wait_free(pe, *key)
                        pe.matmul(tile(*key), mix_w2[:, f, m * P:(m + 1) * P], mix_t[f // 4], start=True,
                                  stop=True).then_inc(full[tiles[key][0]], 1)
                elif st == "dec1":
                    key = ("dec1", c)
                    wait_free(pe, *key)
                    for k in range(KT):
                        pe.wait_ge(xf_done, (5 * c) * KT + k + 1)
                        mm = pe.matmul(tile(*key), dec_w1[:, k, :], xf[1][:, k, :], start=(k == 0), stop=(k == KT - 1))
                    mm.then_inc(full[tiles[key][0]], 1)
                elif st == "dec2":
                    wait_drained(pe, "dec1", c)
                    for m in range(KT):
                        key = ("proj", c, 0, m)
                        wait_free(pe, *key)
                        pe.matmul(tile(*key), dec_w2[:, m * P:(m + 1) * P], dec_t, start=True,
                                  stop=True).then_inc(full[tiles[key][0]], 1)
                elif st == "proj":
                    f = a[0]
                    if c == 0 and f == 1:
                        pe.wait_ge(l1w_in[1], L1N[1])
                    if c == 0 and f == 4:
                        pe.wait_ge(l1w_in[2], L1N[2])
                    for m in range(KT):
                        product(("proj", c, f, m), rkvg_w[MIXES[f]], m, lambda k: xf[(f + 1) % 2][:, k, :], KT,
                                (lambda k: pe.wait_ge(xf_done, (5 * c + f) * KT + k + 1)) if m == 0 else None)
                elif st == "acc":
                    s = a[0]
                    pe.wait_ge(p_done, RS * c + s + 1)
                    for m in range(KT):
                        key = ("y", c, m)
                        if s == 0 and c == 0:
                            wait_free(pe, *key)
                        elif s == 0:
                            pe.wait_ge(y_sum, c)
                        mm = pe.matmul(tile(*key), ident, flat(slots[(RS * c + s) % RING])[:, m * N:(m + 1) * N],
                                       start=(s == 0), stop=(s == RS - 1), skip_group_check=True)
                    mm.then_inc(acc_done, 1)
                elif st == "wo":
                    if c == 0:
                        pe.wait_ge(last_in[1], 16)
                    for m in range(KT):
                        product(("wo", c, m), wo_w, m, lambda k: sq[c][:, k, :], KT,
                                (lambda k: pe.wait_ge(y_gated, c + 1)) if m == 0 else None)
                elif st == "fr":
                    if c == 0:
                        pe.wait_ge(last_in[2], 16)
                    for m in range(KT):
                        product(("fr", c, m), fr_w, m, lambda k: xf[0][:, k, :], KT,
                                (lambda k: pe.wait_ge(fm_done, 2 * KT * c + k + 1)) if m == 0 else None)
                elif st == "fk":
                    if c == 0:
                        pe.wait_ge(last_in[3], 16)
                    for m in range(KT):
                        product(("fk", c, m), fk_w, m, lambda k: xf[1][:, k, :], KT,
                                (lambda k: pe.wait_ge(fm_done, 2 * KT * c + KT + k + 1)) if m == 0 else None)
                elif st == "fv":
                    if c == 0:
                        pe.wait_ge(last_in[4], 16)
                    for m in range(KT):
                        product(("fv", c, m), fv_w, m, lambda k: kk[:, k, :], KT,
                                (lambda k: pe.wait_ge(kk_done, KT * c + k + 1)) if m == 0 else None)

        @block.scalar
        def _(act):
            def attention(n, u, i, first):
                for m in range(KT):
                    act.wait_ge(k_full, n * 4 + m + 1)
                    act.activation(kT[0][:, m, :], PS[:, (m + 1) % 3, 0:KW], ACT.Identity,
                                   bias=col("k_b", m)).then_inc(k_hi, 1)

                def exps(g, heads):
                    for j in heads:
                        hd = g * GH + j
                        if j == 0:
                            if g >= 2:
                                act.wait_ge(t_full, n * 17 + (g - 1) * 4)
                            if g == 0 and (not first or u):
                                act.wait_ge(recip, n)
                        act.wait_ge(s_out, n * NH + hd + 1)
                        act.activation(probs[g % 2][0:T, j, :], S[0:T, hd % 2, :], ACT.Exp, scale=-1.0,
                                       bias=neg_max[0:T, hd:hd + 1],
                                       accum_out=row_sum[0:T, hd:hd + 1]).then_inc(exp_done, 1)

                exps(0, range(GH))
                for kt in range(4):
                    act.wait_ge(v_full, n * 4 + kt + 1)
                    act.copy(V[0][0:KSZ[kt], kt, :], PS[0:KSZ[kt], (5 + kt) % 3, :]).then_inc(v_hi, 1)
                for g in range(NG):
                    for half in ((0, 1), (2, 3)):
                        for kt in half:
                            act.wait_ge(t_full, n * 17 + g * 4 + kt + 1)
                            act.copy(pT[0][0:KSZ[kt], kt, :], PS[0:KSZ[kt], 5 + kt % 2, 0:GH * T]).then_inc(pt_hi, 1)
                        if g + 1 < NG:
                            exps(g + 1, half)
                    act.wait_ge(pv_full, n * 4 + g + 1)
                    if g == 0 and (not first or u):
                        act.wait_ge(att_done, n)
                    for j in range(2, GH):
                        ins = act.copy(att_un[j * DH:(j + 1) * DH, g, :], PS[j * DH:(j + 1) * DH, 7, j * T:(j + 1) * T])
                    ins.then_inc(unA, 1)

            act.wait_ge(consts_in, 48)
            for u in range(2):
                attention(u, u, 0, True)
            with act.Fori(1, B // 2) as i:
                for u in range(2):
                    attention(i * 2 + u, u, i, False)

            act.wait_ge(fills, 4)
            for st, c, *a in sched:
                if st == "oproj":
                    for m in range(KT):
                        wait_drained(act, "oproj", c, m)
                        act.activation(sq_rms[c][:, m, :], attnT[:, m, c * N:(c + 1) * N], ACT.Square).then_inc(sqr_done, 1)
                elif st == "rms":
                    wait_full(act, "rms", c)
                    act.activation(rstd[c], tile("rms", c), ACT.Sqrt, bias=eps[:, 0:1]).then_inc(drained[tiles["rms", c][0]], 1)
                elif st == "up":
                    if c and a[0] == 0:
                        for m in range(KT):
                            wait_full(act, "down", c - 1, m)
                    for m in range(*a):
                        wait_full(act, "up", c, m)
                        act.activation(hid[:, m, :], tile("up", c, m), ACT.Gelu_apprx_tanh,
                                       bias=col("mlp_b1", m)).then_inc(drained[tiles["up", c, m][0]], 1)
                elif st == "mean":
                    wait_drained(act, "mean", c)
                    ch = c % 2
                    act.activation(sq[ch], attnT[:, :, ch * N:(ch + 1) * N], ACT.Square).then_inc(lsq_done, 1)
                elif st == "var":
                    ch = c % 2
                    wait_full(act, "var", c)
                    act.activation(rstd[ch], tile("var", c), ACT.Sqrt, bias=eps[:, 1:2]).then_inc(drained[tiles["var", c][0]], 1)
                    for m in range(KT):
                        act.wait_ge(xn_done, KT * c + m + 1)
                        act.activation(xe[ch][:, m, :, 1:T + 1],
                                       attnT[:, m, ch * N:(ch + 1) * N].rearrange("p (b t) -> p b t", t=T),
                                       ACT.Identity, bias=col("ln1_b" if c < 2 else "ln2_b", m)).then_inc(xe_done, 1)
                elif st == "mix1":
                    if c:
                        for m in range(KT):
                            wait_full(act, "mixf", c - 1, 4, m)
                    for m in range(2):
                        wait_full(act, "mix1", c, m)
                        act.activation(mix_t[m], tile("mix1", c, m), ACT.Tanh).then_inc(drained[tiles["mix1", c, m][0]], 1)
                elif st == "dec1":
                    wait_full(act, "dec1", c)
                    act.activation(dec_t, tile("dec1", c), ACT.Tanh).then_inc(drained[tiles["dec1", c][0]], 1)
                elif st == "dec2" or (st == "proj" and a[0] < 4):
                    f = a[0] if a else 0
                    for m in range(KT):
                        n = stored_count(c, f, m)
                        buf = stage[n % 4]
                        if n >= 4:
                            act.wait_ge(stage_out[n % 4], 16 * (n // 4))
                        wait_full(act, "proj", c, f, m)
                        done = drained[tiles["proj", c, f, m][0]]
                        if f == 0:
                            act.activation(buf, tile("proj", c, f, m), ACT.Exp, bias=col("decay", m)).then_inc(done, 1)
                            wait_drained(act, "proj", c, f, m)
                            act.activation(buf, buf, ACT.Exp, scale=-1.0).then_inc(dec_done, 1)
                        else:
                            act.copy(buf, tile("proj", c, f, m)).then_inc(done, 1)
                elif st == "proj":
                    for m in range(KT):
                        wait_full(act, "proj", c, 4, m)
                        act.activation(gate[c][:, m, :], tile("proj", c, 4, m), ACT.Silu).then_inc(
                            drained[tiles["proj", c, 4, m][0]], 1)
                elif st == "scan":
                    s, idx = a[0], RS * c + a[0]
                    slot = slots[idx % RING]
                    if s == 0:
                        act.wait_ge(loaded[c][3], 16)
                        act.wait_ge(wb_zero, 1)
                        act.wait_ge(s0_in, 32)
                    else:
                        act.wait_ge(scan_done, idx)
                    act.copy(wb[:, :, 1:T], Wl[:, s:s + 1, 0:T - 1].to_broadcast([P, RS, T - 1])).then_inc(wb_done, 1)
                    if idx >= RING:
                        act.wait_ge(acc_done, idx - RING + 1)
                    if s == 2:
                        act.wait_ge(rk_done, c + 1)
                    act.copy(slot[:, :, 0:1], s0[c][:, s * RS:(s + 1) * RS].rearrange("p (t o) -> p t o", o=1)
                             ).then_inc(s0_done, 1)
                elif st == "gn1":
                    act.wait_ge(y_cent, c + 1)
                    act.activation(flat(R_of[c]), flat(K_of[c]), ACT.Square, scale=0.25).then_inc(y_sq, 1)
                elif st == "gn2":
                    act.wait_ge(y_var, c + 1)
                    act.activation(gv, gv, ACT.Sqrt, bias=eps[:, 1:2]).then_inc(y_rs, 1)
                elif st == "fr":
                    if c:
                        act.wait_ge(o_done, KT * c)
                    for m in range(KT):
                        wait_full(act, "fr", c, m)
                        act.activation(rr[:, m, :], tile("fr", c, m), ACT.Sigmoid).then_inc(drained[tiles["fr", c, m][0]], 1)
                elif st == "fk":
                    if c:
                        wait_full(act, "fv", c - 1, KT - 1)
                    for m in range(KT):
                        wait_full(act, "fk", c, m)
                        act.activation(kk[:, m, :], tile("fk", c, m), ACT.Relu).then_inc(drained[tiles["fk", c, m][0]], 1)

        @block.vector
        def _(dve):
            def attention(n, u, i, first):
                dve.wait_ge(m_in[u], i * 16 + 16)
                dve.tensor_scalar(mask_add[u][0:T, 0:NCTX], mask_in[u][0:T, :].bitcast(I32), 0.0, -BIG,
                                  ALU.is_equal, ALU.mult).then_inc(mask_done, 1)
                dve.wait_ge(q_full, n + 1)
                for m in range(KT):
                    ins = dve.scalar_tensor_tensor(
                        q_full32[:, m * GH:(m + 1) * GH, :],
                        PS[:, 0, m * T:(m + 1) * T].rearrange("p (o t) -> p o t", o=1).to_broadcast([P, GH, T]),
                        col("q_b", m), head_mask.rearrange("p (h o) -> p h o", o=1).to_broadcast([P, GH, T]),
                        ALU.add, ALU.mult)
                ins.then_inc(q_raw, 1)
                dve.wait_ge(q_raw, n + 1)
                dve.tensor_copy(q_pad[0], q_full32).then_inc(q_hi, 1)
                for m in range(KT):
                    dve.wait_ge(k_hi, n * 4 + m + 1)
                    dve.scalar_tensor_tensor(kT[1][:, m, :], PS[:, (m + 1) % 3, 0:KW], col("k_b", m),
                                             kT[0][:, m, :].bitcast(F32), ALU.add, ALU.subtract).then_inc(k_out, 1)
                dve.wait_ge(mask_done, n + 1)

                def rows(g, heads):
                    for j in heads:
                        hd = g * GH + j
                        free, ready = n * NH + hd - 1, n * NH + hd + 1
                        if not first:
                            free, ready = exps_needed, scores_needed
                            dve.reg_add(free, free, 1)
                            dve.reg_add(ready, ready, 1)
                        dve.wait_ge(fills, 4)
                        if hd >= 2 or not first or u:
                            dve.wait_ge(exp_done, free)
                        dve.wait_ge(s_full, ready)
                        dve.tensor_tensor_reduce(S[0:T, hd % 2, :], PS[0:T, 3 + hd % 2, 0:NKEY], mask_add[u][0:T, :],
                                                 -1.0 / DH, 3.0e38, ALU.add, ALU.min,
                                                 neg_max[0:T, hd:hd + 1]).then_inc(s_out, 1)

                rows(0, range(GH))
                for kt in range(4):
                    dve.wait_ge(v_hi, n * 4 + kt + 1)
                    dve.tensor_tensor(V[1][0:KSZ[kt], kt, :], PS[0:KSZ[kt], (5 + kt) % 3, :],
                                      V[0][0:KSZ[kt], kt, :].bitcast(F32), ALU.subtract).then_inc(v_out, 1)
                for g in range(NG):
                    for half in ((0, 1), (2, 3)):
                        for kt in half:
                            dve.wait_ge(pt_hi, n * 16 + g * 4 + kt + 1)
                            dve.tensor_tensor(pT[1][0:KSZ[kt], kt, :], PS[0:KSZ[kt], 5 + kt % 2, 0:GH * T],
                                              pT[0][0:KSZ[kt], kt, :].bitcast(F32), ALU.subtract).then_inc(pt_out, 1)
                        if g + 1 < NG:
                            rows(g + 1, half)
                    if g + 1 == NG:
                        dve.wait_ge(exp_done, n * NH + NH)
                        if not first or u:
                            dve.wait_ge(wide, n)
                        dve.reciprocal(rinv[0:T, :], row_sum[0:T, :]).then_inc(recip, 1)
                    dve.wait_ge(pv_full, n * 4 + g + 1)
                    if g == 0 and (not first or u):
                        dve.wait_ge(att_done, n)
                    for j in range(2):
                        ins = dve.tensor_copy(att_un[j * DH:(j + 1) * DH, g, :],
                                              PS[j * DH:(j + 1) * DH, 7, j * T:(j + 1) * T])
                    ins.then_inc(unD, 1)
                dve.wait_ge(unA, n * 4 + 4)
                dve.wait_ge(unD, n * 4 + 4)
                dve.wait_ge(t_full, n * 17 + 17)
                dst = attnT[:, :, n * T:(n + 1) * T] if first else attnT[:, :, bass.ds(n * T, T)]
                dve.tensor_tensor(dst, att_un, PS[:, 5, 0:KT * T].rearrange("p (g t) -> p g t", t=T),
                                  ALU.mult).then_inc(att_done, 1)

            for w, raw, arrived, done in ((k_w, k_w_in, k_in, kw_split), (v_w, v_w_in, v_in, vw_split)):
                dve.wait_ge(arrived, 16)
                dve.tensor_copy(w[0], raw).then_inc(done, 1)
                dve.wait_ge(done, 1)
                dve.tensor_tensor(w[1], raw, w[0].bitcast(F32), ALU.subtract).then_inc(done, 1)
            dve.wait_ge(consts_in, 48)
            for u in range(2):
                attention(u, u, 0, True)
            scores_needed, exps_needed = dve.alloc_register("scores_needed"), dve.alloc_register("exps_needed")
            dve.reg_mov(scores_needed, 2 * NH)
            dve.reg_mov(exps_needed, 2 * NH - 2)
            with dve.Fori(1, B // 2) as i:
                for u in range(2):
                    attention(i * 2 + u, u, i, False)

            dve.wait_ge(x_in, 32)
            dve.wait_ge(x0_in, 16)
            for st, c, *a in sched:
                cols = slice(c * N, (c + 1) * N)
                if st == "oproj":
                    for m in range(KT):
                        wait_full(dve, "oproj", c, m)
                    for m in range(KT):
                        dve.scalar_tensor_tensor(attnT[:, m, cols], tile("oproj", c, m), col("out_b", m), xT[:, m, cols],
                                                 ALU.add, ALU.add).then_inc(drained[tiles["oproj", c, m][0]], 1)
                elif st == "rms":
                    wait_drained(dve, "rms", c)
                    dve.reciprocal(rstd[c], rstd[c]).then_inc(rstd_done, 1)
                    dve.wait_ge(rstd_done, c + 1)
                    for m in range(KT):
                        dve.scalar_tensor_tensor(attnT[:, m, cols], attnT[:, m, cols], col("post_w", m), rstd[c],
                                                 ALU.mult, ALU.mult).then_inc(rn_done, 1)
                elif st == "down":
                    for m in range(KT):
                        wait_full(dve, "down", c, m)
                        dve.scalar_tensor_tensor(xT[:, m, cols], tile("down", c, m), col("mlp_b2", m), xT[:, m, cols],
                                                 ALU.add, ALU.add).then_inc(drained[tiles["down", c, m][0]], 1)
                elif st == "mean":
                    ch = c % 2
                    cc = slice(ch * N, (ch + 1) * N)
                    wait_full(dve, "mean", c)
                    if c < 2:
                        for m in range(MT - 4, MT):
                            wait_full(dve, "up", ch, m)
                    dve.tensor_tensor(attnT[:, :, cc], xT[:, :, cc],
                                      tile("mean", c).rearrange("p (o n) -> p o n", o=1).to_broadcast([P, KT, N]),
                                      ALU.subtract).then_inc(drained[tiles["mean", c][0]], 1)
                elif st == "var":
                    ch = c % 2
                    cc = slice(ch * N, (ch + 1) * N)
                    wait_drained(dve, "var", c)
                    dve.reciprocal(rstd[ch], rstd[ch]).then_inc(lrs_done, 1)
                    dve.wait_ge(lrs_done, c + 1)
                    for m in range(KT):
                        dve.scalar_tensor_tensor(attnT[:, m, cc], attnT[:, m, cc], col("ln1_w" if c < 2 else "ln2_w", m),
                                                 rstd[ch], ALU.mult, ALU.mult).then_inc(xn_done, 1)
                elif st == "shift":
                    ch = c % 2
                    dve.wait_ge(xe_done, KT * (c + 1))
                    dve.wait_ge(edge_done, c + 1)
                    for m in range(KT):
                        ins = dve.tensor_tensor(
                            attnT[:, m, ch * N:(ch + 1) * N].rearrange("p (b t) -> p b t", t=T),
                            xe[ch][:, m, :, 0:T], xe[ch][:, m, :, 1:T + 1], ALU.subtract)
                    ins.then_inc(sx_done, 1)
                elif st == "mix1":
                    dve.wait_ge(sx_done, c + 1)
                    if c:
                        wait_full(dve, "proj", c - 1, 3, KT - 1)
                    for m in range(KT):
                        dve.scalar_tensor_tensor(xf[0][:, m, :].rearrange("p (b t) -> p b t", t=T),
                                                 attnT[:, m, cols].rearrange("p (b t) -> p b t", t=T),
                                                 col("maa_x", m), xe[c][:, m, :, 1:T + 1],
                                                 ALU.mult, ALU.add).then_inc(xx_done, 1)
                elif st == "mixf":
                    f = a[0]
                    for m in range(KT):
                        e = (5 * c + f) * KT + m
                        wait_full(dve, "mixf", c, f, m)
                        if e >= 2:
                            dve.wait_ge(xf_done, e - 1)
                        dve.scalar_tensor_tensor(lerp[e % 2], tile("mixf", c, f, m), col("maa_" + MIXES[f], m),
                                                 attnT[:, m, cols], ALU.add, ALU.mult).then_inc(
                                                     drained[tiles["mixf", c, f, m][0]], 1)
                elif st == "prep":
                    dve.wait_ge(ruk, c + 1)
                    prod = slots[(RS * c + 2) % RING]
                    dve.tensor_tensor(prod, prod,
                                      bonus.rearrange("p (s o) -> p s o", o=1).to_broadcast([P, RS, T]),
                                      ALU.mult).then_inc(ruku, 1)
                    dve.wait_ge(ruku, c + 1)
                    dve.tensor_reduce(rk, prod.rearrange("p s t -> p t s"), AX_X, ALU.add).then_inc(rk_done, 1)
                elif st == "scan":
                    s, idx = a[0], RS * c + a[0]
                    slot = slots[idx % RING]
                    if s == 0:
                        dve.wait_ge(loaded[c][0], 16)
                        dve.wait_ge(loaded[c][1], 16)
                        dve.wait_ge(wb_zero, 1)
                    if idx >= RING:
                        dve.wait_ge(acc_done, idx - RING + 1)
                    if s == 2:
                        dve.wait_ge(rk_done, c + 1)
                    dve.tensor_tensor(slot[:, :, 1:T], K_of[c][:, s:s + 1, 0:T - 1].to_broadcast([P, RS, T - 1]),
                                      V_of[c][:, :, 0:T - 1], ALU.mult).then_inc(a_done, 1)
                    dve.wait_ge(a_done, idx + 1)
                    dve.wait_ge(s0_done, idx + 1)
                    dve.wait_ge(wb_done, idx + 1)
                    dve.tensor_tensor_scan(flat(slot), flat(wb), flat(slot), 0.0, ALU.mult, ALU.add).then_inc(scan_done, 1)
                elif st == "gn1":
                    Vl, yb = V_of[c], K_of[c]
                    dve.wait_ge(a_done, RS * (c + 1))
                    rk_b = rk.rearrange("p (o t) -> p o t", o=1).to_broadcast([P, RS, T])
                    dve.tensor_tensor(Vl, Vl, rk_b, ALU.mult).then_inc(vrk_done, 1)
                    dve.wait_ge(vrk_done, c + 1)
                    dve.wait_ge(acc_done, RS * (c + 1))
                    dve.wait_ge(scan_done, RS * (c + 1))
                    dve.tensor_tensor(flat(yb).rearrange("p (m n) -> p m n", n=N), PS[:, 4:8, 0:N],
                                      flat(Vl).rearrange("p (m n) -> p m n", n=N), ALU.add).then_inc(y_sum, 1)
                    dve.wait_ge(y_sum, c + 1)
                    by_time = yb.rearrange("p v t -> p t v")
                    dve.tensor_reduce(gm, by_time, AX_X, ALU.add).then_inc(y_mean, 1)
                    dve.wait_ge(y_mean, c + 1)
                    dve.scalar_tensor_tensor(yb, gm.rearrange("p (o t) -> p o t", o=1).to_broadcast([P, RS, T]),
                                             -1.0 / RS, yb, ALU.mult, ALU.add).then_inc(y_cent, 1)
                elif st == "gn2":
                    dve.wait_ge(y_sq, c + 1)
                    dve.tensor_reduce(gv, R_of[c].rearrange("p v t -> p t v"), AX_X, ALU.add).then_inc(y_var, 1)
                elif st == "gn3":
                    dve.wait_ge(y_rs, 2 * c + 1)
                    dve.reciprocal(gv, gv).then_inc(y_rs, 1)
                    dve.wait_ge(y_rs, 2 * c + 2)
                    dve.tensor_tensor(K_of[c], K_of[c], gv.rearrange("p (o t) -> p o t", o=1).to_broadcast([P, RS, T]),
                                      ALU.mult).then_inc(y_norm, 1)
                elif st == "wo":
                    dve.wait_ge(y_in[c], 16 * KT)
                    for m in range(KT):
                        dve.tensor_scalar(sq[c][:, m, :], sq[c][:, m, :], col("gn_w", m), col("gn_b", m),
                                          ALU.mult, ALU.add).then_inc(y_aff, 1)
                    dve.wait_ge(y_aff, KT * (c + 1))
                    for m in range(KT):
                        wait_drained(dve, "proj", c, 4, m)
                    dve.tensor_tensor(sq[c], sq[c], gate[c], ALU.mult).then_inc(y_gated, 1)
                    for m in range(KT):
                        wait_full(dve, "wo", c, m)
                        dve.tensor_tensor(xT[:, m, cols], tile("wo", c, m), xT[:, m, cols], ALU.add).then_inc(
                            drained[tiles["wo", c, m][0]], 1)
                elif st == "fmix":
                    dve.wait_ge(sx_done, c + 3)
                    if c:
                        for m in range(KT):
                            wait_full(dve, "fk", c - 1, m)
                    else:
                        wait_full(dve, "proj", 1, 4, KT - 1)
                    for j, name in enumerate(("fmaa_r", "fmaa_k")):
                        for m in range(KT):
                            dve.scalar_tensor_tensor(xf[j][:, m, :].rearrange("p (b t) -> p b t", t=T),
                                                     attnT[:, m, cols].rearrange("p (b t) -> p b t", t=T),
                                                     col(name, m), xe[c][:, m, :, 1:T + 1],
                                                     ALU.mult, ALU.add).then_inc(fm_done, 1)
                elif st == "fv":
                    for m in range(KT):
                        wait_drained(dve, "fr", c, m)
                        wait_full(dve, "fv", c, m)
                        dve.tensor_tensor(rr[:, m, :], tile("fv", c, m), rr[:, m, :], ALU.mult).then_inc(
                            drained[tiles["fv", c, m][0]], 1)

        @block.gpsimd
        def _(pool):
            pool.memset(mean_w, 1.0 / C).then_inc(fills, 1)
            pool.memset(eps[:, 0:1], EPS_RMS).then_inc(fills, 1)
            pool.memset(eps[:, 1:2], EPS_LN).then_inc(fills, 1)
            for u in range(2):
                ins = pool.memset(mask_add[u][0:T, NCTX:NKEY], 0.0)
            ins.then_inc(fills, 1)

            def split_h(n, first):
                ready, free = n * 16 + 16, n * 4
                if not first:
                    ready, free = h_needed, v_needed
                pool.wait_ge(fills, 4)
                pool.wait_ge(h_in, ready)
                if not first or n:
                    pool.wait_ge(v_full, free)
                pool.tensor_scalar(h2[0][:, :, 0:NKEY], hT, 1.0, None, ALU.mult).then_inc(h_hi, 1)
                done = n + 1
                if not first:
                    done = h_done
                pool.wait_ge(h_hi, done)
                pool.tensor_tensor(h2[1][:, :, 0:NKEY], hT, h2[0][:, :, 0:NKEY].bitcast(F32),
                                   ALU.subtract).then_inc(h_split, 1)
                if not first:
                    pool.reg_add(h_needed, h_needed, 16)
                    pool.reg_add(v_needed, v_needed, 4)
                    pool.reg_add(h_done, h_done, 1)

            def split_q(n, first):
                pool.wait_ge(q_hi, n + 1)
                pool.tensor_tensor(q_pad[1], q_full32, q_pad[0].bitcast(F32), ALU.subtract).then_inc(q_out, 1)

            def spread_rinv(n, first):
                ready = n + 1 if first else sums_needed
                pool.wait_ge(fills, 4)
                pool.wait_ge(recip, ready)
                pool.tensor_copy(rinv_wide[0:T, :].rearrange("p (h e) -> p h e", e=DH),
                                 rinv[0:T, :].rearrange("p (h o) -> p h o", o=1).to_broadcast([T, NH, DH])
                                 ).then_inc(wide, 1)
                if not first:
                    pool.reg_add(sums_needed, sums_needed, 1)

            for part in h2:
                pool.memset(part[:, :, NKEY:KW].bitcast(F32), 0.0)
            split_h(0, True)
            split_q(0, True)
            split_h(1, True)
            spread_rinv(0, True)
            split_q(1, True)
            h_needed, v_needed, h_done, sums_needed = (pool.alloc_register(n) for n in (
                "h_needed", "v_needed", "h_done", "sums_needed"))
            pool.reg_mov(h_needed, 48)
            pool.reg_mov(v_needed, 8)
            pool.reg_mov(h_done, 3)
            pool.reg_mov(sums_needed, 2)
            with pool.Fori(1, B // 2) as i:
                for u in range(2):
                    split_h(i * 2 + u, False)
                    spread_rinv(i * 2 + u - 1, False)
                    split_q(i * 2 + u, False)
            spread_rinv(B - 1, True)

            for st, c, *a in sched:
                cols = slice(c * N, (c + 1) * N)
                if st == "oproj":
                    if c == 0:
                        pool.wait_ge(att_done, B)
                    for m in range(KT):
                        pool.tensor_scalar(attnT[:, m, cols], attnT[:, m, cols], col("v_b", m), None,
                                           ALU.add).then_inc(vb_done, 1)
                elif st == "rms":
                    pass
                elif st == "var":
                    ch = c % 2
                    wait_full(pool, "var", c)
                    pool.tensor_copy(xe[ch][:, :, :, 0:1],
                                     state01[:, 1 if c < 2 else 0, :, ch * CB:(ch + 1) * CB].rearrange(
                                         "p k (b o) -> p k b o", o=1)).then_inc(edge_done, 1)
                elif st == "mixf":
                    f = a[0]
                    for m in range(KT):
                        e = (5 * c + f) * KT + m
                        if m == 0:
                            if f == 0 and c:
                                wait_full(pool, "proj", c - 1, 4, KT - 1)
                            if f == 1:
                                wait_full(pool, "mix1", c, 1)
                            if f == 2:
                                wait_full(pool, "dec1", c)
                            if f > 2:
                                wait_full(pool, "proj", c, f - 2, KT - 1)
                        wait_drained(pool, "mixf", c, f, m)
                        pool.tensor_tensor(xf[(f + 1) % 2][:, m, :].rearrange("p (b t) -> p b t", t=T),
                                           lerp[e % 2].rearrange("p (b t) -> p b t", t=T),
                                           xe[c][:, m, :, 1:T + 1], ALU.add).then_inc(xf_done, 1)
                elif st == "prep":
                    pool.wait_ge(loaded[c][0], 16)
                    pool.wait_ge(loaded[c][2], 16)
                    if c:
                        pool.wait_ge(acc_done, RS * c)
                    else:
                        pool.memset(wb[:, :, 0:1], 0.0).then_inc(wb_zero, 1)
                    pool.tensor_tensor(slots[(RS * c + 2) % RING], K_of[c], R_of[c], ALU.mult).then_inc(ruk, 1)
                elif st == "scan":
                    s, idx = a[0], RS * c + a[0]
                    slot = slots[idx % RING]
                    pool.wait_ge(scan_done, idx + 1)
                    pool.tensor_tensor(slot, slot, R_of[c][:, s:s + 1, :].to_broadcast([P, RS, T]), ALU.mult).then_inc(p_done, 1)
                elif st == "fk":
                    for m in range(KT):
                        wait_drained(pool, "fk", c, m)
                        pool.tensor_tensor(kk[:, m, :], kk[:, m, :], kk[:, m, :], ALU.mult).then_inc(kk_done, 1)
                elif st == "fv":
                    for m in range(KT):
                        wait_drained(pool, "fv", c, m)
                        pool.tensor_tensor(xT[:, m, cols], rr[:, m, :], xT[:, m, cols], ALU.add).then_inc(o_done, 1)


def kernel(**inputs):
    import concourse.bacc as bacc
    from concourse.bass_utils import run_bass_kernel_spmd

    a = {k: np.asarray(v) for k, v in inputs.items()}
    l0 = {k[len("L0_xattn_"):]: v for k, v in a.items() if k.startswith("L0_xattn_")}
    l1 = {k[len("L1_xattn_"):]: v for k, v in a.items() if k.startswith("L1_xattn_")}

    def rows(w):
        return np.ascontiguousarray(w.reshape(-1, P, w.shape[1]).transpose(1, 0, 2).reshape(P, -1))

    def vector(v):
        return v.reshape(-1, P).T

    x, ctx = a["x"], a["ctx_2048"]
    kv = l0["kv_w"].reshape(C, C, 2)
    kvb = l0["kv_b"].reshape(C, 2)
    h = np.concatenate([ctx, x], axis=1)
    vecs = {"q_b": l0["q_b"], "k_b": kvb[:, 0], "v_b": kvb[:, 1], "out_b": l0["out_b"], "post_w": l0["postnorm_w"],
            "mlp_b1": l0["mlp_b1"], "mlp_b2": l0["mlp_b2"], "decay": l1["time_decay"], "fmaa_k": l1["fmaa_k"],
            "fmaa_r": l1["fmaa_r"], "gn_w": l1["gn_w"], "gn_b": l1["gn_b"]}
    for n in ("ln1_w", "ln1_b", "ln2_w", "ln2_b", "maa_x", "maa_w", "maa_k", "maa_v", "maa_r", "maa_g"):
        vecs[n] = l1[n]
    w1 = np.zeros((C, 2 * P), np.float32)
    w1[:, 0:5 * MIX] = l1["maa_w1"]
    w2 = np.zeros((P, 5, C), np.float32)
    for f in range(5):
        r0 = MIX * (f % 4)
        w2[r0:r0 + MIX, f, :] = l1["maa_w2"][f]
    d1 = np.zeros((C, P), np.float32)
    d1[:, 0:DEC] = l1["decay_w1"]
    d2 = np.zeros((P, C), np.float32)
    d2[0:DEC] = l1["decay_w2"]
    arrays = {
        "h": h.transpose(0, 2, 1).reshape(B, KT, P, NKEY).transpose(0, 2, 1, 3).reshape(B * P, KT * NKEY),
        "x": rows(x.reshape(B * T, C).T),
        "mask": a["mask_BxS2_ik0"],
        "vec": np.concatenate([vector(vecs[n]) for n in VECS], axis=1),
        "ident": np.eye(P, dtype=np.float32),
        "head_mask": (np.arange(P)[:, None] // DH == np.arange(GH)[None, :]).astype(np.float32),
        "state01": ctx[:, 0:2].transpose(2, 1, 0).reshape(KT, P, 2, B).transpose(1, 2, 0, 3).reshape(P, -1),
        "state": ctx[:, 2:2 + RS].reshape(B * RH, RS * RS),
        "bonus": np.tile(l1["faaaa"].reshape(RH, RS), (CB, 1)),
        "q_w": rows(l0["q_w"]), "k_w": rows(kv[:, :, 0]), "v_w": rows(kv[:, :, 1]), "out_w": rows(l0["out_w"]),
        "up_w": rows(l0["mlp_w1"]), "down_w": rows(l0["mlp_w2"]),
        "mix_w1": rows(w1), "mix_w2": w2.reshape(P, 5 * C), "dec_w1": rows(d1), "dec_w2": d2,
    }
    for n in ("Wr", "Wk", "Wv", "Wg", "Wo", "fWk", "fWr", "fWv"):
        arrays[n] = rows(l1[n].T)
    nc = bacc.Bacc("TRN2", target_bir_lowering=False, num_devices=1)
    data, d = {}, {}
    for name, v in arrays.items():
        v = np.ascontiguousarray(v)
        data["in_" + name] = v
        d[name] = nc.dram_tensor("in_" + name, v.shape, mybir.dt.from_np(v.dtype), kind="ExternalInput").ap()
    out = nc.dram_tensor("out_xT", [P, KT, B * T], F32, kind="ExternalOutput").ap()
    xattn_rwkv_kernel(nc, d, out)
    r = run_bass_kernel_spmd(nc, [data], core_ids=[0])
    got = r.results[0]["out_xT"]
    return np.ascontiguousarray(got.reshape(P, KT, B, T).transpose(2, 3, 1, 0).reshape(B, T, C))
```

```python
import numpy as np
import concourse.bass as bass
from concourse import mybir

P = 128
B, T, C = 8, 100, 512
NCTX = 361
NKEY = NCTX + T
NH, DH = 16, 32
KT = C // P
HID = 4 * C
MT = HID // P
GH = P // DH
NG = NH // GH
KOFF = [0, 116, 231, 346]
KSZ = [116, 115, 115, 115]
NCH = 2
CB = B // NCH
N = CB * T
RH, RS = 32, 16
MIX = 32
DEC = 64
PARTS = 3
KW = NKEY + NKEY % 2
BIG = 1.0e30
EPS_RMS, EPS_LN = 1e-6, 1e-5

F32 = mybir.dt.float32
F32R = mybir.dt.float32r
I32 = mybir.dt.int32
ALU = mybir.AluOpType
ACT = mybir.ActivationFunctionType
AX_X = mybir.AxisListType.X

VECS = ["q_b", "k_b", "v_b", "out_b", "post_w", "mlp_b1", "mlp_b2", "ln1_w", "ln1_b", "ln2_w", "ln2_b",
        "maa_x", "maa_w", "maa_k", "maa_v", "maa_r", "maa_g", "decay", "fmaa_k", "fmaa_r", "gn_w", "gn_b"]
VCOL, _at = {}, 0
for _name in VECS:
    VCOL[_name] = _at
    _at += MT if _name == "mlp_b1" else KT
NVEC = _at
MIXES = ["w", "k", "v", "r", "g"]

RING = 3

STAGES = """
    oproj 0 0, oproj 0 1, oproj 0 2, oproj 0 3, oproj 1 0, oproj 1 1, rsum 0, rms 0, oproj 1 2, rn 0,
    oproj 1 3, mlp 0 0 1, rsum 1, mlp 0 1 2, mlp 0 2 3, mlp 0 3 4, rms 1, mlp 0 4 5, mlp 0 5 6, mlp 0 6 7,
    mlp 0 7 8, mlp 0 8 9, mlp 0 9 10, mlp 0 10 11, mlp 0 11 12, mlp 0 12 13, mlp 0 13 14, mlp 0 14 15,
    mlp 0 15 16, rn 1, mlpend 0, mlp 1 0 1, down 0, mlp 1 1 2, mlp 1 2 3, mlp 1 3 4, mlp 1 4 5, mlp 1 5 6,
    msum 0, mlp 1 6 7, mean 0, vsum 0, mlp 1 7 8, mlp 1 8 9, mlp 1 9 10, mlp 1 10 11, mlp 1 11 12,
    mlp 1 12 13, mlp 1 13 14, var 0, shift 0, mlp 1 14 15, mlp 1 15 16, mlpend 1, down 1, msum 1, mix1 0,
    mixf 0 0, mixf 0 1, dec1 0, mixf 0 2, dec2 0, mean 1, proj 0 1 0, proj 0 1 1, proj 0 1 2, vsum 1,
    proj 0 1 3, mixf 0 3, proj 0 2 0, proj 0 2 1, var 1, proj 0 2 2, proj 0 2 3, mixf 0 4, proj 0 3 0,
    proj 0 3 1, shift 1, proj 0 3 2, proj 0 3 3, load 0, proj 0 4 0, proj 0 4 1, mix1 1, proj 0 4 2,
    proj 0 4 3, loadw 0, mixf 1 0, mixf 1 1, scan 0 0, dec1 1, mixf 1 2, prep 0, scan 0 1, dec2 1,
    proj 1 1 0, acc 0 0, proj 1 1 1, scan 0 2, proj 1 1 2, proj 1 1 3, mixf 1 3, acc 0 1, scan 0 3,
    proj 1 2 0, acc 0 2, scan 0 4, proj 1 2 1, scan 0 5, proj 1 2 2, acc 0 3, scan 0 6, acc 0 4, proj 1 2 3,
    scan 0 7, acc 0 5, acc 0 6, mixf 1 4, scan 0 8, proj 1 3 0, scan 0 9, proj 1 3 1, acc 0 7, scan 0 10,
    proj 1 3 2, acc 0 8, scan 0 11, acc 0 9, scan 0 12, proj 1 3 3, acc 0 10, acc 0 11, scan 0 13, scan 0 14,
    acc 0 12, acc 0 13, load 1, scan 0 15, acc 0 14, loadw 1, scan 1 0, scan 1 1, acc 0 15, gn1 0,
    proj 1 4 0, acc 1 0, prep 1, gn2 0, scan 1 2, gn3 0, acc 1 1, proj 1 4 1, scan 1 3, acc 1 2, acc 1 3,
    scan 1 4, acc 1 4, scan 1 5, gated 0, scan 1 6, scan 1 7, wo 0 0, acc 1 5, wo 0 1, scan 1 8, acc 1 6,
    scan 1 9, wo 0 2, wo 0 3, msum 2, acc 1 7, acc 1 8, scan 1 10, scan 1 11, acc 1 9, scan 1 12, mean 2,
    acc 1 10, acc 1 11, scan 1 13, acc 1 12, scan 1 14, vsum 2, proj 1 4 2, acc 1 13, scan 1 15, var 2,
    shift 2, proj 1 4 3, acc 1 14, acc 1 15, fmix 0, fr 0 0, fr 0 1, gn1 1, gn2 1, fr 0 2, fr 0 3, fk 0 0,
    gn3 1, fk 0 1, fk 0 2, fk 0 3, fv 0 0, gated 1, fv 0 1, wo 1 0, wo 1 1, wo 1 2, wo 1 3, msum 3, fv 0 2,
    mean 3, vsum 3, fv 0 3, var 3, shift 3, fmix 1, fr 1 0, fr 1 1, fr 1 2, fr 1 3, fk 1 0, fk 1 1, fk 1 2,
    fk 1 3, fv 1 0, fv 1 1, fv 1 2, fv 1 3
"""


def schedule():
    stages = []
    for entry in STAGES.replace("\n", " ").split(","):
        name, *numbers = entry.split()
        stages.append((name, *(int(x) for x in numbers)))
    return stages


def plan_banks(sched):
    used, tiles = [0] * 8, {}

    def use(bank, *key):
        tiles[key] = (bank, used[bank])
        used[bank] += 1

    for st, c, *a in sched:
        if st == "oproj":
            use(4 * c + a[0], "oproj", c, a[0])
        elif st == "rms":
            use(2 + c, "rms", c)
        elif st == "mlp":
            for m in range(*a):
                use(m % 2, "up", c, m)
                if m == 2:
                    for t in range(KT):
                        use(4 + t, "down", c, t)
        elif st == "mean":
            use((2, 4, 0, 0)[c], "mean", c)
        elif st == "var":
            use((3, 5, 1, 1)[c], "var", c)
        elif st == "mix1":
            for m in range(2):
                use(m, "mix1", c, m)
        elif st == "mixf":
            for m in range(KT):
                use(m % 2, "mixf", c, a[0], m)
        elif st == "dec1":
            use(2, "dec1", c)
        elif st in ("dec2", "proj"):
            f = a[0] if a else 0
            for m in a[1:] or range(KT):
                use(2 + (m + 1) % 2, "proj", c, f, m)
        elif st == "acc" and a[0] == 0:
            for m in range(KT):
                use(4 + m, "y", c, m)
        elif st in ("wo", "fr", "fk", "fv"):
            use(a[0], st, c, a[0])
    return tiles


def xattn_rwkv_kernel(nc, d, out):
    from contextlib import ExitStack
    sched = schedule()
    tiles = plan_banks(sched)

    with ExitStack() as ctx:
        WORDS = 53200
        base = -(-nc.sbuf_base // 32) * 32
        arena = nc.alloc_sbuf_tensor_at("arena", [P, WORDS], F32, offset=base)
        PS = ctx.enter_context(nc.psum_tensor("PS", [P, 8, 512], F32))
        top = [0]

        def pair(name, *shape, at=None):
            n = int(np.prod(shape))
            both, kept = [], top[0]
            if at is not None:
                top[0] = at
            for part in ("hi", "lo"):
                top[0] = -(-top[0] // 8) * 8
                t = nc.alloc_sbuf_tensor_at(f"{name}_{part}", [P, n], F32R, offset=base + 4 * top[0])
                top[0] += n
                assert top[0] <= WORDS
                both.append(t[:, :].rearrange("p (a b) -> p a b", b=shape[1]) if len(shape) == 2 else t[:, :])
            if at is not None:
                top[0] = kept
            return both

        def place(*shape, at=None):
            n = int(np.prod(shape))
            o = top[0] if at is None else at
            if at is None:
                top[0] += n
            assert o + n <= WORDS, (o, n)
            v = arena[:, o:o + n]
            if len(shape) == 2:
                v = v.rearrange("p (a b) -> p a b", b=shape[1])
            if len(shape) == 3:
                v = v.rearrange("p (a b c) -> p a b c", b=shape[1], c=shape[2])
            return v

        vec = place(NVEC)
        ident = place(P)
        mean_w = place(P)
        head_mask = place(GH)
        state01 = place(2, KT, B)
        eps = place(2)
        bonus = place(RS)
        attnT = place(KT, B * T)
        tail = top[0]
        out_w = place(KT, C)
        b_at = top[0]
        up_w = place(KT, HID)
        a_at = top[0]
        k_w, v_w = pair("k_w", KT, C), pair("v_w", KT, C)
        q_w = place(KT, C)
        hT = place(KT, NKEY)
        h2 = pair("h", KT, KW)
        kT = pair("kT", KT, KW)
        V = pair("V", 4, C)
        q_full32 = place(NH, T)
        q_pad = pair("q_pad", NH, T)
        S = place(2, NKEY)
        probs_at = top[0]
        probs = [place(GH, NKEY) for _ in range(2)]
        pT_at = top[0]
        pT = pair("pT", 4, GH * T)
        k_w_in, v_w_in = place(KT, C, at=probs_at), place(KT, C, at=pT_at)
        mask_in = [place(NCTX) for _ in range(2)]
        mask_add = [place(NKEY) for _ in range(2)]
        att_un = place(KT, T)
        rinv_wide = place(C)
        neg_max, row_sum, rinv = place(NH), place(NH), place(NH)
        a_end = top[0]
        top[0] = a_at
        down_w = place(MT, C)
        xT = place(KT, B * T)
        l1_at = top[0]
        mix_w1 = place(KT, 2 * P)
        mix_w2 = place(5, C)
        dec_w1 = place(KT, P)
        dec_w2 = place(C)
        rkvg_w = {n: place(KT, C) for n in "rkvg"}
        wo_w, fr_w, fk_w, fv_w = (rkvg_w[n] for n in "kvrg")
        rstd = [place(N) for _ in range(2)]
        hid_at = top[0]
        rn2 = pair("normed", KT, N)
        up_part = [pair(f"up_w{i}", KT, P) for i in range(PARTS)]
        down_part = [pair(f"down_w{i}", C) for i in range(PARTS)]
        ring_at = top[0]
        hid = [pair(f"hidden{i}", N) for i in range(PARTS)]
        gelu = [place(N) for _ in range(2)]
        mlp_end = top[0]
        sq_rms = [place(KT, N, at=ring_at), place(KT, N, at=tail)]
        top[0] = c_at = hid_at + 4 * RS * T
        xe = [place(KT, CB, T + 1, at=tail), place(KT, CB, T + 1)]
        sq = [place(KT, N, at=tail), place(KT, N, at=c_at)]
        wl_at = top[0]
        Wl = place(RS, T)
        top[0] = -(-top[0] // 8) * 8
        xp = [rn2, pair("mixed", KT, N, at=top[0])]
        V1, R1 = place(RS, T), place(RS, T)
        dec_t = place(N)
        assert mlp_end <= top[0]
        s0 = [place(RS * RS) for _ in range(NCH)]
        rk, gm, gv = place(T), place(T), place(T)
        assert top[0] <= WORDS and a_end <= WORDS, (top[0], a_end)
        top[0] = b_at
        xf = [place(KT, N) for _ in range(2)]
        small_at = top[0]
        mix_t = [place(N) for _ in range(2)]
        stage = [place(N) for _ in range(4)]
        lerp = [place(N) for _ in range(2)]
        gate = [place(KT, N) for _ in range(2)]
        rr, kk = place(KT, N, at=small_at), place(KT, N, at=small_at + KT * N)
        top[0] = -(-top[0] // 8) * 8
        k0_at = top[0]
        K_of, V_of, R_of = ([place(RS, T)] for _ in range(3))
        K_of.append(place(RS, T))
        V_of.append(V1)
        R_of.append(R1)
        assert top[0] <= l1_at - KT * B * T, (top[0], l1_at)
        gated_p = relu_p = pair("gated", KT, N, at=k0_at)
        fmix_p = [pair("ffn_r", KT, N, at=k0_at + 2 * KT * N), pair("ffn_k", KT, N, at=-(-wl_at // 8) * 8)]
        top[0] = hid_at
        slots = [place(RS, T) for _ in range(3)]
        wb = place(RS, T)
        assert top[0] <= c_at

        def bank(b, n=512):
            return PS[:, b, 0:n]

        def score_bank(hd):
            return (3, 4, 6, 7)[hd] if hd < GH else (3, 4, 1, 2)[hd % GH]

        def turn_bank(g, kt):
            return (5, 6, 3, 4)[kt] if g == NG - 1 else 5 + kt % 2

        def col(name, m):
            return vec[:, VCOL[name] + m:VCOL[name] + m + 1]

        def sem(name):
            return ctx.enter_context(nc.semaphore(name))

        full = [sem(f"bank{b}_full") for b in range(8)]
        drained = [sem(f"bank{b}_drained") for b in range(8)]

        def wait_full(eng, *key):
            b, n = tiles[key]
            eng.wait_ge(full[b], n + 1)

        def wait_drained(eng, *key):
            b, n = tiles[key]
            eng.wait_ge(drained[b], n + 1)

        def wait_free(eng, *key):
            b, n = tiles[key]
            if n:
                eng.wait_ge(drained[b], n)

        def wait_step(eng, j):
            c, k = j // MT, j % MT
            if k == MT - 1:
                wait_full(eng, "down", c, KT - 1)
            else:
                eng.wait_ge(step_done, c * (MT - 1) + k + 1)

        def tile(*key):
            return PS[:, tiles[key][0], 0:N]

        consts_in, x_in, qk_in, k_in, v_in, ow_in, up_in, down_in = (sem(n) for n in (
            "consts_in", "states_in", "q_w_in", "k_w_in", "v_w_in", "out_w_in", "up_w_in", "down_w_in"))
        h_in, m_in = sem("h_in"), [sem("mask0_in"), sem("mask1_in")]
        kw_split, vw_split, h_split, q_raw, q_hi, k_hi, v_hi = (sem(n) for n in (
            "k_w_split", "v_w_split", "h_split", "q_biased", "q_rounded", "k_rounded", "v_rounded"))
        h_hi, x0_in = sem("h_rounded"), sem("latents_in")
        padded, kw_hi, vw_hi = sem("h_padded"), sem("k_w_rounded"), sem("v_w_rounded")
        fills = sem("constants_filled")
        l1w_in = [sem(f"l1_weights{i}_in") for i in range(3)]
        q_full, k_full, s_full, v_full, t_full, pv_full = (sem(n) for n in (
            "q_full", "k_full", "scores_full", "v_full", "turned_full", "pv_full"))
        q_out, v_out, mask_done, s_out, pt_out, unD, recip, att_done = (sem(n) for n in (
            "q_stored", "v_stored", "mask_ready", "scores_masked", "pT_stored", "att_by_vector",
            "rinv_ready", "attention_done"))
        k_out, exp_done, pt_hi, unA = (sem(n) for n in ("k_stored", "exp_done", "pT_rounded", "att_by_scalar"))
        wide = sem("rinv_spread")
        tp_hi, tp_split, tw_hi, tw_split = (sem(n) for n in (
            "operand_rounded", "operand_split", "weight_rounded", "weight_split"))
        xp_hi, xp_split = sem("mix_rounded"), sem("mix_split")
        rn_hi, rn_split, upw_hi, upw_split, dw_hi, dw_split, gelu_done, hid_hi, hid_split, step_done = (sem(n) for n in (
            "normed_rounded", "normed_split", "up_w_rounded", "up_w_split", "down_w_rounded", "down_w_split",
            "gelu_done", "hidden_rounded", "hidden_split", "down_step"))
        vb_done, sqr_done, rhalf_done, rsum_done, rstd_done, rn_done = (sem(n) for n in (
            "v_bias_added", "rms_squares", "rms_half_sum", "rms_sum", "rms_rstd", "rms_done"))
        centered, lsq_done, mhalf_done, msum_done, vhalf_done, vsum_done, lrs_done, xn_done, xe_done, edge_done, sx_done = (sem(n) for n in (
            "ln_centered", "ln_squares", "mean_half_sum", "mean_sum", "var_half_sum", "var_sum", "ln_rstd", "ln_scaled", "ln_done", "shift_edge", "shift_done"))
        xx_done, xf_done = sem("mixed_x"), sem("mix_ready")
        dec_done, stage_out = sem("decay_done"), [sem(f"stage{i}_out") for i in range(4)]
        loaded = [[sem(f"{n}{c}_loaded") for n in "KVRW"] for c in range(NCH)]
        s0_in = sem("state_in")
        ruk, ruku, rk_done, wb_zero, wb_done, s0_done, a_done, scan_done, p_done, acc_done = (sem(n) for n in (
            "rk_product", "rk_bonus", "rk_sum", "decay_edge", "decay_spread", "state_placed", "kv_done", "scan_done",
            "r_times_state", "accumulated"))
        vrk_done, y_sum, y_mean, y_cent, y_sq, y_var, y_rs, y_norm, y_st = (sem(n) for n in (
            "bonus_term", "y_summed", "y_mean", "y_centered", "y_squares", "y_var", "y_rstd", "y_normed", "y_stored"))
        y_in, y_aff, y_gated = [sem("yT0_in"), sem("yT1_in")], sem("y_affine"), sem("y_gated")
        fm_done, kk_done, rv_done, o_done, o_st = (sem(n) for n in (
            "ffn_mixed", "relu_squared", "ffn_gated", "result_done", "result_stored"))

        scratch = {n: nc.dram_tensor(f"scratch_{n}", [NCH, CB, C, T], F32).ap() for n in ("k", "v", "r", "w", "y")}
        block = ctx.enter_context(nc.Block())

        L1W = [(mix_w1, "mix_w1", 0), (mix_w2, "mix_w2", 0), (dec_w1, "dec_w1", 0), (dec_w2, "dec_w2", 0),
               (rkvg_w["k"], "Wk", 1), (rkvg_w["v"], "Wv", 1), (rkvg_w["r"], "Wr", 1), (rkvg_w["g"], "Wg", 2)]
        L1N = [16 * sum(g == i for _, _, g in L1W) for i in range(3)]
        LAST = {1: (wo_w, "Wo"), 2: (fr_w, "fWr"), 3: (fk_w, "fWk"), 4: (fv_w, "fWv")}
        last_in = {f: sem(LAST[f][1] + "_in") for f in LAST}

        def flat(v):
            return v.rearrange("p a b -> p (a b)") if len(v.shape) == 3 else v

        TAIL = ["wo", "fr", "fk", "fv"]

        def stored_count(c, f, m):
            return (c * 4 + f) * KT + m

        @block.sync
        def _(sp):
            def load_batch(n, u, first):
                if not first:
                    sp.wait_ge(qk_in, 16)
                    sp.wait_ge(mask_done, masks_used)
                    sp.reg_add(masks_used, masks_used, 1)
                row = slice(n, n + 1) if first else bass.ds(n, 1)
                sp.dma_start(mask_in[u][0:T, :].bitcast(I32),
                             d["mask"][row, :].to_broadcast([T, NCTX])).then_inc(m_in[u], 16)
                if not first:
                    sp.wait_ge(qk_in, 16)
                    sp.wait_ge(q_full, batches_used)
                    sp.wait_ge(h_split, batches_used)
                    sp.reg_add(batches_used, batches_used, 1)
                elif n:
                    sp.wait_ge(q_full, n)
                    sp.wait_ge(h_split, n)
                rows = slice(n * P, n * P + P) if first else bass.ds(n * P, P)
                sp.dma_start(flat(hT), d["h"][rows, :]).then_inc(h_in, 16)

            sp.dma_start(flat(q_w), d["q_w"]).then_inc(qk_in, 16)
            load_batch(0, 0, True)
            sp.dma_start(flat(k_w_in), d["k_w"]).then_inc(k_in, 16)
            sp.dma_start(arena[:, 0:NVEC], d["vec"]).then_inc(consts_in, 16)
            sp.dma_start(ident, d["ident"]).then_inc(consts_in, 16)
            sp.dma_start(head_mask, d["head_mask"]).then_inc(consts_in, 16)
            sp.dma_start(flat(v_w_in), d["v_w"]).then_inc(v_in, 16)
            load_batch(1, 1, True)
            sp.dma_start(state01.rearrange("p a b c -> p (a b c)"), d["state01"]).then_inc(x_in, 16)
            sp.dma_start(bonus, d["bonus"]).then_inc(x_in, 16)
            sp.dma_start(flat(out_w), d["out_w"]).then_inc(ow_in, 16)
            sp.dma_start(flat(up_w), d["up_w"]).then_inc(up_in, 16)
            masks_used, batches_used = sp.alloc_register("masks_used"), sp.alloc_register("batches_used")
            sp.reg_mov(masks_used, 1)
            sp.reg_mov(batches_used, 2)
            with sp.Fori(1, B // 2) as i:
                for u in range(2):
                    load_batch(i * 2 + u, u, False)
            sp.wait_ge(att_done, B)
            sp.dma_start(flat(xT), d["x"]).then_inc(x0_in, 16)
            sp.dma_start(flat(down_w), d["down_w"]).then_inc(down_in, 16)
            for dst, name, g in L1W:
                sp.dma_start(flat(dst), d[name]).then_inc(l1w_in[g], 16)
            for c in range(NCH):
                sp.dma_start(s0[c], d["state"][c * P:c * P + P, :]).then_inc(s0_in, 16)

            def store_tile(c, f, m):
                n = stored_count(c, f, m)
                name = MIXES[f]
                if f == 0:
                    sp.wait_ge(dec_done, c * KT + m + 1)
                else:
                    wait_drained(sp, "proj", c, f, m)
                sp.dma_start(scratch[name][c, :, m * P:m * P + P, :].rearrange("b p t -> p b t"),
                             stage[n % 4].rearrange("p (b t) -> p b t", t=T)).then_inc(stage_out[n % 4], 16)

            for st, c, *a in sched:
                if st == "dec2":
                    for m in range(KT):
                        store_tile(c, 0, m)
                elif st == "proj":
                    if a[0] < 4:
                        store_tile(c, *a)
                    if c == NCH - 1 and a[1] == KT - 1:
                        wait_full(sp, "proj", c, a[0], KT - 1)
                        sp.dma_start(flat(LAST[a[0]][0]), d[LAST[a[0]][1]]).then_inc(last_in[a[0]], 16)
                elif st == "load":
                    for k in range(4):
                        sp.wait_ge(stage_out[k], 16 * 4 * (c + 1))
                    for k, (buf, name) in enumerate(((K_of, "k"), (V_of, "v"), (R_of, "r"))):
                        sp.dma_start(flat(buf[c]), scratch[name][c].rearrange("b (h s) t -> (b h) (s t)", s=RS)
                                     ).then_inc(loaded[c][k], 16)
                elif st == "loadw":
                    if c:
                        sp.wait_ge(wb_done, RS * c)
                    sp.dma_start(flat(Wl), scratch["w"][c].rearrange("b (h s) t -> (b h) (s t)", s=RS)
                                 ).then_inc(loaded[c][3], 16)
                elif st == "gn3":
                    sp.wait_ge(y_norm, c + 1)
                    sp.dma_start(scratch["y"][c].rearrange("b (h s) t -> (b h) (s t)", s=RS),
                                 flat(K_of[c])).then_inc(y_st, 16)
                    sp.wait_ge(y_st, 16 * (c + 1))
                    wait_full(sp, "proj", c, 4, KT - 1)
                    for m in range(KT):
                        sp.dma_start(sq[c][:, m, :].rearrange("p (b t) -> p b t", t=T),
                                     scratch["y"][c, :, m * P:m * P + P, :].rearrange("b p t -> p b t")
                                     ).then_inc(y_in[c], 16)
                elif st == "fv":
                    for m in a:
                        sp.wait_ge(o_done, c * KT + m + 1)
                        sp.dma_start(out[:, m, c * N:(c + 1) * N], xT[:, m, c * N:(c + 1) * N]).then_inc(o_st, 16)
            sp.wait_ge(o_st, 16 * KT * NCH)

        @block.tensor
        def _(pe):
            def split_product(out, left, right, start, stop):
                pe.matmul(out, left[1], right[0], start=start, stop=False)
                pe.matmul(out, left[0], right[1], start=False, stop=False)
                return pe.matmul(out, left[0], right[0], start=False, stop=stop)

            def attention(n, u, i, first):
                pe.wait_ge(h_in, n * 16 + 16)
                if first and u == 0:
                    pe.wait_ge(qk_in, 16)
                if not first or u:
                    pe.wait_ge(v_out, n * 4 - 2)
                for m in range(KT):
                    for k in range(KT):
                        mm = pe.matmul(PS[:, 0, m * T:(m + 1) * T], q_w[:, k, m * P:(m + 1) * P],
                                       hT[:, k, NCTX:NKEY], start=(k == 0), stop=(k == KT - 1))
                mm.then_inc(q_full, 1)
                pe.wait_ge(h_split, n + 1)
                if first and u == 0:
                    pe.wait_ge(padded, 2)
                for m in range(KT):
                    if m == 2:
                        pe.wait_ge(q_raw, n + 1)
                    elif m == 3:
                        pe.wait_ge(k_out, n * 4 + 1)
                    elif not first or u:
                        pe.wait_ge(v_out, n * 4 - 1 + m)
                    for k in range(KT):
                        if first and u == 0 and m == 0:
                            pe.wait_ge(kw_split, k + 1)
                        mm = split_product(PS[:, (m + 1) % 3, 0:KW], [w[:, k, m * P:(m + 1) * P] for w in k_w],
                                           [h[:, k, :] for h in h2], k == 0, k == KT - 1)
                    mm.then_inc(k_full, 1)

                def scores(g, heads):
                    for j in heads:
                        hd = g * GH + j
                        if j == 0:
                            pe.wait_ge(k_out, n * 4 + g + 1)
                        if g == 0 and j == 0:
                            pe.wait_ge(q_out, n + 1)
                        if hd == 3 and (not first or u):
                            pe.wait_ge(unD, n * 4)
                            pe.wait_ge(unA, n * 4)
                        elif 6 <= hd < 8:
                            pe.wait_ge(v_out, n * 4 + 4)
                        elif hd >= 4:
                            pe.wait_ge(s_out, n * NH + hd - 3)
                        split_product(PS[0:T, score_bank(hd), 0:KW], [q[:, hd, :] for q in q_pad],
                                      [k[:, g, :] for k in kT], True, True).then_inc(s_full, 1)

                def turn(g, kts):
                    for kt in kts:
                        if g == NG - 1 and kt > 1:
                            pass
                        elif g or kt:
                            if g or kt > 1 or not first or u:
                                pe.wait_ge(pt_out, n * 16 + 4 * g + kt - 1)
                        elif not first or u:
                            pe.wait_ge(att_done, n)
                        for j in range(GH):
                            if kt == 0:
                                pe.wait_ge(exp_done, n * NH + g * GH + j + 1)
                            mm = pe.transpose(PS[0:KSZ[kt], turn_bank(g, kt), j * T:(j + 1) * T],
                                              probs[g % 2][0:T, j, KOFF[kt]:KOFF[kt] + KSZ[kt]], ident[0:T, 0:T])
                        mm.then_inc(t_full, 1)

                def pv(g):
                    if g or not first or u:
                        pe.wait_ge(unD, n * 4 + g)
                        pe.wait_ge(unA, n * 4 + g)
                    for kt in range(4):
                        pe.wait_ge(pt_out, n * 16 + 4 * g + kt + 1)
                        if g == 0:
                            pe.wait_ge(v_out, n * 4 + kt + 1)
                        mm = split_product(PS[:, 7, 0:GH * T], [v[0:KSZ[kt], kt, g * P:(g + 1) * P] for v in V],
                                           [p[0:KSZ[kt], kt, :] for p in pT], kt == 0, kt == 3)
                    mm.then_inc(pv_full, 1)

                scores(0, range(GH))
                if first and u == 0:
                    pe.wait_ge(vw_split, 1)
                    pe.wait_ge(consts_in, 48)
                for kt in range(4):
                    if kt < 3:
                        pe.wait_ge(k_out, n * 4 + 2 + kt)
                    else:
                        pe.wait_ge(v_out, n * 4 + 1)
                    for k in range(KT):
                        mm = split_product(PS[0:KSZ[kt], (5 + kt) % 3, :],
                                           [h[:, k, KOFF[kt]:KOFF[kt] + KSZ[kt]] for h in h2],
                                           [w[:, k, :] for w in v_w], k == 0, k == KT - 1)
                    mm.then_inc(v_full, 1)
                for g in range(NG):
                    for half in ((0, 1), (2, 3)):
                        if g + 1 < NG:
                            scores(g + 1, half)
                        turn(g, half)
                    pv(g)
                pe.wait_ge(wide, n + 1)
                pe.wait_ge(pt_out, n * 16 + 13)
                for g in range(NG):
                    mm = pe.transpose(PS[:, 5, g * T:(g + 1) * T], rinv_wide[0:T, g * P:(g + 1) * P], ident[0:T, 0:T])
                mm.then_inc(t_full, 1)

            for u in range(2):
                attention(u, u, 0, True)
            with pe.Fori(1, B // 2) as i:
                for u in range(2):
                    attention(i * 2 + u, u, i, False)

            def product(key, w, m, rhs, tiles_k, waits=None):
                wait_free(pe, *key)
                for k in range(tiles_k):
                    if waits:
                        waits(k)
                    mm = pe.matmul(tile(*key), w[:, k, m * P:(m + 1) * P], rhs(k), start=(k == 0), stop=(k == tiles_k - 1))
                mm.then_inc(full[tiles[key][0]], 1)
                return mm

            def average(key, sums):
                wait_free(pe, *key)
                pe.matmul(tile(*key), mean_w, sums, start=True, stop=True).then_inc(full[tiles[key][0]], 1)

            def down_step(c, k):
                j = MT * c + k
                pe.wait_ge(dw_split, j + 1)
                pe.wait_ge(hid_split, j + 1)
                for m in range(KT):
                    key = ("down", c, m)
                    if k == 0:
                        wait_free(pe, *key)
                    mm = split_product(tile(*key), [w[:, m * P:(m + 1) * P] for w in down_part[j % PARTS]],
                                       hid[j % PARTS], k == 0, k == MT - 1)
                    if k == MT - 1:
                        mm.then_inc(full[tiles[key][0]], 1)
                if k < MT - 1:
                    mm.then_inc(step_done, 1)

            pe.wait_ge(fills, 4)
            for st, c, *a in sched:
                cols = slice(c * N, (c + 1) * N)
                if st == "oproj":
                    if c == 0 and a[0] == 0:
                        pe.wait_ge(ow_in, 16)
                        pe.wait_ge(att_done, B)
                    for m in a:
                        product(("oproj", c, m), out_w, m, lambda k: attnT[:, k, cols], KT,
                                (lambda k: pe.wait_ge(vb_done, KT * c + k + 1)) if m == 0 else None)
                elif st == "rms":
                    pe.wait_ge(rsum_done, c + 1)
                    average(("rms", c), sq_rms[c][:, 0, :])
                elif st == "mlp":
                    for m in range(*a):
                        j = MT * c + m
                        key = ("up", c, m)
                        wait_free(pe, *key)
                        pe.wait_ge(upw_split, j + 1)
                        for k in range(KT):
                            if m == 0:
                                pe.wait_ge(rn_split, KT * c + k + 1)
                            mm = split_product(tile(*key), [w[:, k, :] for w in up_part[j % PARTS]],
                                               [r[:, k, :] for r in rn2], k == 0, k == KT - 1)
                        mm.then_inc(full[tiles[key][0]], 1)
                        if m >= 2:
                            down_step(c, m - 2)
                elif st == "mlpend":
                    down_step(c, MT - 2)
                    down_step(c, MT - 1)
                elif st == "mean":
                    ch = c % 2
                    pe.wait_ge(msum_done, c + 1)
                    average(("mean", c), sq[ch][:, 2, :])
                elif st == "var":
                    pe.wait_ge(vsum_done, c + 1)
                    average(("var", c), sq[c % 2][:, 0, :])
                elif st == "mix1":
                    if c == 0:
                        pe.wait_ge(l1w_in[0], L1N[0])
                    for m in range(2):
                        product(("mix1", c, m), mix_w1, m, lambda k: xf[(6 * c) % 2][:, k, :], KT,
                                (lambda k: pe.wait_ge(xx_done, KT * c + k + 1)) if m == 0 else None)
                elif st == "mixf":
                    f = a[0]
                    wait_drained(pe, "mix1", c, 0)
                    wait_drained(pe, "mix1", c, 1)
                    for m in range(KT):
                        key = ("mixf", c, f, m)
                        wait_free(pe, *key)
                        pe.matmul(tile(*key), mix_w2[:, f, m * P:(m + 1) * P], mix_t[f // 4], start=True,
                                  stop=True).then_inc(full[tiles[key][0]], 1)
                elif st == "dec1":
                    key = ("dec1", c)
                    wait_free(pe, *key)
                    for k in range(KT):
                        pe.wait_ge(xf_done, (5 * c) * KT + k + 1)
                        mm = pe.matmul(tile(*key), dec_w1[:, k, :], xf[1][:, k, :], start=(k == 0), stop=(k == KT - 1))
                    mm.then_inc(full[tiles[key][0]], 1)
                elif st == "dec2":
                    wait_drained(pe, "dec1", c)
                    for m in range(KT):
                        key = ("proj", c, 0, m)
                        wait_free(pe, *key)
                        pe.matmul(tile(*key), dec_w2[:, m * P:(m + 1) * P], dec_t, start=True,
                                  stop=True).then_inc(full[tiles[key][0]], 1)
                elif st == "proj":
                    f, m = a
                    if c == 0 and f == 1:
                        pe.wait_ge(l1w_in[1], L1N[1])
                    if c == 0 and f == 4:
                        pe.wait_ge(l1w_in[2], L1N[2])
                    if c == 0:
                        key = ("proj", c, f, m)
                        j = NCH * MT + (f - 1) * KT + m
                        wait_free(pe, *key)
                        pe.wait_ge(upw_split, j + 1)
                        for k in range(KT):
                            if m == 0:
                                pe.wait_ge(xp_split, (f - 1) * KT + k + 1)
                            mm = split_product(tile(*key), [w[:, k, :] for w in up_part[j % PARTS]],
                                               [x[:, k, :] for x in xp[(f + 1) % 2]], k == 0, k == KT - 1)
                        mm.then_inc(full[tiles[key][0]], 1)
                    else:
                        product(("proj", c, f, m), rkvg_w[MIXES[f]], m, lambda k: xf[(f + 1) % 2][:, k, :], KT,
                                (lambda k: pe.wait_ge(xf_done, (5 * c + f) * KT + k + 1)) if m == 0 else None)
                elif st == "acc":
                    s = a[0]
                    pe.wait_ge(p_done, RS * c + s + 1)
                    for m in range(KT):
                        key = ("y", c, m)
                        if s == 0 and c == 0:
                            wait_free(pe, *key)
                        elif s == 0:
                            pe.wait_ge(y_sum, c)
                        mm = pe.matmul(tile(*key), ident, flat(slots[(RS * c + s) % RING])[:, m * N:(m + 1) * N],
                                       start=(s == 0), stop=(s == RS - 1), skip_group_check=True)
                    mm.then_inc(acc_done, 1)
                elif st in TAIL and c == 1:
                    i, m = TAIL.index(st) * KT + a[0], a[0]
                    key = (st, c, m)
                    right = {"wo": gated_p, "fr": fmix_p[0], "fk": fmix_p[1], "fv": relu_p}[st]
                    wait_free(pe, *key)
                    pe.wait_ge(tw_split, i + 1)
                    for k in range(KT):
                        if m == 0:
                            pe.wait_ge(tp_split, i + k + 1)
                        mm = split_product(tile(*key), [w[:, k, :] for w in up_part[i % PARTS]],
                                           [x[:, k, :] for x in right], k == 0, k == KT - 1)
                    mm.then_inc(full[tiles[key][0]], 1)
                elif st == "wo":
                    if c == 0:
                        pe.wait_ge(last_in[1], 16)
                    for m in a:
                        product(("wo", c, m), wo_w, m, lambda k: sq[c][:, k, :], KT,
                                (lambda k: pe.wait_ge(y_gated, k + 1)) if m == 0 else None)
                elif st == "fr":
                    if c == 0:
                        pe.wait_ge(last_in[2], 16)
                    for m in a:
                        product(("fr", c, m), fr_w, m, lambda k: xf[0][:, k, :], KT,
                                (lambda k: pe.wait_ge(fm_done, 2 * KT * c + k + 1)) if m == 0 else None)
                elif st == "fk":
                    if c == 0:
                        pe.wait_ge(last_in[3], 16)
                    for m in a:
                        product(("fk", c, m), fk_w, m, lambda k: xf[1][:, k, :], KT,
                                (lambda k: pe.wait_ge(fm_done, 2 * KT * c + KT + k + 1)) if m == 0 else None)
                elif st == "fv":
                    if c == 0:
                        pe.wait_ge(last_in[4], 16)
                    for m in a:
                        product(("fv", c, m), fv_w, m, lambda k: kk[:, k, :], KT,
                                (lambda k: pe.wait_ge(kk_done, KT * c + k + 1)) if m == 0 else None)

        @block.scalar
        def _(act):
            def attention(n, u, i, first):
                for m in range(KT):
                    act.wait_ge(k_full, n * 4 + m + 1)
                    act.activation(kT[0][:, m, :], PS[:, (m + 1) % 3, 0:KW], ACT.Identity,
                                   bias=col("k_b", m)).then_inc(k_hi, 1)

                def exps(g, heads):
                    for j in heads:
                        hd = g * GH + j
                        if j == 0:
                            if g >= 2:
                                act.wait_ge(t_full, n * 17 + (g - 1) * 4)
                            if g == 0 and (not first or u):
                                act.wait_ge(recip, n)
                        act.wait_ge(s_out, n * NH + hd + 1)
                        act.activation(probs[g % 2][0:T, j, :], S[0:T, hd % 2, :], ACT.Exp, scale=-1.0,
                                       bias=neg_max[0:T, hd:hd + 1],
                                       accum_out=row_sum[0:T, hd:hd + 1]).then_inc(exp_done, 1)

                exps(0, range(GH))
                for kt in range(4):
                    act.wait_ge(v_full, n * 4 + kt + 1)
                    act.copy(V[0][0:KSZ[kt], kt, :], PS[0:KSZ[kt], (5 + kt) % 3, :]).then_inc(v_hi, 1)
                for g in range(NG):
                    for half in ((0, 1), (2, 3)):
                        for kt in half:
                            act.wait_ge(t_full, n * 17 + g * 4 + kt + 1)
                            act.copy(pT[0][0:KSZ[kt], kt, :], PS[0:KSZ[kt], turn_bank(g, kt), 0:GH * T]).then_inc(pt_hi, 1)
                        if g + 1 < NG:
                            exps(g + 1, half)
                    act.wait_ge(pv_full, n * 4 + g + 1)
                    if g == 0 and (not first or u):
                        act.wait_ge(att_done, n)
                    for j in range(2, GH):
                        ins = act.copy(att_un[j * DH:(j + 1) * DH, g, :], PS[j * DH:(j + 1) * DH, 7, j * T:(j + 1) * T])
                    ins.then_inc(unA, 1)

            act.wait_ge(h_in, 16)
            act.copy(h2[0][:, :, 0:NKEY], hT).then_inc(h_hi, 1)
            act.wait_ge(consts_in, 48)
            for u in range(2):
                attention(u, u, 0, True)
            with act.Fori(1, B // 2) as i:
                for u in range(2):
                    attention(i * 2 + u, u, i, False)

            def round_tail(i):
                if i >= 4 * KT:
                    return
                f, m = i // KT, i % KT
                if i < 2:
                    act.wait_ge(acc_done, NCH * RS)
                act.wait_ge(last_in[f + 1], 16)
                if i >= PARTS:
                    wait_full(act, TAIL[(i - PARTS) // KT], 1, (i - PARTS) % KT)
                act.copy(up_part[i % PARTS][0], LAST[f + 1][0][:, :, m * P:(m + 1) * P]).then_inc(tw_hi, 1)

            def round_relu(m):
                act.wait_ge(kk_done, KT + m + 1)
                if m == 0:
                    wait_full(act, "wo", 1, KT - 1)
                act.copy(relu_p[0][:, m, :], kk[:, m, :]).then_inc(tp_hi, 1)

            act.wait_ge(fills, 4)
            for st, c, *a in sched:
                if st == "oproj" and c == 0 and a[0] == 0:
                    act.wait_ge(att_done, B)
                    for i in range(NCH * KT):
                        att = attnT[:, i % KT, i // KT * N:(i // KT + 1) * N]
                        act.activation(att, att, ACT.Identity, bias=col("v_b", i % KT)).then_inc(vb_done, 1)
                elif st == "rsum":
                    if c:
                        wait_full(act, "oproj", c, KT - 1)
                    for m in range(KT):
                        wait_drained(act, "oproj", c, m)
                        act.activation(sq_rms[c][:, m, :], attnT[:, m, c * N:(c + 1) * N], ACT.Square).then_inc(sqr_done, 1)
                elif st == "rms":
                    wait_full(act, "rms", c)
                    act.activation(rstd[c], tile("rms", c), ACT.Sqrt, bias=eps[:, 0:1]).then_inc(drained[tiles["rms", c][0]], 1)
                elif st == "rn":
                    if c:
                        wait_full(act, "up", c - 1, MT - 1)
                    for m in range(KT):
                        act.wait_ge(rn_done, KT * c + m + 1)
                        act.copy(rn2[0][:, m, :], attnT[:, m, c * N:(c + 1) * N]).then_inc(rn_hi, 1)
                elif st == "mlp":
                    for m in range(*a):
                        j = MT * c + m
                        wait_full(act, "up", c, m)
                        if j >= 2:
                            act.wait_ge(hid_split, j - 1)
                        act.activation(gelu[j % 2], tile("up", c, m), ACT.Gelu_apprx_tanh,
                                       bias=col("mlp_b1", m)).then_inc(drained[tiles["up", c, m][0]], 1)
                        wait_drained(act, "up", c, m)
                        if j >= PARTS:
                            wait_step(act, j - PARTS)
                        act.copy(hid[j % PARTS][0], gelu[j % 2]).then_inc(hid_hi, 1)
                elif st == "mean":
                    ch = c % 2
                    for m in range(KT):
                        if m < KT - 1:
                            act.wait_ge(centered, (KT - 1) * c + m + 1)
                        else:
                            wait_drained(act, "mean", c)
                        act.activation(sq[ch][:, m, :], attnT[:, m, ch * N:(ch + 1) * N],
                                       ACT.Square).then_inc(lsq_done, 1)
                elif st == "var":
                    ch = c % 2
                    wait_full(act, "var", c)
                    act.activation(rstd[ch], tile("var", c), ACT.Sqrt, bias=eps[:, 1:2]).then_inc(drained[tiles["var", c][0]], 1)
                    for m in range(KT):
                        act.wait_ge(xn_done, KT * c + m + 1)
                        act.activation(xe[ch][:, m, :, 1:T + 1],
                                       attnT[:, m, ch * N:(ch + 1) * N].rearrange("p (b t) -> p b t", t=T),
                                       ACT.Identity, bias=col("ln1_b" if c < 2 else "ln2_b", m)).then_inc(xe_done, 1)
                elif st == "mix1":
                    if c:
                        for m in range(KT):
                            wait_full(act, "mixf", c - 1, 4, m)
                    for m in range(2):
                        wait_full(act, "mix1", c, m)
                        act.activation(mix_t[m], tile("mix1", c, m), ACT.Tanh).then_inc(drained[tiles["mix1", c, m][0]], 1)
                elif st == "mixf" and c == 0 and a[0]:
                    f = a[0]
                    if f > 2:
                        wait_full(act, "proj", c, f - 2, KT - 1)
                    for m in range(KT):
                        act.wait_ge(xf_done, (5 * c + f) * KT + m + 1)
                        act.copy(xp[(f + 1) % 2][0][:, m, :], xf[(f + 1) % 2][:, m, :]).then_inc(xp_hi, 1)
                elif st == "dec1":
                    wait_full(act, "dec1", c)
                    act.activation(dec_t, tile("dec1", c), ACT.Tanh).then_inc(drained[tiles["dec1", c][0]], 1)
                elif st == "dec2" or (st == "proj" and a[0] < 4):
                    f = a[0] if a else 0
                    for m in a[1:] or range(KT):
                        n = stored_count(c, f, m)
                        buf = stage[n % 4]
                        if n >= 4:
                            act.wait_ge(stage_out[n % 4], 16 * (n // 4))
                        wait_full(act, "proj", c, f, m)
                        done = drained[tiles["proj", c, f, m][0]]
                        if f == 0:
                            act.activation(buf, tile("proj", c, f, m), ACT.Exp, bias=col("decay", m)).then_inc(done, 1)
                            wait_drained(act, "proj", c, f, m)
                            act.activation(buf, buf, ACT.Exp, scale=-1.0).then_inc(dec_done, 1)
                        else:
                            act.copy(buf, tile("proj", c, f, m)).then_inc(done, 1)
                elif st == "proj":
                    for m in a[1:]:
                        wait_full(act, "proj", c, 4, m)
                        act.activation(gate[c][:, m, :], tile("proj", c, 4, m), ACT.Silu).then_inc(
                            drained[tiles["proj", c, 4, m][0]], 1)
                elif st == "scan":
                    s, idx = a[0], RS * c + a[0]
                    slot = slots[idx % RING]
                    if idx == 0:
                        wait_full(act, "proj", 0, 3, KT - 1)
                    if s == 0:
                        act.wait_ge(loaded[c][3], 16)
                        act.wait_ge(wb_zero, 1)
                        act.wait_ge(s0_in, 32)
                    if idx:
                        act.wait_ge(scan_done, idx)
                    act.copy(wb[:, :, 1:T], Wl[:, s:s + 1, 0:T - 1].to_broadcast([P, RS, T - 1])).then_inc(wb_done, 1)
                    if idx >= RING:
                        act.wait_ge(acc_done, idx - RING + 1)
                    if s == 2:
                        act.wait_ge(rk_done, c + 1)
                    act.copy(slot[:, :, 0:1], s0[c][:, s * RS:(s + 1) * RS].rearrange("p (t o) -> p t o", o=1)
                             ).then_inc(s0_done, 1)
                elif st == "gn3" and c:
                    round_tail(0)
                    round_tail(1)
                elif st == "gated" and c:
                    for m in range(KT):
                        act.wait_ge(y_gated, KT * c + m + 1)
                        act.copy(gated_p[0][:, m, :], sq[c][:, m, :]).then_inc(tp_hi, 1)
                elif st == "fmix" and c:
                    for j in range(2):
                        for m in range(KT):
                            act.wait_ge(fm_done, (2 * c + j) * KT + m + 1)
                            act.copy(fmix_p[j][0][:, m, :], xf[j][:, m, :]).then_inc(tp_hi, 1)
                elif st == "gn1":
                    act.wait_ge(y_cent, c + 1)
                    act.activation(flat(R_of[c]), flat(K_of[c]), ACT.Square, scale=0.25).then_inc(y_sq, 1)
                elif st == "gn2":
                    act.wait_ge(y_var, c + 1)
                    act.activation(gv, gv, ACT.Sqrt, bias=eps[:, 1:2]).then_inc(y_rs, 1)
                if st in TAIL and c:
                    round_tail(TAIL.index(st) * KT + a[0] + 2)
                if st == "fr":
                    if c:
                        act.wait_ge(o_done, KT * c)
                    for m in a:
                        wait_full(act, "fr", c, m)
                        act.activation(rr[:, m, :], tile("fr", c, m), ACT.Sigmoid).then_inc(drained[tiles["fr", c, m][0]], 1)
                elif st == "fk":
                    if c:
                        wait_full(act, "fv", c - 1, KT - 1)
                    for m in a:
                        wait_full(act, "fk", c, m)
                        act.activation(kk[:, m, :], tile("fk", c, m), ACT.Relu).then_inc(drained[tiles["fk", c, m][0]], 1)
                        if c:
                            wait_drained(act, "fk", c, m)
                            act.activation(kk[:, m, :], kk[:, m, :], ACT.Square).then_inc(kk_done, 1)
                            round_relu(m)

        @block.vector
        def _(dve):
            def attention(n, u, i, first):
                dve.wait_ge(m_in[u], i * 16 + 16)
                dve.tensor_scalar(mask_add[u][0:T, 0:NCTX], mask_in[u][0:T, :].bitcast(I32), 0.0, -BIG,
                                  ALU.is_equal, ALU.mult).then_inc(mask_done, 1)
                dve.wait_ge(q_full, n + 1)
                for m in range(KT):
                    ins = dve.scalar_tensor_tensor(
                        q_full32[:, m * GH:(m + 1) * GH, :],
                        PS[:, 0, m * T:(m + 1) * T].rearrange("p (o t) -> p o t", o=1).to_broadcast([P, GH, T]),
                        col("q_b", m), head_mask.rearrange("p (h o) -> p h o", o=1).to_broadcast([P, GH, T]),
                        ALU.add, ALU.mult)
                ins.then_inc(q_raw, 1)
                dve.wait_ge(q_raw, n + 1)
                dve.tensor_copy(q_pad[0], q_full32).then_inc(q_hi, 1)
                for m in range(KT):
                    dve.wait_ge(k_hi, n * 4 + m + 1)
                    dve.scalar_tensor_tensor(kT[1][:, m, :], PS[:, (m + 1) % 3, 0:KW], col("k_b", m),
                                             kT[0][:, m, :].bitcast(F32), ALU.add, ALU.subtract).then_inc(k_out, 1)
                    if first and u == 0 and m == 1:
                        dve.wait_ge(v_in, 16)
                        dve.tensor_copy(v_w[0], v_w_in).then_inc(vw_hi, 1)
                        dve.wait_ge(vw_hi, 1)
                        dve.tensor_tensor(v_w[1], v_w_in, v_w[0].bitcast(F32), ALU.subtract).then_inc(vw_split, 1)
                dve.wait_ge(mask_done, n + 1)

                def rows(g, heads):
                    for j in heads:
                        hd = g * GH + j
                        free, ready = n * NH + hd - 1, n * NH + hd + 1
                        if not first:
                            free, ready = exps_needed, scores_needed
                            dve.reg_add(free, free, 1)
                            dve.reg_add(ready, ready, 1)
                        dve.wait_ge(fills, 4)
                        if hd >= 2 or not first or u:
                            dve.wait_ge(exp_done, free)
                        dve.wait_ge(s_full, ready)
                        dve.tensor_tensor_reduce(S[0:T, hd % 2, :], PS[0:T, score_bank(hd), 0:NKEY], mask_add[u][0:T, :],
                                                 -1.0 / DH, 3.0e38, ALU.add, ALU.min,
                                                 neg_max[0:T, hd:hd + 1]).then_inc(s_out, 1)

                rows(0, range(GH))
                for kt in range(4):
                    dve.wait_ge(v_hi, n * 4 + kt + 1)
                    dve.tensor_tensor(V[1][0:KSZ[kt], kt, :], PS[0:KSZ[kt], (5 + kt) % 3, :],
                                      V[0][0:KSZ[kt], kt, :].bitcast(F32), ALU.subtract).then_inc(v_out, 1)
                for g in range(NG):
                    if g + 1 == NG:
                        dve.wait_ge(exp_done, n * NH + NH)
                        if not first or u:
                            dve.wait_ge(wide, n)
                        dve.reciprocal(rinv[0:T, :], row_sum[0:T, :]).then_inc(recip, 1)
                    for half in ((0, 1), (2, 3)):
                        if g + 1 < NG:
                            rows(g + 1, half)
                        for kt in half:
                            dve.wait_ge(pt_hi, n * 16 + g * 4 + kt + 1)
                            dve.tensor_tensor(pT[1][0:KSZ[kt], kt, :], PS[0:KSZ[kt], turn_bank(g, kt), 0:GH * T],
                                              pT[0][0:KSZ[kt], kt, :].bitcast(F32), ALU.subtract).then_inc(pt_out, 1)
                    dve.wait_ge(pv_full, n * 4 + g + 1)
                    if g == 0 and (not first or u):
                        dve.wait_ge(att_done, n)
                    for j in range(2):
                        ins = dve.tensor_copy(att_un[j * DH:(j + 1) * DH, g, :],
                                              PS[j * DH:(j + 1) * DH, 7, j * T:(j + 1) * T])
                    ins.then_inc(unD, 1)
                dve.wait_ge(unA, n * 4 + 4)
                dve.wait_ge(unD, n * 4 + 4)
                dve.wait_ge(t_full, n * 17 + 17)
                dst = attnT[:, :, n * T:(n + 1) * T] if first else attnT[:, :, bass.ds(n * T, T)]
                dve.tensor_tensor(dst, att_un, PS[:, 5, 0:KT * T].rearrange("p (g t) -> p g t", t=T),
                                  ALU.mult).then_inc(att_done, 1)

            dve.wait_ge(h_hi, 1)
            dve.tensor_tensor(h2[1][:, :, 0:NKEY], hT, h2[0][:, :, 0:NKEY].bitcast(F32), ALU.subtract).then_inc(h_split, 1)
            dve.wait_ge(k_in, 16)
            for k in range(KT):
                dve.tensor_copy(k_w[0][:, k, :], k_w_in[:, k, :]).then_inc(kw_hi, 1)
                dve.wait_ge(kw_hi, k + 1)
                dve.tensor_tensor(k_w[1][:, k, :], k_w_in[:, k, :], k_w[0][:, k, :].bitcast(F32),
                                  ALU.subtract).then_inc(kw_split, 1)
            dve.wait_ge(consts_in, 48)
            for u in range(2):
                attention(u, u, 0, True)
            scores_needed, exps_needed = dve.alloc_register("scores_needed"), dve.alloc_register("exps_needed")
            dve.reg_mov(scores_needed, 2 * NH)
            dve.reg_mov(exps_needed, 2 * NH - 2)
            with dve.Fori(1, B // 2) as i:
                for u in range(2):
                    attention(i * 2 + u, u, i, False)

            def rest(i, parts, x, m):
                dve.wait_ge(tp_hi, i + 1)
                dve.tensor_tensor(parts[1][:, m, :], x[:, m, :], parts[0][:, m, :].bitcast(F32),
                                  ALU.subtract).then_inc(tp_split, 1)

            def add_tiles(src, dst, at, half_done, done, count):
                dve.tensor_tensor(dst[:, 0:2, :], src[:, 0:2, :], src[:, 2:4, :], ALU.add).then_inc(half_done, 1)
                dve.wait_ge(half_done, count)
                dve.tensor_tensor(dst[:, at, :], dst[:, 0, :], dst[:, 1, :], ALU.add).then_inc(done, 1)

            def split_up(j):
                if j < NCH * MT:
                    w, m = up_w, j % MT
                else:
                    f, m = 1 + (j - NCH * MT) // KT, (j - NCH * MT) % KT
                    w = rkvg_w[MIXES[f]]
                    group = 2 if f == 4 else 1
                    dve.wait_ge(l1w_in[group], L1N[group])
                if NCH * MT <= j - PARTS:
                    p = j - PARTS - NCH * MT
                    wait_full(dve, "proj", 0, 1 + p // KT, p % KT)
                elif j >= PARTS:
                    wait_full(dve, "up", (j - PARTS) // MT, (j - PARTS) % MT)
                hi, lo = up_part[j % PARTS]
                dve.tensor_copy(hi, w[:, :, m * P:(m + 1) * P]).then_inc(upw_hi, 1)
                dve.wait_ge(upw_hi, j + 1)
                dve.tensor_tensor(lo, w[:, :, m * P:(m + 1) * P], hi.bitcast(F32), ALU.subtract).then_inc(upw_split, 1)

            dve.wait_ge(att_done, B)
            dve.wait_ge(wide, B)
            dve.wait_ge(up_in, 16)
            split_up(0)
            split_up(1)
            dve.wait_ge(x_in, 32)
            dve.wait_ge(x0_in, 16)
            for st, c, *a in sched:
                cols = slice(c * N, (c + 1) * N)
                if st == "oproj" and a[0] == KT - 1:
                    for m in range(KT):
                        wait_full(dve, "oproj", c, m)
                    for m in range(KT):
                        dve.scalar_tensor_tensor(attnT[:, m, cols], tile("oproj", c, m), col("out_b", m), xT[:, m, cols],
                                                 ALU.add, ALU.add).then_inc(drained[tiles["oproj", c, m][0]], 1)
                elif st == "rsum":
                    dve.wait_ge(sqr_done, KT * (c + 1))
                    add_tiles(sq_rms[c], sq_rms[c], 0, rhalf_done, rsum_done, c + 1)
                elif st == "msum":
                    ch = c % 2
                    for m in range(KT):
                        wait_drained(dve, "down" if c < 2 else "wo", ch, m)
                    add_tiles(xT[:, :, ch * N:(ch + 1) * N], sq[ch], 2, mhalf_done, msum_done, c + 1)
                elif st == "vsum":
                    dve.wait_ge(lsq_done, KT * (c + 1))
                    add_tiles(sq[c % 2], sq[c % 2], 0, vhalf_done, vsum_done, c + 1)
                elif st == "rms":
                    wait_drained(dve, "rms", c)
                    dve.reciprocal(rstd[c], rstd[c]).then_inc(rstd_done, 1)
                    dve.wait_ge(rstd_done, c + 1)
                    for m in range(KT):
                        dve.scalar_tensor_tensor(attnT[:, m, cols], attnT[:, m, cols], col("post_w", m), rstd[c],
                                                 ALU.mult, ALU.mult).then_inc(rn_done, 1)
                elif st == "rn":
                    for m in range(KT):
                        dve.wait_ge(rn_hi, KT * c + m + 1)
                        dve.tensor_tensor(rn2[1][:, m, :], attnT[:, m, cols], rn2[0][:, m, :].bitcast(F32),
                                          ALU.subtract).then_inc(rn_split, 1)
                elif st == "mlp":
                    for m in range(*a):
                        j = MT * c + m
                        if j + 2 < NCH * MT:
                            split_up(j + 2)
                        dve.wait_ge(hid_hi, j + 1)
                        dve.tensor_tensor(hid[j % PARTS][1], gelu[j % 2], hid[j % PARTS][0].bitcast(F32),
                                          ALU.subtract).then_inc(hid_split, 1)
                elif st == "down":
                    for m in range(KT):
                        wait_full(dve, "down", c, m)
                        dve.scalar_tensor_tensor(xT[:, m, cols], tile("down", c, m), col("mlp_b2", m), xT[:, m, cols],
                                                 ALU.add, ALU.add).then_inc(drained[tiles["down", c, m][0]], 1)
                elif st == "mean":
                    ch = c % 2
                    cc = slice(ch * N, (ch + 1) * N)
                    wait_full(dve, "mean", c)
                    for m in range(KT):
                        ins = dve.tensor_tensor(attnT[:, m, cc], xT[:, m, cc], tile("mean", c), ALU.subtract)
                        ins.then_inc(centered if m < KT - 1 else drained[tiles["mean", c][0]], 1)
                elif st == "var":
                    ch = c % 2
                    cc = slice(ch * N, (ch + 1) * N)
                    wait_drained(dve, "var", c)
                    dve.reciprocal(rstd[ch], rstd[ch]).then_inc(lrs_done, 1)
                    dve.wait_ge(lrs_done, c + 1)
                    for m in range(KT):
                        dve.scalar_tensor_tensor(attnT[:, m, cc], attnT[:, m, cc], col("ln1_w" if c < 2 else "ln2_w", m),
                                                 rstd[ch], ALU.mult, ALU.mult).then_inc(xn_done, 1)
                elif st == "shift" and c < 2:
                    ch = c % 2
                    dve.wait_ge(edge_done, c + 1)
                    for m in range(KT):
                        dve.wait_ge(xe_done, KT * c + m + 1)
                        dve.tensor_tensor(
                            attnT[:, m, ch * N:(ch + 1) * N].rearrange("p (b t) -> p b t", t=T),
                            xe[ch][:, m, :, 0:T], xe[ch][:, m, :, 1:T + 1], ALU.subtract).then_inc(sx_done, 1)
                elif st == "mix1":
                    dve.wait_ge(sx_done, KT * (c + 1))
                    if c:
                        wait_full(dve, "proj", c - 1, 3, KT - 1)
                    for m in range(KT):
                        dve.scalar_tensor_tensor(xf[0][:, m, :].rearrange("p (b t) -> p b t", t=T),
                                                 attnT[:, m, cols].rearrange("p (b t) -> p b t", t=T),
                                                 col("maa_x", m), xe[c][:, m, :, 1:T + 1],
                                                 ALU.mult, ALU.add).then_inc(xx_done, 1)
                elif st == "mixf":
                    f = a[0]
                    for m in range(KT):
                        e = (5 * c + f) * KT + m
                        wait_full(dve, "mixf", c, f, m)
                        if e >= 2:
                            dve.wait_ge(xf_done, e - 1)
                        dve.scalar_tensor_tensor(lerp[e % 2], tile("mixf", c, f, m), col("maa_" + MIXES[f], m),
                                                 attnT[:, m, cols], ALU.add, ALU.mult).then_inc(
                                                     drained[tiles["mixf", c, f, m][0]], 1)
                    if c == 0 and f:
                        for m in range(KT):
                            dve.wait_ge(xp_hi, (f - 1) * KT + m + 1)
                            dve.tensor_tensor(xp[(f + 1) % 2][1][:, m, :], xf[(f + 1) % 2][:, m, :],
                                              xp[(f + 1) % 2][0][:, m, :].bitcast(F32), ALU.subtract).then_inc(xp_split, 1)
                    if c == 0 and f == 1:
                        split_up(NCH * MT)
                        split_up(NCH * MT + 1)
                elif st == "proj" and c == 0:
                    i = (a[0] - 1) * KT + a[1] + 2
                    if i < 4 * KT:
                        split_up(NCH * MT + i)
                elif st == "prep":
                    dve.wait_ge(ruk, c + 1)
                    prod = slots[(RS * c + 2) % RING]
                    dve.tensor_tensor(prod, prod,
                                      bonus.rearrange("p (s o) -> p s o", o=1).to_broadcast([P, RS, T]),
                                      ALU.mult).then_inc(ruku, 1)
                    dve.wait_ge(ruku, c + 1)
                    dve.tensor_reduce(rk, prod.rearrange("p s t -> p t s"), AX_X, ALU.add).then_inc(rk_done, 1)
                elif st == "scan":
                    s, idx = a[0], RS * c + a[0]
                    slot = slots[idx % RING]
                    if idx == 0:
                        wait_full(dve, "proj", 0, 3, KT - 1)
                    if s == 0:
                        dve.wait_ge(loaded[c][0], 16)
                        dve.wait_ge(loaded[c][1], 16)
                        dve.wait_ge(wb_zero, 1)
                    if idx >= RING:
                        dve.wait_ge(acc_done, idx - RING + 1)
                    if s == 2:
                        dve.wait_ge(rk_done, c + 1)
                    dve.tensor_tensor(slot[:, :, 1:T], K_of[c][:, s:s + 1, 0:T - 1].to_broadcast([P, RS, T - 1]),
                                      V_of[c][:, :, 0:T - 1], ALU.mult).then_inc(a_done, 1)
                    dve.wait_ge(a_done, idx + 1)
                    dve.wait_ge(s0_done, idx + 1)
                    dve.wait_ge(wb_done, idx + 1)
                    dve.tensor_tensor_scan(flat(slot), flat(wb), flat(slot), 0.0, ALU.mult, ALU.add).then_inc(scan_done, 1)
                elif st == "gn1":
                    Vl, yb = V_of[c], K_of[c]
                    dve.wait_ge(a_done, RS * (c + 1))
                    rk_b = rk.rearrange("p (o t) -> p o t", o=1).to_broadcast([P, RS, T])
                    dve.tensor_tensor(Vl, Vl, rk_b, ALU.mult).then_inc(vrk_done, 1)
                    dve.wait_ge(vrk_done, c + 1)
                    dve.wait_ge(acc_done, RS * (c + 1))
                    dve.wait_ge(scan_done, RS * (c + 1))
                    dve.tensor_tensor(flat(yb).rearrange("p (m n) -> p m n", n=N), PS[:, 4:8, 0:N],
                                      flat(Vl).rearrange("p (m n) -> p m n", n=N), ALU.add).then_inc(y_sum, 1)
                    dve.wait_ge(y_sum, c + 1)
                    by_time = yb.rearrange("p v t -> p t v")
                    dve.tensor_reduce(gm, by_time, AX_X, ALU.add).then_inc(y_mean, 1)
                    dve.wait_ge(y_mean, c + 1)
                    dve.scalar_tensor_tensor(yb, gm.rearrange("p (o t) -> p o t", o=1).to_broadcast([P, RS, T]),
                                             -1.0 / RS, yb, ALU.mult, ALU.add).then_inc(y_cent, 1)
                elif st == "gn2":
                    dve.wait_ge(y_sq, c + 1)
                    dve.tensor_reduce(gv, R_of[c].rearrange("p v t -> p t v"), AX_X, ALU.add).then_inc(y_var, 1)
                elif st == "gn3":
                    dve.wait_ge(y_rs, 2 * c + 1)
                    dve.reciprocal(gv, gv).then_inc(y_rs, 1)
                    dve.wait_ge(y_rs, 2 * c + 2)
                    dve.tensor_tensor(K_of[c], K_of[c], gv.rearrange("p (o t) -> p o t", o=1).to_broadcast([P, RS, T]),
                                      ALU.mult).then_inc(y_norm, 1)
                elif st == "gated":
                    dve.wait_ge(y_in[c], 16 * KT)
                    for m in range(KT):
                        dve.tensor_scalar(sq[c][:, m, :], sq[c][:, m, :], col("gn_w", m), col("gn_b", m),
                                          ALU.mult, ALU.add).then_inc(y_aff, 1)
                    dve.wait_ge(y_aff, KT * (c + 1))
                    for m in range(KT):
                        wait_drained(dve, "proj", c, 4, m)
                    for m in range(KT):
                        dve.tensor_tensor(sq[c][:, m, :], sq[c][:, m, :], gate[c][:, m, :], ALU.mult).then_inc(y_gated, 1)
                        if c and m:
                            rest(m - 1, gated_p, sq[c], m - 1)
                    if c:
                        rest(KT - 1, gated_p, sq[c], KT - 1)
                elif st == "wo":
                    for m in a:
                        wait_full(dve, "wo", c, m)
                        dve.tensor_tensor(xT[:, m, cols], tile("wo", c, m), xT[:, m, cols], ALU.add).then_inc(
                            drained[tiles["wo", c, m][0]], 1)
                elif st == "fmix":
                    if c:
                        for m in range(KT):
                            wait_full(dve, "fk", c - 1, m)
                    else:
                        wait_full(dve, "proj", 1, 4, KT - 1)
                    for j, name in enumerate(("fmaa_r", "fmaa_k")):
                        for m in range(KT):
                            dve.wait_ge(sx_done, (c + 2) * KT + m + 1)
                            dve.scalar_tensor_tensor(xf[j][:, m, :].rearrange("p (b t) -> p b t", t=T),
                                                     attnT[:, m, cols].rearrange("p (b t) -> p b t", t=T),
                                                     col(name, m), xe[c][:, m, :, 1:T + 1],
                                                     ALU.mult, ALU.add).then_inc(fm_done, 1)
                            n = j * KT + m
                            if c and n:
                                rest(KT + n - 1, fmix_p[(n - 1) // KT], xf[(n - 1) // KT], (n - 1) % KT)
                    if c:
                        rest(3 * KT - 1, fmix_p[1], xf[1], KT - 1)
                elif st == "fk" and c and a[0]:
                    rest(3 * KT + a[0] - 1, relu_p, kk, a[0] - 1)
                elif st == "fv":
                    if c and a[0] == 0:
                        rest(4 * KT - 1, relu_p, kk, KT - 1)
                    for m in a:
                        wait_drained(dve, "fr", c, m)
                        wait_full(dve, "fv", c, m)
                        dve.tensor_tensor(rr[:, m, :], tile("fv", c, m), rr[:, m, :], ALU.mult).then_inc(
                            drained[tiles["fv", c, m][0]], 1)

        @block.gpsimd
        def _(pool):
            pool.memset(mean_w, 1.0 / C).then_inc(fills, 1)
            pool.memset(eps[:, 0:1], EPS_RMS).then_inc(fills, 1)
            pool.memset(eps[:, 1:2], EPS_LN).then_inc(fills, 1)
            for u in range(2):
                ins = pool.memset(mask_add[u][0:T, NCTX:NKEY], 0.0)
            ins.then_inc(fills, 1)

            def split_h(n, first):
                ready, free = n * 16 + 16, n * 4
                if not first:
                    ready, free = h_needed, v_needed
                pool.wait_ge(fills, 4)
                pool.wait_ge(h_in, ready)
                if not first or n:
                    pool.wait_ge(v_full, free)
                pool.tensor_scalar(h2[0][:, :, 0:NKEY], hT, 1.0, None, ALU.mult).then_inc(h_hi, 1)
                done = n + 1
                if not first:
                    done = h_done
                pool.wait_ge(h_hi, done)
                pool.tensor_tensor(h2[1][:, :, 0:NKEY], hT, h2[0][:, :, 0:NKEY].bitcast(F32),
                                   ALU.subtract).then_inc(h_split, 1)
                if not first:
                    pool.reg_add(h_needed, h_needed, 16)
                    pool.reg_add(v_needed, v_needed, 4)
                    pool.reg_add(h_done, h_done, 1)

            def split_q(n, first):
                pool.wait_ge(q_hi, n + 1)
                pool.tensor_tensor(q_pad[1], q_full32, q_pad[0].bitcast(F32), ALU.subtract).then_inc(q_out, 1)

            def spread_rinv(n, first):
                ready = n + 1 if first else sums_needed
                pool.wait_ge(fills, 4)
                pool.wait_ge(recip, ready)
                pool.tensor_copy(rinv_wide[0:T, :].rearrange("p (h e) -> p h e", e=DH),
                                 rinv[0:T, :].rearrange("p (h o) -> p h o", o=1).to_broadcast([T, NH, DH])
                                 ).then_inc(wide, 1)
                if not first:
                    pool.reg_add(sums_needed, sums_needed, 1)

            for part in h2:
                pool.memset(part[:, :, NKEY:KW].bitcast(F32), 0.0).then_inc(padded, 1)
            split_q(0, True)
            split_h(1, True)
            spread_rinv(0, True)
            split_q(1, True)
            h_needed, v_needed, h_done, sums_needed = (pool.alloc_register(n) for n in (
                "h_needed", "v_needed", "h_done", "sums_needed"))
            pool.reg_mov(h_needed, 48)
            pool.reg_mov(v_needed, 8)
            pool.reg_mov(h_done, 3)
            pool.reg_mov(sums_needed, 2)
            with pool.Fori(1, B // 2) as i:
                for u in range(2):
                    split_h(i * 2 + u, False)
                    spread_rinv(i * 2 + u - 1, False)
                    split_q(i * 2 + u, False)
            spread_rinv(B - 1, True)

            def split_tail(i):
                if i >= 4 * KT:
                    return
                f, m = i // KT, i % KT
                w, (hi, lo) = LAST[f + 1][0], up_part[i % PARTS]
                pool.wait_ge(tw_hi, i + 1)
                pool.tensor_tensor(lo, w[:, :, m * P:(m + 1) * P], hi.bitcast(F32), ALU.subtract).then_inc(tw_split, 1)

            for st, c, *a in sched:
                cols = slice(c * N, (c + 1) * N)
                if st == "mlp":
                    for m in range(*a):
                        j = MT * c + m
                        hi, lo = down_part[j % PARTS]
                        if j == 0:
                            pool.wait_ge(down_in, 16)
                        if j >= PARTS:
                            wait_step(pool, j - PARTS)
                        pool.tensor_scalar(hi, down_w[:, m, :], 1.0, None, ALU.mult).then_inc(dw_hi, 1)
                        pool.wait_ge(dw_hi, j + 1)
                        pool.tensor_tensor(lo, down_w[:, m, :], hi.bitcast(F32), ALU.subtract).then_inc(dw_split, 1)
                elif st == "shift" and c >= 2:
                    ch = c % 2
                    pool.wait_ge(edge_done, c + 1)
                    for m in range(KT):
                        pool.wait_ge(xe_done, KT * c + m + 1)
                        pool.tensor_tensor(
                            attnT[:, m, ch * N:(ch + 1) * N].rearrange("p (b t) -> p b t", t=T),
                            xe[ch][:, m, :, 0:T], xe[ch][:, m, :, 1:T + 1], ALU.subtract).then_inc(sx_done, 1)
                elif st == "var":
                    ch = c % 2
                    wait_full(pool, "var", c)
                    pool.tensor_copy(xe[ch][:, :, :, 0:1],
                                     state01[:, 1 if c < 2 else 0, :, ch * CB:(ch + 1) * CB].rearrange(
                                         "p k (b o) -> p k b o", o=1)).then_inc(edge_done, 1)
                elif st == "mixf":
                    f = a[0]
                    for m in range(KT):
                        e = (5 * c + f) * KT + m
                        if m == 0:
                            if f == 0 and c:
                                wait_full(pool, "proj", c - 1, 4, KT - 1)
                            if f == 1:
                                wait_full(pool, "mix1", c, 1)
                            if f == 2:
                                wait_full(pool, "dec1", c)
                            if f > 2:
                                wait_full(pool, "proj", c, f - 2, KT - 1)
                        wait_drained(pool, "mixf", c, f, m)
                        pool.tensor_tensor(xf[(f + 1) % 2][:, m, :].rearrange("p (b t) -> p b t", t=T),
                                           lerp[e % 2].rearrange("p (b t) -> p b t", t=T),
                                           xe[c][:, m, :, 1:T + 1], ALU.add).then_inc(xf_done, 1)
                elif st == "loadw" and c == 0:
                    wait_full(pool, "proj", 0, 4, KT - 1)
                    pool.memset(wb[:, :, 0:1], 0.0).then_inc(wb_zero, 1)
                elif st == "prep":
                    pool.wait_ge(loaded[c][0], 16)
                    pool.wait_ge(loaded[c][2], 16)
                    if c:
                        pool.wait_ge(acc_done, RS * c)
                    pool.tensor_tensor(slots[(RS * c + 2) % RING], K_of[c], R_of[c], ALU.mult).then_inc(ruk, 1)
                elif st == "scan":
                    s, idx = a[0], RS * c + a[0]
                    slot = slots[idx % RING]
                    pool.wait_ge(scan_done, idx + 1)
                    pool.tensor_tensor(slot, slot, R_of[c][:, s:s + 1, :].to_broadcast([P, RS, T]), ALU.mult).then_inc(p_done, 1)
                elif st == "gn3" and c:
                    split_tail(0)
                    split_tail(1)
                elif st in TAIL:
                    if c:
                        split_tail(TAIL.index(st) * KT + a[0] + 2)
                if st == "fk" and c == 0:
                    for m in a:
                        wait_drained(pool, "fk", c, m)
                        pool.tensor_tensor(kk[:, m, :], kk[:, m, :], kk[:, m, :], ALU.mult).then_inc(kk_done, 1)
                elif st == "fv":
                    for m in a:
                        wait_drained(pool, "fv", c, m)
                        pool.tensor_tensor(xT[:, m, cols], rr[:, m, :], xT[:, m, cols], ALU.add).then_inc(o_done, 1)


def kernel(**inputs):
    import concourse.bacc as bacc
    from concourse.bass_utils import run_bass_kernel_spmd

    a = {k: np.asarray(v) for k, v in inputs.items()}
    l0 = {k[len("L0_xattn_"):]: v for k, v in a.items() if k.startswith("L0_xattn_")}
    l1 = {k[len("L1_xattn_"):]: v for k, v in a.items() if k.startswith("L1_xattn_")}

    def rows(w):
        return np.ascontiguousarray(w.reshape(-1, P, w.shape[1]).transpose(1, 0, 2).reshape(P, -1))

    def vector(v):
        return v.reshape(-1, P).T

    x, ctx = a["x"], a["ctx_2048"]
    kv = l0["kv_w"].reshape(C, C, 2)
    kvb = l0["kv_b"].reshape(C, 2)
    h = np.concatenate([ctx, x], axis=1)
    vecs = {"q_b": l0["q_b"], "k_b": kvb[:, 0], "v_b": kvb[:, 1], "out_b": l0["out_b"], "post_w": l0["postnorm_w"],
            "mlp_b1": l0["mlp_b1"], "mlp_b2": l0["mlp_b2"], "decay": l1["time_decay"], "fmaa_k": l1["fmaa_k"],
            "fmaa_r": l1["fmaa_r"], "gn_w": l1["gn_w"], "gn_b": l1["gn_b"]}
    for n in ("ln1_w", "ln1_b", "ln2_w", "ln2_b", "maa_x", "maa_w", "maa_k", "maa_v", "maa_r", "maa_g"):
        vecs[n] = l1[n]
    w1 = np.zeros((C, 2 * P), np.float32)
    w1[:, 0:5 * MIX] = l1["maa_w1"]
    w2 = np.zeros((P, 5, C), np.float32)
    for f in range(5):
        r0 = MIX * (f % 4)
        w2[r0:r0 + MIX, f, :] = l1["maa_w2"][f]
    d1 = np.zeros((C, P), np.float32)
    d1[:, 0:DEC] = l1["decay_w1"]
    d2 = np.zeros((P, C), np.float32)
    d2[0:DEC] = l1["decay_w2"]
    arrays = {
        "h": h.transpose(0, 2, 1).reshape(B, KT, P, NKEY).transpose(0, 2, 1, 3).reshape(B * P, KT * NKEY),
        "x": rows(x.reshape(B * T, C).T),
        "mask": a["mask_BxS2_ik0"],
        "vec": np.concatenate([vector(vecs[n]) for n in VECS], axis=1),
        "ident": np.eye(P, dtype=np.float32),
        "head_mask": (np.arange(P)[:, None] // DH == np.arange(GH)[None, :]).astype(np.float32),
        "state01": ctx[:, 0:2].transpose(2, 1, 0).reshape(KT, P, 2, B).transpose(1, 2, 0, 3).reshape(P, -1),
        "state": ctx[:, 2:2 + RS].reshape(B * RH, RS * RS),
        "bonus": np.tile(l1["faaaa"].reshape(RH, RS), (CB, 1)),
        "q_w": rows(l0["q_w"]), "k_w": rows(kv[:, :, 0]), "v_w": rows(kv[:, :, 1]), "out_w": rows(l0["out_w"]),
        "up_w": rows(l0["mlp_w1"]), "down_w": rows(l0["mlp_w2"]),
        "mix_w1": rows(w1), "mix_w2": w2.reshape(P, 5 * C), "dec_w1": rows(d1), "dec_w2": d2,
    }
    for n in ("Wr", "Wk", "Wv", "Wg", "Wo", "fWk", "fWr", "fWv"):
        arrays[n] = rows(l1[n].T)
    nc = bacc.Bacc("TRN2", target_bir_lowering=False, num_devices=1)
    data, d = {}, {}
    for name, v in arrays.items():
        v = np.ascontiguousarray(v)
        data["in_" + name] = v
        d[name] = nc.dram_tensor("in_" + name, v.shape, mybir.dt.from_np(v.dtype), kind="ExternalInput").ap()
    out = nc.dram_tensor("out_xT", [P, KT, B * T], F32, kind="ExternalOutput").ap()
    xattn_rwkv_kernel(nc, d, out)
    r = run_bass_kernel_spmd(nc, [data], core_ids=[0])
    got = r.results[0]["out_xT"]
    return np.ascontiguousarray(got.reshape(P, KT, B, T).transpose(2, 3, 1, 0).reshape(B, T, C))
```
